# Optimizing a Trainium2 kernel written in Bass

```python
import numpy as np
import jax
import jax.numpy as jnp

def _softmax(x, axis=-1):
    return jax.nn.softmax(x, axis=axis)

def _gelu(x):
    return jax.nn.gelu(x, approximate=True)

def _silu(x):
    return jax.nn.silu(x)

def _sigmoid(x):
    return jax.nn.sigmoid(x)

def _layernorm(x, axis=-1, eps=1e-05):
    m = jnp.mean(x, axis=axis, keepdims=True)
    v = jnp.var(x, axis=axis, keepdims=True)
    return (x - m) / jnp.sqrt(v + eps)

def _scatter_add(tgt, idx, src, axis=0):
    return tgt.at[idx].add(src)

def _segment_sum(src, seg, n):
    return jax.ops.segment_sum(src, seg, n)
kernel_name = 'mk_gnn_preln_d2_gnn_r32_3b771b'

def setup_inputs(seed: int=0):
    np.random.seed(seed)
    _w = jnp.asarray

    def _rec_inputs():
        import jax
        import jax.numpy as jnp
        _gk = jax.random.key(seed)
        x = -0.0001006 + 1 * jax.random.normal(jax.random.fold_in(_gk, 1), (50000, 96), jnp.float32)
        src = jax.random.randint(jax.random.fold_in(_gk, 2), (25000,), 0, 50000, jnp.int32)
        dst = jax.random.randint(jax.random.fold_in(_gk, 3), (25000,), 0, 50000, jnp.int32)
        _o = jnp.argsort(dst, stable=True)
        src = src[_o]
        dst = dst[_o]
        edge_attr_32 = 0.000196303 + 1.00016 * jax.random.normal(jax.random.fold_in(_gk, 11), (25000, 32), jnp.float32)
        return (x, src, dst, edge_attr_32)
    x, src, dst, edge_attr_32 = _rec_inputs()

    def _L0_gnn_setup():
        import jax, jax.numpy as jnp
        import numpy as np
        N = 50000
        E = 25000
        D = 96

        def _mean_aggr(h, src, dst, num_nodes):
            msgs = h[src]
            summed = jax.ops.segment_sum(msgs, dst, num_segments=num_nodes)
            deg = jax.ops.segment_sum(jnp.ones((src.shape[0],), h.dtype), dst, num_segments=num_nodes)
            return summed / jnp.maximum(deg, 1.0)[:, None]

        def _sage_conv(h, src, dst, Wl, bl, Wr, num_nodes):
            agg = _mean_aggr(h, src, dst, num_nodes)
            return agg @ Wl.T + bl + h @ Wr.T
        key = jax.random.key(seed)
        ks = jax.random.split(key, 8)
        s = 1.0 / np.sqrt(D)
        return {'x': jax.random.normal(ks[0], (N, D), dtype=jnp.float32), 'edge_index': jax.random.randint(ks[1], (2, E), 0, N, dtype=jnp.int64), 'Wl1': jax.random.normal(ks[2], (D, D), dtype=jnp.float32) * s, 'bl1': jnp.zeros((D,), dtype=jnp.float32), 'Wr1': jax.random.normal(ks[3], (D, D), dtype=jnp.float32) * s, 'Wl2': jax.random.normal(ks[4], (D, D), dtype=jnp.float32) * s, 'bl2': jnp.zeros((D,), dtype=jnp.float32), 'Wr2': jax.random.normal(ks[5], (D, D), dtype=jnp.float32) * s}
    _L0_gnn_all = _L0_gnn_setup()
    _L0_gnn_in = {k: v for k, v in _L0_gnn_all.items() if k in ('Wl1', 'bl1', 'Wr1', 'Wl2', 'bl2', 'Wr2')}
    del _L0_gnn_all

    def _L1_gnn_setup():
        import jax, jax.numpy as jnp
        import numpy as np
        N, E = (50000, 25000)
        ND, ED = (96, 32)

        def _gelu(x):
            return jax.nn.gelu(x, approximate=False)
        key = jax.random.key(seed)
        ks = jax.random.split(key, 16)
        s = lambda fan_in: 1.0 / np.sqrt(fan_in)
        inp = {'x': jax.random.normal(ks[0], (N, ND), jnp.float32), 'edge_index': jax.random.randint(ks[1], (2, E), 0, N, jnp.int32), 'edge_attr': jax.random.normal(ks[2], (E, ED), jnp.float32), 'mW1': jax.random.uniform(ks[3], (ND + ED, ND), jnp.float32, -s(ND + ED), s(ND + ED)), 'mb1': jnp.zeros((ND,), jnp.float32), 'mW2': jax.random.uniform(ks[4], (ND, ND), jnp.float32, -s(ND), s(ND)), 'mb2': jnp.zeros((ND,), jnp.float32), 'gW1': jax.random.uniform(ks[5], (ND + ED, ND), jnp.float32, -s(ND + ED), s(ND + ED)), 'gb1': jnp.zeros((ND,), jnp.float32), 'gW2': jax.random.uniform(ks[6], (ND, 1), jnp.float32, -s(ND), s(ND)), 'gb2': jnp.zeros((1,), jnp.float32), 'uW1': jax.random.uniform(ks[7], (2 * ND, ND), jnp.float32, -s(2 * ND), s(2 * ND)), 'ub1': jnp.zeros((ND,), jnp.float32), 'uW2': jax.random.uniform(ks[8], (ND, ND), jnp.float32, -s(ND), s(ND)), 'ub2': jnp.zeros((ND,), jnp.float32), 'ln_g': jnp.ones((ND,), jnp.float32), 'ln_b': jnp.zeros((ND,), jnp.float32)}
        return inp
    _L1_gnn_all = _L1_gnn_setup()
    _L1_gnn_in = {k: v for k, v in _L1_gnn_all.items() if k in ('mW1', 'mb1', 'mW2', 'mb2', 'gW1', 'gb1', 'gW2', 'gb2', 'uW1', 'ub1', 'uW2', 'ub2', 'ln_g', 'ln_b')}
    del _L1_gnn_all
    return {'x': x, 'src': src, 'dst': dst, 'edge_attr_32': edge_attr_32, 'L0_gnn_Wl1': _L0_gnn_in['Wl1'], 'L0_gnn_bl1': _L0_gnn_in['bl1'], 'L0_gnn_Wr1': _L0_gnn_in['Wr1'], 'L0_gnn_Wl2': _L0_gnn_in['Wl2'], 'L0_gnn_bl2': _L0_gnn_in['bl2'], 'L0_gnn_Wr2': _L0_gnn_in['Wr2'], 'L1_gnn_mW1': _L1_gnn_in['mW1'], 'L1_gnn_mb1': _L1_gnn_in['mb1'], 'L1_gnn_mW2': _L1_gnn_in['mW2'], 'L1_gnn_mb2': _L1_gnn_in['mb2'], 'L1_gnn_gW1': _L1_gnn_in['gW1'], 'L1_gnn_gb1': _L1_gnn_in['gb1'], 'L1_gnn_gW2': _L1_gnn_in['gW2'], 'L1_gnn_gb2': _L1_gnn_in['gb2'], 'L1_gnn_uW1': _L1_gnn_in['uW1'], 'L1_gnn_ub1': _L1_gnn_in['ub1'], 'L1_gnn_uW2': _L1_gnn_in['uW2'], 'L1_gnn_ub2': _L1_gnn_in['ub2'], 'L1_gnn_ln_g': _L1_gnn_in['ln_g'], 'L1_gnn_ln_b': _L1_gnn_in['ln_b']}

def reference(x, src, dst, edge_attr_32, L0_gnn_Wl1, L0_gnn_bl1, L0_gnn_Wr1, L0_gnn_Wl2, L0_gnn_bl2, L0_gnn_Wr2, L1_gnn_mW1, L1_gnn_mb1, L1_gnn_mW2, L1_gnn_mb2, L1_gnn_gW1, L1_gnn_gb1, L1_gnn_gW2, L1_gnn_gb2, L1_gnn_uW1, L1_gnn_ub1, L1_gnn_uW2, L1_gnn_ub2, L1_gnn_ln_g, L1_gnn_ln_b):
    import jax
    import jax.numpy as jnp

    def _L0_gnn_ref(x, edge_index, Wl1, bl1, Wr1, Wl2, bl2, Wr2):
        import jax, jax.numpy as jnp
        import numpy as np
        N = 50000
        E = 25000
        D = 96

        def _mean_aggr(h, src, dst, num_nodes):
            msgs = h[src]
            summed = jax.ops.segment_sum(msgs, dst, num_segments=num_nodes)
            deg = jax.ops.segment_sum(jnp.ones((src.shape[0],), h.dtype), dst, num_segments=num_nodes)
            return summed / jnp.maximum(deg, 1.0)[:, None]

        def _sage_conv(h, src, dst, Wl, bl, Wr, num_nodes):
            agg = _mean_aggr(h, src, dst, num_nodes)
            return agg @ Wl.T + bl + h @ Wr.T
        src, dst = (edge_index[0], edge_index[1])
        n = x.shape[0]
        h = _sage_conv(x, src, dst, Wl1, bl1, Wr1, n)
        h = jax.nn.relu(h)
        h = _sage_conv(h, src, dst, Wl2, bl2, Wr2, n)
        return h

    def _L1_gnn_ref(x, edge_index, edge_attr, mW1, mb1, mW2, mb2, gW1, gb1, gW2, gb2, uW1, ub1, uW2, ub2, ln_g, ln_b):
        import jax, jax.numpy as jnp
        import numpy as np
        N, E = (50000, 25000)
        ND, ED = (96, 32)

        def _gelu(x):
            return jax.nn.gelu(x, approximate=False)
        src, dst = (edge_index[0], edge_index[1])
        edge_input = jnp.concatenate([x[src], edge_attr], axis=-1)
        messages = _gelu(edge_input @ mW1 + mb1) @ mW2 + mb2
        gates = jax.nn.sigmoid(_gelu(edge_input @ gW1 + gb1) @ gW2 + gb2)
        aggregated = jax.ops.segment_sum(messages * gates, dst, num_segments=x.shape[0])
        combined = jnp.concatenate([x, aggregated], axis=-1)
        update = _gelu(combined @ uW1 + ub1) @ uW2 + ub2
        h = x + update
        mu = jnp.mean(h, axis=-1, keepdims=True)
        var = jnp.mean(jnp.square(h - mu), axis=-1, keepdims=True)
        return (h - mu) * jax.lax.rsqrt(var + 1e-05) * ln_g + ln_b
    edge_index = jnp.stack([src, dst])
    h = jnp.maximum(_layernorm(x, axis=-1), 0.0)
    x = x + _L0_gnn_ref(h, edge_index, L0_gnn_Wl1, L0_gnn_bl1, L0_gnn_Wr1, L0_gnn_Wl2, L0_gnn_bl2, L0_gnn_Wr2)
    h = jnp.maximum(_layernorm(x, axis=-1), 0.0)
    x = x + _L1_gnn_ref(h, edge_index, edge_attr_32, L1_gnn_mW1, L1_gnn_mb1, L1_gnn_mW2, L1_gnn_mb2, L1_gnn_gW1, L1_gnn_gb1, L1_gnn_gW2, L1_gnn_gb2, L1_gnn_uW1, L1_gnn_ub1, L1_gnn_uW2, L1_gnn_ub2, L1_gnn_ln_g, L1_gnn_ln_b)
    return x

_drawn_inputs = setup_inputs


def setup_inputs(seed=0):
    import zlib

    import numpy as np

    out = dict(_drawn_inputs(seed))
    spreads = {'L0_gnn_bl1': (0.0, 0.1),
     'L0_gnn_bl2': (0.0, 0.1),
     'L1_gnn_mb1': (0.0, 0.8),
     'L1_gnn_mb2': (0.0, 0.8),
     'L1_gnn_gb1': (0.0, 0.8),
     'L1_gnn_ub1': (0.0, 0.309),
     'L1_gnn_ub2': (0.0, 0.1),
     'L1_gnn_ln_g': (1.0, 0.2),
     'L1_gnn_ln_b': (0.0, 0.1)}
    factors = {'edge_attr_32': 8.0,
     'L1_gnn_mW1': 8.0,
     'L1_gnn_mW2': 8.0,
     'L1_gnn_gW1': 8.0,
     'L1_gnn_gW2': 8.0}
    for name, (base, spread) in spreads.items():
        noise = np.random.default_rng([zlib.crc32(name.encode()), seed]).standard_normal(out[name].shape)
        drawn = base * np.exp(spread * noise) if base else spread * noise
        out[name] = jnp.asarray(drawn.astype(out[name].dtype))
    for name, factor in factors.items():
        out[name] = (out[name] * factor).astype(out[name].dtype)
    return out
```

```python
import concourse.bass as bass
from concourse import mybir
from contextlib import ExitStack

FP32 = mybir.dt.float32
INT32 = mybir.dt.int32
UINT8 = mybir.dt.uint8
ALU = mybir.AluOpType
ACT = mybir.ActivationFunctionType
AXX = mybir.AxisListType.X

P = 128
D = 96
ED = 32
N = 50000
E = 25000
LN_EPS = 1e-5

T = 5
GROUP_ROWS = P * T
NODE_GROUPS = N // GROUP_ROWS
TAIL = N - NODE_GROUPS * GROUP_ROWS

Q = 4
EDGE_TILES = 200
EP = EDGE_TILES * P
EDGE_GROUPS = EDGE_TILES // Q
SPARE = 2 * Q
ROWS = N + SPARE * P
assert TAIL <= P and EP >= E and EDGE_GROUPS % 2 == 0 and NODE_GROUPS % 2 == 0

RANK_CHUNK = 2560
RANK_CHUNKS = EP // RANK_CHUNK
INDEX_STEP = 1.0 / 32768.0
assert EP < 32768

ZERO_COLS = 1250
ZERO_CHUNKS = N * D // P // ZERO_COLS
assert ZERO_CHUNKS * ZERO_COLS * P == N * D


class Group:

    def __init__(self, n, slot, use):
        self.n, self.slot, self.use = n, slot, use

    def second(self):
        return not (isinstance(self.n, int) and self.n < 2)


def pipelined(engine, groups, step):
    def fixed(n):
        return Group(n, n % 2, n // 2)

    step(fixed(0), None)
    step(fixed(1), fixed(0))
    step(fixed(2), fixed(1))
    with engine.Fori(1, groups // 2 - 1) as i:
        step(Group(2 * i + 1, 1, i), Group(2 * i, 0, i))
        step(Group(2 * i + 2, 0, i + 1), Group(2 * i + 1, 1, i))
    step(fixed(groups - 1), fixed(groups - 2))
    step(None, fixed(groups - 1))


def gnn_kernel(nc, x, src, dst, edge_attr, Wl1t, bl1, Wr1t, Wl2t, bl2, Wr2t, mW1, mb1, mW2, mb2, gW1, gb1, gW2, gb2,
               uW1, ub1, uW2, ub2, ln_g, ln_b, out):
    ctx = ExitStack()
    with ctx:
        def sb(name, shape, dt=FP32):
            return ctx.enter_context(nc.sbuf_tensor(name, shape, dt))

        of_stage = None

        def sem(name):
            if of_stage is None:
                return ctx.enter_context(nc.semaphore(name))
            of_stage.append(nc.alloc_semaphore(name))
            return of_stage[-1]

        def run(part, *args):
            nonlocal of_stage
            of_stage = []
            part(*args)
            nc.clear_and_free_semaphores(of_stage)
            nc.all_engine_barrier()
            of_stage = None

        s_seen = sem("s_seen")

        def wait_apart(engine, semaphore, value):
            engine.wait_ge(semaphore, value)
            engine.sem_inc(s_seen, 1)

        def dram(name, shape, dt=FP32):
            return nc.dram_tensor(name, shape, dt, kind="Internal").ap()

        pre1 = dram("pre1", (ROWS, D))
        x1 = dram("x1", (ROWS, D))
        aggu = dram("aggu", (ROWS, D))
        src_sorted = dram("src_sorted", (EP, 1), INT32)
        dst_sorted = dram("dst_sorted", (EP, 1), INT32)
        attr_sorted = dram("attr_sorted", (EP, ED))

        ident = sb("ident", [P, P])
        causal = sb("causal", [P, P])
        ones = sb("ones", [P, P])
        minus_half = sb("minus_half", [P, T])
        zeros = sb("zeros", [P, ZERO_COLS])
        wr1 = sb("wr1", [D + 1, D])
        wl1 = sb("wl1", [D + 1, D + 1])
        wr2 = sb("wr2", [D + 1, D])
        wl2 = sb("wl2", [D, D])
        mw1 = sb("mw1", [P, D])
        gw1 = sb("gw1", [P, D])
        mb1c = sb("mb1c", [D, 1])
        gb1c = sb("gb1c", [D, 1])
        mw2 = sb("mw2", [D + 1, D])
        gw2 = sb("gw2", [D + 1, 1])
        uw1n = sb("uw1n", [D, D])
        uw1e = sb("uw1e", [D, D])
        ub1c = sb("ub1c", [D, 1])
        uw2 = sb("uw2", [D + 1, D])
        lng = sb("lng", [P, D])
        lnb = sb("lnb", [P, D])

        same = sb("same", [P, EDGE_TILES, P])
        dst_wide = same.bitcast(INT32) if False else None
        follows = sb("follows", [P, EDGE_TILES, P], UINT8)
        src_i = sb("src_i", [P, EDGE_TILES], INT32)
        dst_i = sb("dst_i", [P, EDGE_TILES], INT32)
        next_i = sb("next_i", [P, EDGE_TILES], INT32)
        dst_f = sb("dst_f", [P, EDGE_TILES])
        row_i = sb("row_i", [P, EDGE_TILES], INT32)
        inv_deg = sb("inv_deg", [P, EDGE_TILES])
        carry0 = sb("carry0", [P, 1])

        rows_in = sb("rows_in", [P, 2, T * D])
        rows_in2 = sb("rows_in2", [P, 2, T * D])
        stats = sb("stats", [P, 2, T, 6])
        moments = sb("moments", [P, 2, T, 2])
        var_eps = sb("var_eps", [P, 2, T])
        rstd = sb("rstd", [P, 2, T])
        stats2 = sb("stats2", [P, 2, T, 6])
        moments2 = sb("moments2", [P, 2, T, 2])
        var_eps2 = sb("var_eps2", [P, 2, T])
        rstd2 = sb("rstd2", [P, 2, T])
        normed = sb("normed", [P, 2, T * D])
        cols = sb("cols", [D + 1, 2, T * P])
        cols2 = sb("cols2", [D + 1, 2, T * P])
        rows_mid = sb("rows_mid", [P, 2, T * D])
        rows_out = sb("rows_out", [P, 2, T * D])
        edge_in = sb("edge_in", [P, 2, Q * P])
        msgs = sb("msgs", [P, 2, Q, D + 1])
        aggs = sb("aggs", [D + 1, 2, Q * P])
        gate = sb("gate", [P, 2, Q])
        gate1 = sb("gate1", [P, 2, Q])
        idx = sb("idx", [P, 2, Q], INT32)
        to_row = sb("to_row", [P, 2, Q], INT32)

        psum = ctx.enter_context(nc.psum_tensor("psum", [P, 8, 512], FP32))

        def two_banks(b, w):
            return psum[:, b:b + 2, :].rearrange("p b n -> p (b n)")[:, 0:w]

        def bank(b, w):
            return psum[:, b, 0:w]

        dst_wide = same[:, :, :].bitcast(INT32)

        s_weights = sem("s_weights")
        s_edges = sem("s_edges")
        s_attr = sem("s_attr")
        s_const = sem("s_const")
        s_const_step = sem("s_const_step")
        s_spare = sem("s_spare")
        s_order = sem("s_order")
        s_inversions = sem("s_inversions")
        s_flag = sem("s_flag")
        flag_f = sb("flag_f", [P, 1])
        flag_i = sb("flag_i", [1, 1], INT32)
        scr = [sb(f"order_scratch{k}", [P, EDGE_TILES]) for k in range(3)]

        with nc.Block() as block:
            @block.sync
            def _(sp):
                sp.dma_start(src_i[:, :], src.rearrange("(e p) -> p e", p=P) if False else src).then_inc(s_edges, 16)
                sp.dma_start(dst_i[:, :], dst[0]).then_inc(s_edges, 16)
                sp.dma_start(next_i[:, :], dst[1]).then_inc(s_edges, 16)
                flat = dst[2].rearrange("p e -> (p e)")
                sp.dma_start(dst_wide.rearrange("p e i -> p (e i)"),
                             flat.rearrange("(a n) -> a n", a=1).broadcast_to([P, EP])).then_inc(s_edges, 16)
                loads = [(wr1[0:D, :], Wr1t), (wr1[D:D + 1, :], bl1), (wl1[0:D, 0:D], Wl1t),
                         (wr2[0:D, :], Wr2t), (wr2[D:D + 1, :], bl2), (wl2[:, :], Wl2t),
                         (mw1[:, :], mW1), (gw1[:, :], gW1), (mb1c[:, :], mb1), (gb1c[:, :], gb1),
                         (mw2[0:D, :], mW2), (mw2[D:D + 1, :], mb2), (gw2[0:D, :], gW2), (gw2[D:D + 1, :], gb2),
                         (uw1n[:, :], uW1[0:D, :]), (uw1e[:, :], uW1[D:2 * D, :]), (ub1c[:, :], ub1),
                         (uw2[0:D, :], uW2), (uw2[D:D + 1, :], ub2),
                         (lng[:, :], ln_g.broadcast_to([P, D])), (lnb[:, :], ln_b.broadcast_to([P, D]))]
                sp.wait_ge(s_const, 1)
                for dest, source in loads:
                    sp.dma_start(dest, source).then_inc(s_weights, 16)
                sp.dma_start(attr_sorted.rearrange("(p a) n -> p (a n)", p=P),
                             edge_attr.rearrange("(p a) n -> p (a n)", p=P)).then_inc(s_attr, 16)
                for rows in (pre1, x1):
                    sp.dma_start(rows[N:ROWS, :].rearrange("(p a) n -> p (a n)", p=P),
                                 zeros[:, 0:SPARE * D]).then_inc(s_spare, 16)
                sp.wait_ge(s_weights, 16 * len(loads))
                sp.wait_ge(s_attr, 16)
                sp.wait_ge(s_spare, 32)

            @block.gpsimd
            def _(pool):
                step = [0]

                def done(instruction):
                    step[0] += 1
                    instruction.then_inc(s_const_step, 1)
                    pool.wait_ge(s_const_step, step[0])

                done(pool.memset(wl1[:, :], 0.0))
                done(pool.memset(wl1[D:D + 1, D:D + 1], 1.0))
                done(pool.memset(zeros[:, :], 0.0))
                pool.memset(ones[:, :], 1.0).then_inc(s_const, 1)
                pool.wait_ge(s_const, 1)
                done(pool.memset(minus_half[:, :], -0.5))
                done(pool.memset(carry0[:, :], 0.0))
                done(pool.memset(cols[D:D + 1, :, :], 1.0))
                done(pool.memset(cols2[D:D + 1, :, :], 1.0))
                done(pool.memset(msgs[:, :, :, D:D + 1], 1.0))
                done(pool.affine_select(out=ident[:, :], in_=ones[:, :], compare_op=ALU.is_equal, fill=0.0, base=0,
                                        pattern=[[-1, P]], channel_multiplier=1))
                done(pool.affine_select(out=causal[:, :], in_=ones[:, :], compare_op=ALU.is_ge, fill=0.0, base=0,
                                        pattern=[[1, P]], channel_multiplier=-1))
                done(pool.iota(row_i[:, :].rearrange("p (a b) -> p a b", b=SPARE),
                               [[0, EDGE_TILES // SPARE], [P, SPARE]], base=N, channel_multiplier=1))

            @block.vector
            def _(dve):
                dve.wait_ge(s_edges, 64)
                nc.vector.tensor_tensor(scr[0][:, :], dst_i[:, :], next_i[:, :], ALU.is_gt).then_inc(s_order, 1)
                dve.wait_ge(s_order, 1)
                nc.vector.reduce_sum(flag_f[:, :], scr[0][:, :], AXX).then_inc(s_order, 1)
                dve.wait_ge(s_inversions, 1)
                nc.vector.tensor_copy(flag_i[:, :], psum[0:1, 0, 0:1]).then_inc(s_flag, 1)

            @block.tensor
            def _(pe):
                pe.wait_ge(s_order, 2)
                pe.wait_ge(s_const, 1)
                nc.tensor.matmul(psum[0:1, 0, 0:1], flag_f[:, :], ones[:, 0:1], start=True,
                                 stop=True).then_inc(s_inversions, 1)

        place_f = [sb(f"place_f{k}", [P, 1]) for k in range(1)][0]
        place_i = sb("place_i", [P, 1], INT32)
        counts = sb("counts", [P, RANK_CHUNKS])
        limits = sb("limits", [P, RANK_CHUNKS])
        frac_i = follows[:, 0:4 * RANK_CHUNK // P, :].rearrange("p e i -> p (e i)").bitcast(INT32)
        frac = follows[:, 80:80 + 4 * RANK_CHUNK // P, :].rearrange("p e i -> p (e i)").bitcast(FP32)
        diff = rows_in[:, :, :].rearrange("p s n -> p (s n)")[:, 0:0 + 2 * T * D]
        del diff
        diff = sb("diff", [P, RANK_CHUNK])
        attr_tile = sb("attr_tile", [P, ED])
        own_i = sb("own_i", [P, 2], INT32)
        index_i = sb("index_i", [P, EDGE_TILES], INT32)
        r_iota = sem("r_iota")
        r_prep = sem("r_prep")
        r_step = sem("r_step")
        r_place = sem("r_place")
        r_attr = sem("r_attr")
        r_moved = sem("r_moved")
        r_done = sem("r_done")
        r_sorted = sem("r_sorted")
        index_f = scr[1]
        limit_base = scr[2]

        with nc.Block() as block:
            @block.gpsimd
            def _(pool):
                unsorted = pool.value_load(flag_i[0:1, 0:1], min_val=0, max_val=EP)
                with pool.If(unsorted > 0):
                    pool.iota(frac_i, [[1, RANK_CHUNK]], base=0, channel_multiplier=0).then_inc(r_iota, 1)
                    pool.iota(index_i[:, :], [[P, EDGE_TILES]], base=0, channel_multiplier=1).then_inc(r_iota, 1)
                    pool.wait_ge(r_iota, 2)
                    pool.sem_inc(r_done, 1)
                    with pool.Fori(0, EDGE_TILES) as e:
                        pool.dma_start(attr_tile[:, :], edge_attr.rearrange("(e p) n -> e p n", p=P)[e])\
                            .then_inc(r_attr, 16)
                        pool.wait_ge(r_attr, 16 * e + 16)
                        wait_apart(pool, r_place, e + 1)
                        at = bass.IndirectOffsetOnAxis(ap=place_i[:, 0:1], axis=0)
                        pool.indirect_dma_start(src_sorted, at, own_i[:, 0:1], None).then_inc(r_moved, 16)
                        pool.indirect_dma_start(dst_sorted, at, own_i[:, 1:2], None).then_inc(r_moved, 16)
                        pool.indirect_dma_start(attr_sorted, at, attr_tile[:, :], None).then_inc(r_moved, 16)
                        pool.wait_ge(r_moved, 48 * e + 48)
                        pool.sem_inc(r_done, 1)
                    with pool.Fori(0, EDGE_TILES) as e:
                        with nc.allow_non_contiguous_dma(reason="one index per partition"):
                            by_tile = [a.rearrange("(e p) n -> e p n", p=P) for a in (src_sorted, dst_sorted)]
                            pool.dma_start(src_i[:, bass.ds(e, 1)], by_tile[0][e]).then_inc(r_sorted, 16)
                            pool.dma_start(dst_i[:, bass.ds(e, 1)], by_tile[1][e]).then_inc(r_sorted, 16)
                        pool.wait_ge(r_sorted, 32 * e + 32)
                    with pool.Fori(0, EDGE_TILES - 1) as e:
                        after = dst_sorted[1:EP - P + 1, :].rearrange("(e p) n -> e p n", p=P)
                        pool.dma_start(next_i[:, bass.ds(e, 1)], after[e]).then_inc(r_sorted, 16)
                        pool.wait_ge(r_sorted, 16 * e + 32 * EDGE_TILES + 16)
                    pool.dma_start(next_i[0:P - 1, EDGE_TILES - 1:EDGE_TILES], dst_sorted[EP - P + 1:EP, :])\
                        .then_inc(r_sorted, 16)
                    pool.wait_ge(r_sorted, 16 * (3 * EDGE_TILES))
                    pool.dma_start(dst_wide.rearrange("p e i -> p (e i)"),
                                   dst_sorted.rearrange("a n -> n a").broadcast_to([P, EP])).then_inc(r_sorted, 16)
                    pool.wait_ge(r_sorted, 16 * (3 * EDGE_TILES + 1))
                with pool.Else():
                    pool.sem_inc(r_iota, 1)

            @block.vector
            def _(dve):
                unsorted = dve.value_load(flag_i[0:1, 0:1], min_val=0, max_val=EP)
                with dve.If(unsorted > 0):
                    dve.wait_ge(r_iota, 2)
                    nc.vector.tensor_scalar(frac, frac_i, INDEX_STEP, None, ALU.mult).then_inc(r_prep, 1)
                    nc.vector.tensor_scalar(index_f[:, :], index_i[:, :], INDEX_STEP, None, ALU.mult)\
                        .then_inc(r_prep, 1)
                    nc.vector.tensor_copy(dst_f[:, :], dst_i[:, :]).then_inc(r_prep, 1)
                    nc.vector.tensor_scalar(limit_base[:, 0:RANK_CHUNKS], index_i[:, 0:RANK_CHUNKS], 0.0, None,
                                            ALU.mult).then_inc(r_prep, 1)
                    dve.wait_ge(r_prep, 4)
                    for c in range(RANK_CHUNKS):
                        nc.vector.memset(limit_base[:, c:c + 1], -c * RANK_CHUNK * INDEX_STEP).then_inc(r_prep, 1)
                    dve.wait_ge(r_prep, 4 + RANK_CHUNKS)
                    per_tile = 2 * RANK_CHUNKS + 5
                    with dve.Fori(0, EDGE_TILES) as e:
                        step = [0]

                        def done(instruction):
                            step[0] += 1
                            instruction.then_inc(r_step, 1)
                            dve.wait_ge(r_step, e * per_tile + step[0])

                        done(nc.vector.tensor_scalar(limits[:, :], limit_base[:, 0:RANK_CHUNKS],
                                                     index_f[:, bass.ds(e, 1)], None, ALU.add))
                        for c in range(RANK_CHUNKS):
                            wide = dst_wide.rearrange("p e i -> p (e i)")[:, c * RANK_CHUNK:(c + 1) * RANK_CHUNK]
                            done(nc.vector.scalar_tensor_tensor(out=diff[:, :], in0=wide,
                                                                scalar=dst_f[:, bass.ds(e, 1)], in1=frac,
                                                                op0=ALU.subtract, op1=ALU.add))
                            done(nc.vector.tensor_scalar(diff[:, :], diff[:, :], limits[:, c:c + 1], 0.0,
                                                         ALU.is_lt, ALU.add, accum_out=counts[:, c:c + 1]))
                        done(nc.vector.reduce_sum(place_f[:, :], counts[:, :], AXX))
                        dve.wait_ge(r_done, e + 1)
                        done(nc.vector.tensor_copy(own_i[:, 0:1], src_i[:, bass.ds(e, 1)]))
                        done(nc.vector.tensor_copy(own_i[:, 1:2], dst_i[:, bass.ds(e, 1)]))
                        done(nc.vector.tensor_copy(place_i[:, :], place_f[:, :]))
                        nc.vector.memset(counts[:, :], 0.0).then_inc(r_place, 1)
                with dve.Else():
                    dve.sem_inc(r_prep, 1)

        m_step = sem("m_step")
        m_wide = sem("m_wide")
        MASK_TILES = 8
        with nc.Block() as block:
            @block.vector
            def _(dve):
                step = [0]

                def done(instruction):
                    step[0] += 1
                    instruction.then_inc(m_step, 1)
                    dve.wait_ge(m_step, step[0])

                done(nc.vector.memset(follows[:, 0:1, :], 0.0))
                a, b, c = scr
                done(nc.vector.tensor_copy(dst_f[:, :], dst_i[:, :]))
                done(nc.vector.tensor_tensor(a[:, :], dst_i[:, :], next_i[:, :], ALU.not_equal))
                done(nc.vector.tensor_scalar(b[:, :], dst_f[:, :], float(N), None, ALU.is_lt))
                done(nc.vector.tensor_tensor(a[:, :], a[:, :], b[:, :], ALU.mult))
                done(nc.vector.tensor_copy(c[:, :], row_i[:, :]))
                done(nc.vector.tensor_tensor(b[:, :], dst_f[:, :], c[:, :], ALU.subtract))
                done(nc.vector.tensor_tensor(b[:, :], b[:, :], a[:, :], ALU.mult))
                done(nc.vector.tensor_tensor(row_i[:, :], b[:, :], c[:, :], ALU.add))
                ins = nc.vector.tensor_tensor(follows[:, 1:EDGE_TILES, :], dst_wide[:, 1:EDGE_TILES, :],
                                              dst_wide[:, 0:EDGE_TILES - 1, P - 1:P]
                                              .broadcast_to([P, EDGE_TILES - 1, P]), ALU.is_equal)
                done(ins)
                first = step[0]
                with dve.Fori(0, EDGE_TILES // MASK_TILES) as i:
                    for k in range(MASK_TILES):
                        e = i * MASK_TILES + k
                        nc.vector.scalar_tensor_tensor(
                            out=same[:, bass.ds(e, 1), :].rearrange("p a i -> p (a i)"),
                            in0=dst_wide[:, bass.ds(e, 1), :].rearrange("p a i -> p (a i)"),
                            scalar=dst_f[:, bass.ds(e, 1)], in1=causal[:, :],
                            op0=ALU.is_equal, op1=ALU.mult).then_inc(m_wide, 1)
                dve.wait_ge(m_wide, EDGE_TILES)

        def by_group(rows):
            return rows[0:NODE_GROUPS * GROUP_ROWS, :].rearrange("(g p t) d -> g p (t d)", p=P, t=T)

        def tail(rows):
            return rows[NODE_GROUPS * GROUP_ROWS:N, :]

        def node_pass(name, source, addend, norm, weight, dest):
            loaded = [sem(f"{name}_loaded{s}") for s in range(2)]
            addend_in = [sem(f"{name}_addend{s}") for s in range(2)]
            stats_done = sem(f"{name}_stats")
            moments_done = sem(f"{name}_moments")
            var_done = sem(f"{name}_var")
            rstd_done = sem(f"{name}_rstd")
            normed_done = sem(f"{name}_normed")
            turned = sem(f"{name}_turned")
            cols_done = sem(f"{name}_cols")
            product = sem(f"{name}_product")
            result = sem(f"{name}_result")
            stored = [sem(f"{name}_stored{s}") for s in range(2)]
            G = NODE_GROUPS
            uses = G // 2
            END = Group(G, 0, uses)

            def shape(g):
                return (TAIL, 1) if g is END else (P, T)

            with nc.Block() as block:
                @block.sync
                def _(sp):
                    def load(g):
                        p, t = shape(g)
                        if g.second():
                            if norm:
                                sp.wait_ge(normed_done, g.n - 1)
                            else:
                                sp.wait_ge(turned, g.n - 1)
                        at = tail(source) if g is END else by_group(source)[g.n]
                        sp.dma_start(rows_in[0:p, g.slot, 0:t * D], at).then_inc(loaded[g.slot], 16)
                        if addend is not None:
                            if g.second():
                                sp.wait_ge(result, g.n - 1)
                            at = tail(addend) if g is END else by_group(addend)[g.n]
                            sp.dma_start(rows_in2[0:p, g.slot, 0:t * D], at).then_inc(addend_in[g.slot], 16)

                    load(Group(0, 0, 0))
                    load(Group(1, 1, 0))
                    with sp.Fori(1, G // 2) as i:
                        load(Group(2 * i, 0, i))
                        load(Group(2 * i + 1, 1, i))
                    load(END)

                if norm:
                    @block.gpsimd
                    def _(pool):
                        def root(g):
                            p, t = shape(g)
                            wait_apart(pool, moments_done, g.n + 1)
                            if g.second():
                                wait_apart(pool, normed_done, g.n - 1)
                            pool.tensor_scalar(var_eps[0:p, g.slot, 0:t], moments[0:p, g.slot, 0:t, 1], LN_EPS,
                                               None, ALU.add).then_inc(var_done, 1)
                            pool.wait_ge(var_done, g.n + 1)
                            pool.tensor_tensor(rstd[0:p, g.slot, 0:t], var_eps[0:p, g.slot, 0:t],
                                               minus_half[0:p, 0:t], ALU.pow).then_inc(rstd_done, 1)

                        pipelined(pool, G, lambda new, old: new and root(new))
                        root(END)

                @block.vector
                def _(dve):
                    def measure(g):
                        p, t = shape(g)
                        dve.wait_ge(loaded[g.slot], 16 * (g.use + 1))
                        for k in range(t):
                            last = nc.vector.bn_stats(stats[0:p, g.slot, k, :],
                                                      rows_in[0:p, g.slot, k * D:(k + 1) * D])
                        last.then_inc(stats_done, 1)
                        wait_apart(dve, stats_done, g.n + 1)
                        for k in range(t):
                            last = nc.vector.bn_aggr(moments[0:p, g.slot, k, :], stats[0:p, g.slot, k, :])
                        last.then_inc(moments_done, 1)

                    def normalize(g):
                        p, t = shape(g)
                        dve.wait_ge(rstd_done, g.n + 1)
                        if g.second():
                            dve.wait_ge(turned, g.n - 1)
                        for k in range(t):
                            last = nc.vector.tensor_scalar(normed[0:p, g.slot, k * D:(k + 1) * D],
                                                           rows_in[0:p, g.slot, k * D:(k + 1) * D],
                                                           moments[0:p, g.slot, k, 0:1], rstd[0:p, g.slot, k:k + 1],
                                                           ALU.subtract, ALU.mult)
                        last.then_inc(normed_done, 1)

                    def add(g):
                        p, t = shape(g)
                        dve.wait_ge(product, g.n + 1)
                        dve.wait_ge(addend_in[g.slot], 16 * (g.use + 1))
                        if g.second():
                            dve.wait_ge(stored[g.slot], 16 * g.use)
                        nc.vector.tensor_tensor(rows_out[0:p, g.slot, 0:t * D], bank(4 + g.slot, t * D)[0:p, :],
                                                rows_in2[0:p, g.slot, 0:t * D], ALU.add).then_inc(result, 1)

                    if norm:
                        def step(new, old):
                            if new:
                                measure(new)
                            if old:
                                normalize(old)

                        pipelined(dve, G, step)
                        measure(END)
                        normalize(END)
                    if addend is not None:
                        pipelined(dve, G, lambda new, old: new and add(new))
                        add(END)

                @block.tensor
                def _(pe):
                    rows = normed if norm else rows_in

                    def turn(g):
                        p, t = shape(g)
                        if norm:
                            pe.wait_ge(normed_done, g.n + 1)
                        else:
                            pe.wait_ge(loaded[g.slot], 16 * (g.use + 1))
                        if g.second():
                            pe.wait_ge(cols_done, g.n - 1)
                        for k in range(t):
                            last = nc.tensor.transpose(two_banks(2 * g.slot, T * P)[0:D, k * P:k * P + p],
                                                       rows[0:p, g.slot, k * D:(k + 1) * D], ident[0:p, 0:p])
                        last.then_inc(turned, 1)

                    def multiply(g):
                        p, t = shape(g)
                        pe.wait_ge(cols_done, g.n + 1)
                        if g.second():
                            pe.wait_ge(result, g.n - 1)
                        for k in range(t):
                            last = nc.tensor.matmul(bank(4 + g.slot, T * D)[0:p, k * D:(k + 1) * D],
                                                    cols[:, g.slot, k * P:k * P + p], weight[:, :],
                                                    start=True, stop=True)
                        last.then_inc(product, 1)

                    def step(new, old):
                        if new:
                            turn(new)
                        if old:
                            multiply(old)

                    pipelined(pe, G, step)
                    turn(END)
                    multiply(END)

                @block.scalar
                def _(act):
                    def rectify(g):
                        p, t = shape(g)
                        act.wait_ge(turned, g.n + 1)
                        if g.second():
                            act.wait_ge(product, g.n - 1)
                        w = (t - 1) * P + p
                        nc.scalar.activation(cols[0:D, g.slot, 0:w], two_banks(2 * g.slot, w)[0:D, :],
                                             ACT.Relu).then_inc(cols_done, 1)

                    def copy_out(g):
                        p, t = shape(g)
                        if addend is None:
                            act.wait_ge(product, g.n + 1)
                            if g.second():
                                act.wait_ge(stored[g.slot], 16 * g.use)
                            nc.scalar.activation(rows_out[0:p, g.slot, 0:t * D], bank(4 + g.slot, t * D)[0:p, :],
                                                 ACT.Copy).then_inc(result, 1)
                        act.wait_ge(result, g.n + 1)
                        at = tail(dest) if g is END else by_group(dest)[g.n]
                        act.dma_start(at, rows_out[0:p, g.slot, 0:t * D]).then_inc(stored[g.slot], 16)

                    def step(new, old):
                        if new:
                            rectify(new)
                        if old:
                            copy_out(old)

                    pipelined(act, G, step)
                    rectify(END)
                    copy_out(END)
                    act.wait_ge(stored[0], 16 * (uses + 1))
                    act.wait_ge(stored[1], 16 * uses)

        def edge_pass(name, source, kind, weight, dest):
            mlp = kind == "mlp"
            norm = kind != "relu"
            mean = not mlp
            W = D + 1 if kind == "norm" else D
            G = EDGE_GROUPS
            indices = sem(f"{name}_indices")
            gathered = [sem(f"{name}_gathered{s}") for s in range(2)]
            attr_in = [sem(f"{name}_attr{s}") for s in range(2)]
            stats_done = sem(f"{name}_stats")
            moments_done = sem(f"{name}_moments")
            var_done = sem(f"{name}_var")
            rstd_done = sem(f"{name}_rstd")
            normed_done = sem(f"{name}_normed")
            turned = sem(f"{name}_turned")
            cols_done = sem(f"{name}_cols")
            attr_cols = sem(f"{name}_attr_cols")
            hidden = sem(f"{name}_hidden")
            gelu_done = sem(f"{name}_gelu")
            message_done = sem(f"{name}_message")
            tanh_done = sem(f"{name}_tanh")
            gate_done = sem(f"{name}_gate")
            msgs_done = sem(f"{name}_msgs")
            summed = sem(f"{name}_summed")
            carried = sem(f"{name}_carried")
            product = sem(f"{name}_product")
            deg_step = sem(f"{name}_deg")
            result = sem(f"{name}_result")
            targets = sem(f"{name}_targets")
            scattered = [sem(f"{name}_scattered{s}") for s in range(2)]
            zeroed = sem(f"{name}_zeroed")
            gathered_rows = edge_in if mlp else rows_in
            stride = P if mlp else D
            AGG, OUT = 4, 6
            HID, MSG = 1, 3

            def row(g, k):
                return gathered_rows[:, g.slot, k * stride:k * stride + D]

            def agg_slot(g):
                return aggs[0:W, g.slot, :]

            def wide(buffer, g, k):
                return buffer[:, bass.ds(g.n * Q + k, 1), :].rearrange("p a i -> p (a i)")

            with nc.Block() as block:
                @block.sync
                def _(sp):
                    if kind == "norm":
                        flat = aggu[0:N, :].rearrange("(p a) n -> p (a n)", p=P // 8)
                        flat = aggu[0:N, :].rearrange("a n -> (a n)").rearrange("(p m) -> p m", p=P)
                        for c in range(ZERO_CHUNKS):
                            sp.dma_start(flat[:, c * ZERO_COLS:(c + 1) * ZERO_COLS], zeros[:, :])\
                                .then_inc(zeroed, 16)
                        sp.wait_ge(zeroed, 16 * ZERO_CHUNKS)
                    if mlp:
                        def load_attr(g):
                            if g.second():
                                sp.wait_ge(turned, g.n - 1)
                            at = attr_sorted.rearrange("(g q p) n -> g p q n", q=Q, p=P)[g.n]
                            edge_rows = edge_in[:, g.slot, :].rearrange("p (q n) -> p q n", n=P)
                            sp.dma_start(edge_rows[:, :, D:P], at).then_inc(attr_in[g.slot], 16)

                        pipelined(sp, G, lambda new, old: new and load_attr(new))

                @block.gpsimd
                def _(pool):
                    def gather(g):
                        if g.second():
                            pool.wait_ge(gathered[g.slot], 16 * Q * g.use)
                            pool.wait_ge(normed_done if norm else msgs_done, g.n - 1)
                            if mlp:
                                pool.wait_ge(turned, g.n - 1)
                        pool.tensor_copy(idx[:, g.slot, :], src_i[:, bass.ds(g.n * Q, Q)]).then_inc(indices, 1)
                        wait_apart(pool, indices, g.n + 1)
                        for k in range(Q):
                            at = bass.IndirectOffsetOnAxis(ap=idx[:, g.slot, k:k + 1], axis=0)
                            pool.indirect_dma_start(row(g, k), None, source, at).then_inc(gathered[g.slot], 16)

                    def root(g):
                        wait_apart(pool, moments_done, g.n + 1)
                        if g.second():
                            wait_apart(pool, normed_done, g.n - 1)
                        pool.tensor_scalar(var_eps[:, g.slot, 0:Q], moments[:, g.slot, 0:Q, 1], LN_EPS, None,
                                           ALU.add).then_inc(var_done, 1)
                        pool.wait_ge(var_done, g.n + 1)
                        pool.tensor_tensor(rstd[:, g.slot, 0:Q], var_eps[:, g.slot, 0:Q], minus_half[:, 0:Q],
                                           ALU.pow).then_inc(rstd_done, 1)

                    def scatter(g):
                        if g.second():
                            pool.wait_ge(scattered[g.slot], 16 * Q * g.use)
                        pool.tensor_copy(to_row[:, g.slot, :], row_i[:, bass.ds(g.n * Q, Q)]).then_inc(targets, 1)
                        wait_apart(pool, targets, g.n + 1)
                        wait_apart(pool, result, g.n + 1)
                        for k in range(Q):
                            at = bass.IndirectOffsetOnAxis(ap=to_row[:, g.slot, k:k + 1], axis=0)
                            pool.indirect_dma_start(dest, at, rows_out[:, g.slot, k * D:(k + 1) * D], None,
                                                    compute_op=ALU.bypass if mlp else ALU.add)\
                                .then_inc(scattered[g.slot], 16)

                    def step(new, old):
                        if new:
                            gather(new)
                            if norm:
                                root(new)
                        if old:
                            scatter(old)

                    pipelined(pool, G, step)
                    pool.wait_ge(scattered[0], 16 * Q * (G // 2))
                    pool.wait_ge(scattered[1], 16 * Q * (G // 2))

                @block.vector
                def _(dve):
                    def measure(g):
                        dve.wait_ge(gathered[g.slot], 16 * Q * (g.use + 1))
                        for k in range(Q):
                            last = nc.vector.bn_stats(stats[:, g.slot, k, :], row(g, k))
                        last.then_inc(stats_done, 1)
                        wait_apart(dve, stats_done, g.n + 1)
                        for k in range(Q):
                            last = nc.vector.bn_aggr(moments[:, g.slot, k, :], stats[:, g.slot, k, :])
                        last.then_inc(moments_done, 1)

                    def normalize(g):
                        dve.wait_ge(rstd_done, g.n + 1)
                        if g.second():
                            dve.wait_ge(turned if mlp else msgs_done, g.n - 1)
                        for k in range(Q):
                            if mlp:
                                to = row(g, k)
                            else:
                                to = normed[:, g.slot, k * D:(k + 1) * D]
                            last = nc.vector.tensor_scalar(to, row(g, k), moments[:, g.slot, k, 0:1],
                                                           rstd[:, g.slot, k:k + 1], ALU.subtract, ALU.mult)
                        last.then_inc(normed_done, 1)

                    def copy_attr(g):
                        dve.wait_ge(turned, g.n + 1)
                        if g.second():
                            dve.wait_ge(hidden, g.n - 1)
                        nc.vector.tensor_copy(edge_cols[D:P, g.slot, :], bank(0, 512)[D:P, :]).then_inc(attr_cols, 1)

                    def gate_messages(g):
                        dve.wait_ge(tanh_done, g.n + 1)
                        nc.vector.tensor_scalar(gate1[:, g.slot, :], gate[:, g.slot, :], 0.5, 0.5, ALU.mult,
                                                ALU.add).then_inc(gate_done, 1)
                        dve.wait_ge(gate_done, g.n + 1)
                        if g.second():
                            dve.wait_ge(summed, g.n - 1)
                        m = bank(MSG, Q * (D + 1)).rearrange("p (q n) -> p q n", q=Q)[:, :, 0:D]
                        nc.vector.tensor_tensor(msgs[:, g.slot, :, 0:D], m,
                                                gate1[:, g.slot, :].rearrange("p (q a) -> p q a", a=1)
                                                .broadcast_to([P, Q, D]), ALU.mult).then_inc(msgs_done, 1)

                    def carry(g):
                        dve.wait_ge(summed, g.n + 1)
                        if g.second():
                            dve.wait_ge(product, g.n - 1)
                        for k in range(Q):
                            if k:
                                before = aggs[0:W, g.slot, k * P - 1:k * P]
                            elif isinstance(g.n, int) and g.n == 0:
                                before = carry0[0:W, :]
                            else:
                                before = aggs[0:W, 1 - g.slot, Q * P - 1:Q * P]
                            nc.vector.scalar_tensor_tensor(out=aggs[0:W, g.slot, k * P:(k + 1) * P],
                                                           in0=wide(follows, g, k)[0:W, :], scalar=before,
                                                           in1=bank(AGG + g.slot, 512)[0:W, k * P:(k + 1) * P],
                                                           op0=ALU.mult, op1=ALU.add).then_inc(carried, 1)
                            dve.wait_ge(carried, g.n * Q + (k + 1))

                    def finish(g):
                        dve.wait_ge(product, g.n + 1)
                        wv = D + 1 if kind == "norm" else D
                        v = bank(OUT + g.slot, Q * wv).rearrange("p (q n) -> p q n", q=Q)
                        o = rows_out[:, g.slot, 0:Q * D].rearrange("p (q n) -> p q n", q=Q)
                        inv = inv_deg[:, bass.ds(g.n * Q, Q)]
                        if kind == "norm":
                            nc.vector.tensor_scalar(gate[:, g.slot, :], v[:, :, D], 1.0, None, ALU.max)\
                                .then_inc(deg_step, 1)
                            dve.wait_ge(deg_step, 2 * g.n + 1)
                            nc.vector.reciprocal(inv, gate[:, g.slot, :]).then_inc(deg_step, 1)
                            dve.wait_ge(deg_step, 2 * g.n + 2)
                        if g.second():
                            dve.wait_ge(scattered[g.slot], 16 * Q * g.use)
                        if mean:
                            nc.vector.tensor_tensor(o, v[:, :, 0:D], inv.rearrange("p (q a) -> p q a", a=1)
                                                    .broadcast_to([P, Q, D]), ALU.mult).then_inc(result, 1)
                        else:
                            nc.vector.tensor_copy(o, v[:, :, 0:D]).then_inc(result, 1)

                    def step(new, old):
                        if new and norm:
                            measure(new)
                            if mlp:
                                normalize(new)
                        if old:
                            if mlp:
                                gate_messages(old)
                            carry(old)
                        if new and norm:
                            if mlp:
                                copy_attr(new)
                            else:
                                normalize(new)
                        if old:
                            finish(old)

                    pipelined(dve, G, step)

                @block.scalar
                def _(act):
                    def rectify(g):
                        if norm:
                            act.wait_ge(normed_done, g.n + 1)
                        else:
                            act.wait_ge(gathered[g.slot], 16 * Q * (g.use + 1))
                        if g.second():
                            act.wait_ge(summed, g.n - 1)
                        rows = normed if norm else rows_in
                        nc.scalar.activation(msgs[:, g.slot, :, 0:D],
                                             rows[:, g.slot, 0:Q * D].rearrange("p (q n) -> p q n", q=Q),
                                             ACT.Relu).then_inc(msgs_done, 1)

                    def rectify_cols(g):
                        act.wait_ge(turned, g.n + 1)
                        if g.second():
                            act.wait_ge(hidden, g.n - 1)
                        nc.scalar.activation(edge_cols[0:D, g.slot, :], bank(0, 512)[0:D, :], ACT.Relu)\
                            .then_inc(cols_done, 1)

                    def gelus(g):
                        act.wait_ge(hidden, g.n + 1)
                        if g.second():
                            act.wait_ge(message_done, g.n - 1)
                        nc.scalar.activation(cols[0:D, g.slot, 0:Q * P], bank(HID, 512)[0:D, :], ACT.Gelu,
                                             bias=mb1c[:, :])
                        nc.scalar.activation(cols2[0:D, g.slot, 0:Q * P], bank(HID + 1, 512)[0:D, :], ACT.Gelu,
                                             bias=gb1c[:, :]).then_inc(gelu_done, 1)

                    def tanh(g):
                        act.wait_ge(message_done, g.n + 1)
                        if g.second():
                            act.wait_ge(gate_done, g.n - 1)
                        z = bank(MSG, Q * (D + 1)).rearrange("p (q n) -> p q n", q=Q)[:, :, D]
                        nc.scalar.activation(gate[:, g.slot, :], z, ACT.Tanh, scale=0.5).then_inc(tanh_done, 1)

                    if not mlp:
                        pipelined(act, G, lambda new, old: new and rectify(new))
                    else:
                        def step(new, old):
                            if old:
                                gelus(old)
                                tanh(old)
                            if new:
                                rectify_cols(new)

                        pipelined(act, G, step)

                @block.tensor
                def _(pe):
                    def turn(g):
                        pe.wait_ge(normed_done, g.n + 1)
                        pe.wait_ge(attr_in[g.slot], 16 * (g.use + 1))
                        if not (isinstance(g.n, int) and g.n == 0):
                            pe.wait_ge(cols_done, g.n)
                            pe.wait_ge(attr_cols, g.n)
                        for k in range(Q):
                            last = nc.tensor.transpose(bank(0, 512)[:, k * P:(k + 1) * P],
                                                       edge_in[:, g.slot, k * P:(k + 1) * P], ident[:, :])
                        last.then_inc(turned, 1)

                    def hide(g):
                        pe.wait_ge(cols_done, g.n + 1)
                        pe.wait_ge(attr_cols, g.n + 1)
                        if not (isinstance(g.n, int) and g.n == 0):
                            pe.wait_ge(gelu_done, g.n)
                        nc.tensor.matmul(bank(HID, 512)[0:D, :], mw1[:, :], edge_cols[:, g.slot, :], start=True,
                                         stop=True)
                        nc.tensor.matmul(bank(HID + 1, 512)[0:D, :], gw1[:, :], edge_cols[:, g.slot, :], start=True,
                                         stop=True).then_inc(hidden, 1)

                    def message(g):
                        pe.wait_ge(gelu_done, g.n + 1)
                        if not (isinstance(g.n, int) and g.n == 0):
                            pe.wait_ge(msgs_done, g.n)
                            pe.wait_ge(tanh_done, g.n)
                        for k in range(Q):
                            at = k * (D + 1)
                            nc.tensor.matmul(bank(MSG, 512)[:, at:at + D], cols[:, g.slot, k * P:(k + 1) * P],
                                             mw2[:, :], start=True, stop=True)
                            last = nc.tensor.matmul(bank(MSG, 512)[:, at + D:at + D + 1],
                                                    cols2[:, g.slot, k * P:(k + 1) * P], gw2[:, :], start=True,
                                                    stop=True)
                        last.then_inc(message_done, 1)

                    def aggregate(g):
                        pe.wait_ge(msgs_done, g.n + 1)
                        if g.second():
                            pe.wait_ge(carried, (g.n - 1) * Q)
                        for k in range(Q):
                            last = nc.tensor.matmul(bank(AGG + g.slot, 512)[0:W, k * P:(k + 1) * P],
                                                    msgs[:, g.slot, k, 0:W], wide(same, g, k), start=True, stop=True)
                        last.then_inc(summed, 1)

                    def multiply(g):
                        pe.wait_ge(carried, g.n * Q + Q)
                        if g.second():
                            pe.wait_ge(result, g.n - 1)
                        wv = D + 1 if kind == "norm" else D
                        for k in range(Q):
                            last = nc.tensor.matmul(bank(OUT + g.slot, 512)[:, k * wv:(k + 1) * wv],
                                                    aggs[0:W, g.slot, k * P:(k + 1) * P], weight[:, :], start=True,
                                                    stop=True)
                        last.then_inc(product, 1)

                    def step(new, old):
                        if mlp:
                            if old:
                                hide(old)
                            if new:
                                turn(new)
                            if old:
                                message(old)
                                aggregate(old)
                                multiply(old)
                        else:
                            if new:
                                aggregate(new)
                            if old:
                                multiply(old)

                    pipelined(pe, G, step)

        edge_cols = sb("edge_cols", [P, 2, Q * P])

        def update_pass():
            name = "u"
            G = NODE_GROUPS
            uses = G // 2
            END = Group(G, 0, uses)
            loaded = [sem(f"{name}_loaded{s}") for s in range(2)]
            agg_in = [sem(f"{name}_agg{s}") for s in range(2)]
            stats_done = sem("u_stats")
            moments_done = sem("u_moments")
            var_done = sem("u_var")
            rstd_done = sem("u_rstd")
            normed_done = sem("u_normed")
            relu_done = sem("u_relu")
            turned = sem("u_turned")
            cols_done = sem("u_cols")
            product = sem("u_product")
            summed = sem("u_summed")
            turned2 = sem("u_turned2")
            gelu_done = sem("u_gelu")
            product2 = sem("u_product2")
            h_done = sem("u_h")
            stats2_done = sem("u_stats2")
            moments2_done = sem("u_moments2")
            var2_done = sem("u_var2")
            rstd2_done = sem("u_rstd2")
            normed2_done = sem("u_normed2")
            scaled = sem("u_scaled")
            biased = sem("u_biased")
            result = sem("u_result")
            stored = [sem(f"{name}_stored{s}") for s in range(2)]
            h2, agg, mid, fin = normed, rows_in2, rows_mid, rows_out
            def over_masks(k):
                n = -(-2 * T * D // P)
                v = same[:, k * n:(k + 1) * n, :].rearrange("p e i -> p (e i)")[:, 0:2 * T * D]
                return v.rearrange("p (s n) -> p s n", s=2)

            hres, xb, fin_in = (over_masks(k) for k in range(3))

            def shape(g):
                return (TAIL, 1) if g is END else (P, T)

            with nc.Block() as block:
                @block.sync
                def _(sp):
                    def load(g):
                        p, t = shape(g)
                        if g.second():
                            sp.wait_ge(biased, g.n - 1)
                            sp.wait_ge(normed_done, g.n - 1)
                        at = tail(x1) if g is END else by_group(x1)[g.n]
                        sp.dma_start(rows_in[0:p, g.slot, 0:t * D], at).then_inc(loaded[g.slot], 16)
                        if g.second():
                            sp.wait_ge(summed, g.n - 1)
                        at = tail(aggu) if g is END else by_group(aggu)[g.n]
                        sp.dma_start(agg[0:p, g.slot, 0:t * D], at).then_inc(agg_in[g.slot], 16)

                    load(Group(0, 0, 0))
                    load(Group(1, 1, 0))
                    with sp.Fori(1, G // 2) as i:
                        load(Group(2 * i, 0, i))
                        load(Group(2 * i + 1, 1, i))
                    load(END)

                @block.gpsimd
                def _(pool):
                    def root(g):
                        p, t = shape(g)
                        wait_apart(pool, moments_done, g.n + 1)
                        if g.second():
                            wait_apart(pool, normed_done, g.n - 1)
                        pool.tensor_scalar(var_eps[0:p, g.slot, 0:t], moments[0:p, g.slot, 0:t, 1], LN_EPS, None,
                                           ALU.add).then_inc(var_done, 1)
                        pool.wait_ge(var_done, g.n + 1)
                        pool.tensor_tensor(rstd[0:p, g.slot, 0:t], var_eps[0:p, g.slot, 0:t],
                                           minus_half[0:p, 0:t], ALU.pow).then_inc(rstd_done, 1)

                    def bias(g):
                        p, t = shape(g)
                        pool.wait_ge(loaded[g.slot], 16 * (g.use + 1))
                        if g.second():
                            pool.wait_ge(result, g.n - 1)
                        b = lnb[0:p, :].rearrange("p (a d) -> p a d", a=1).broadcast_to([p, t, D])
                        pool.tensor_tensor(xb[0:p, g.slot, 0:t * D].rearrange("p (t d) -> p t d", t=t),
                                           rows_in[0:p, g.slot, 0:t * D].rearrange("p (t d) -> p t d", t=t), b,
                                           ALU.add).then_inc(biased, 1)

                    def root2(g):
                        p, t = shape(g)
                        wait_apart(pool, moments2_done, g.n + 1)
                        if g.second():
                            wait_apart(pool, normed2_done, g.n - 1)
                        pool.tensor_scalar(var_eps2[0:p, g.slot, 0:t], moments2[0:p, g.slot, 0:t, 1], LN_EPS, None,
                                           ALU.add).then_inc(var2_done, 1)
                        pool.wait_ge(var2_done, g.n + 1)
                        pool.tensor_tensor(rstd2[0:p, g.slot, 0:t], var_eps2[0:p, g.slot, 0:t],
                                           minus_half[0:p, 0:t], ALU.pow).then_inc(rstd2_done, 1)

                    def scale(g):
                        p, t = shape(g)
                        pool.wait_ge(normed2_done, g.n + 1)
                        if g.second():
                            pool.wait_ge(result, g.n - 1)
                        gg = lng[0:p, :].rearrange("p (a d) -> p a d", a=1).broadcast_to([p, t, D])
                        v = hres[0:p, g.slot, 0:t * D].rearrange("p (t d) -> p t d", t=t)
                        pool.tensor_tensor(v, v, gg, ALU.mult).then_inc(scaled, 1)

                    def step(new, old):
                        if new:
                            root(new)
                            bias(new)
                        if old:
                            root2(old)
                            scale(old)

                    pipelined(pool, G, step)
                    for part in (root, bias, root2, scale):
                        part(END)

                @block.vector
                def _(dve):
                    def measure(g):
                        p, t = shape(g)
                        dve.wait_ge(loaded[g.slot], 16 * (g.use + 1))
                        for k in range(t):
                            last = nc.vector.bn_stats(stats[0:p, g.slot, k, :],
                                                      rows_in[0:p, g.slot, k * D:(k + 1) * D])
                        last.then_inc(stats_done, 1)
                        wait_apart(dve, stats_done, g.n + 1)
                        for k in range(t):
                            last = nc.vector.bn_aggr(moments[0:p, g.slot, k, :], stats[0:p, g.slot, k, :])
                        last.then_inc(moments_done, 1)

                    def normalize(g):
                        p, t = shape(g)
                        dve.wait_ge(rstd_done, g.n + 1)
                        if g.second():
                            dve.wait_ge(relu_done, g.n - 1)
                        for k in range(t):
                            last = nc.vector.tensor_scalar(mid[0:p, g.slot, k * D:(k + 1) * D],
                                                           rows_in[0:p, g.slot, k * D:(k + 1) * D],
                                                           moments[0:p, g.slot, k, 0:1], rstd[0:p, g.slot, k:k + 1],
                                                           ALU.subtract, ALU.mult)
                        last.then_inc(normed_done, 1)

                    def add_agg(g):
                        p, t = shape(g)
                        dve.wait_ge(product, g.n + 1)
                        dve.wait_ge(agg_in[g.slot], 16 * (g.use + 1))
                        v = agg[0:p, g.slot, 0:t * D]
                        nc.vector.tensor_tensor(fin_in[0:p, g.slot, 0:t * D], bank(6, t * D)[0:p, :], v,
                                                ALU.add).then_inc(summed, 1)

                    def residual(g):
                        p, t = shape(g)
                        dve.wait_ge(product2, g.n + 1)
                        if g.second():
                            dve.wait_ge(result, g.n - 1)
                        nc.vector.tensor_tensor(hres[0:p, g.slot, 0:t * D], bank(7, t * D)[0:p, :],
                                                h2[0:p, g.slot, 0:t * D], ALU.add).then_inc(h_done, 1)
                        dve.wait_ge(h_done, g.n + 1)
                        for k in range(t):
                            last = nc.vector.bn_stats(stats2[0:p, g.slot, k, :],
                                                      hres[0:p, g.slot, k * D:(k + 1) * D])
                        last.then_inc(stats2_done, 1)
                        wait_apart(dve, stats2_done, g.n + 1)
                        for k in range(t):
                            last = nc.vector.bn_aggr(moments2[0:p, g.slot, k, :], stats2[0:p, g.slot, k, :])
                        last.then_inc(moments2_done, 1)

                    def normalize2(g):
                        p, t = shape(g)
                        dve.wait_ge(rstd2_done, g.n + 1)
                        for k in range(t):
                            v = hres[0:p, g.slot, k * D:(k + 1) * D]
                            last = nc.vector.tensor_scalar(v, v, moments2[0:p, g.slot, k, 0:1],
                                                           rstd2[0:p, g.slot, k:k + 1], ALU.subtract, ALU.mult)
                        last.then_inc(normed2_done, 1)

                    def last_add(g):
                        p, t = shape(g)
                        dve.wait_ge(scaled, g.n + 1)
                        dve.wait_ge(biased, g.n + 1)
                        if g.second():
                            dve.wait_ge(stored[g.slot], 16 * g.use)
                        nc.vector.tensor_tensor(fin[0:p, g.slot, 0:t * D], hres[0:p, g.slot, 0:t * D],
                                                xb[0:p, g.slot, 0:t * D], ALU.add).then_inc(result, 1)

                    def step(new, old):
                        if new:
                            measure(new)
                        if old:
                            residual(old)
                        if new:
                            normalize(new)
                        if old:
                            normalize2(old)
                        if new:
                            add_agg(new)
                        if old:
                            last_add(old)

                    pipelined(dve, G, step)
                    for part in (measure, normalize, add_agg, residual, normalize2, last_add):
                        part(END)

                @block.scalar
                def _(act):
                    def rectify(g):
                        p, t = shape(g)
                        act.wait_ge(normed_done, g.n + 1)
                        if g.second():
                            act.wait_ge(h_done, g.n - 1)
                            act.wait_ge(turned, g.n - 1)
                        nc.scalar.activation(h2[0:p, g.slot, 0:t * D], mid[0:p, g.slot, 0:t * D], ACT.Relu)\
                            .then_inc(relu_done, 1)

                    def copy_cols(g):
                        p, t = shape(g)
                        act.wait_ge(turned, g.n + 1)
                        if g.second():
                            act.wait_ge(product, g.n - 1)
                        w = (t - 1) * P + p
                        nc.scalar.activation(cols2[0:D, g.slot, 0:w], two_banks(0, w)[0:D, :], ACT.Copy)\
                            .then_inc(cols_done, 1)

                    def gelu(g):
                        p, t = shape(g)
                        act.wait_ge(turned2, g.n + 1)
                        if g.second():
                            act.wait_ge(product2, g.n - 1)
                        w = (t - 1) * P + p
                        nc.scalar.activation(cols[0:D, g.slot, 0:w], two_banks(2, w)[0:D, :], ACT.Gelu,
                                             bias=ub1c[:, :]).then_inc(gelu_done, 1)

                    def store(g):
                        p, t = shape(g)
                        act.wait_ge(result, g.n + 1)
                        at = tail(out) if g is END else by_group(out)[g.n]
                        act.dma_start(at, fin[0:p, g.slot, 0:t * D]).then_inc(stored[g.slot], 16)

                    def step(new, old):
                        if old:
                            gelu(old)
                        if new:
                            rectify(new)
                            copy_cols(new)
                        if old:
                            store(old)

                    pipelined(act, G, step)
                    for part in (rectify, copy_cols, gelu, store):
                        part(END)
                    act.wait_ge(stored[0], 16 * (uses + 1))
                    act.wait_ge(stored[1], 16 * uses)

                @block.tensor
                def _(pe):
                    def turn(g):
                        p, t = shape(g)
                        pe.wait_ge(relu_done, g.n + 1)
                        if not (isinstance(g.n, int) and g.n == 0):
                            pe.wait_ge(cols_done, g.n)
                        for k in range(t):
                            last = nc.tensor.transpose(two_banks(0, T * P)[0:D, k * P:k * P + p],
                                                       h2[0:p, g.slot, k * D:(k + 1) * D], ident[0:p, 0:p])
                        last.then_inc(turned, 1)

                    def multiply(g):
                        p, t = shape(g)
                        pe.wait_ge(cols_done, g.n + 1)
                        if not (isinstance(g.n, int) and g.n == 0):
                            pe.wait_ge(summed, g.n)
                        for k in range(t):
                            last = nc.tensor.matmul(bank(6, T * D)[0:p, k * D:(k + 1) * D],
                                                    cols2[0:D, g.slot, k * P:k * P + p], uw1n[:, :],
                                                    start=True, stop=True)
                        last.then_inc(product, 1)

                    def turn2(g):
                        p, t = shape(g)
                        pe.wait_ge(summed, g.n + 1)
                        if not (isinstance(g.n, int) and g.n == 0):
                            pe.wait_ge(gelu_done, g.n)
                        for k in range(t):
                            last = nc.tensor.transpose(two_banks(2, T * P)[0:D, k * P:k * P + p],
                                                       fin_in[0:p, g.slot, k * D:(k + 1) * D], ident[0:p, 0:p])
                        last.then_inc(turned2, 1)

                    def multiply2(g):
                        p, t = shape(g)
                        pe.wait_ge(gelu_done, g.n + 1)
                        if not (isinstance(g.n, int) and g.n == 0):
                            pe.wait_ge(h_done, g.n)
                        for k in range(t):
                            last = nc.tensor.matmul(bank(7, T * D)[0:p, k * D:(k + 1) * D],
                                                    cols[:, g.slot, k * P:k * P + p], uw2[:, :],
                                                    start=True, stop=True)
                        last.then_inc(product2, 1)

                    def step(new, old):
                        if old:
                            turn2(old)
                            multiply2(old)
                        if new:
                            turn(new)
                            multiply(new)

                    pipelined(pe, G, step)
                    for part in (turn, multiply, turn2, multiply2):
                        part(END)

        run(node_pass, "a", x, None, True, wr1, pre1)
        run(edge_pass, "ea", x, "norm", wl1, pre1)
        run(node_pass, "b", pre1, x, False, wr2, x1)
        run(edge_pass, "eb", pre1, "relu", wl2, x1)
        run(edge_pass, "ec", x1, "mlp", uw1e, aggu)
        run(update_pass)


def kernel(**inputs):
    import numpy as _np
    import concourse.bacc as _bacc
    from concourse import mybir as _mybir
    from concourse.bass_utils import run_bass_kernel_spmd as _run

    nc = _bacc.Bacc("TRN2", target_bir_lowering=False, num_devices=1)
    get = {k: _np.asarray(v) for k, v in inputs.items()}

    def column(name):
        return get[name].reshape(-1, 1)

    def line(name):
        return get[name].reshape(1, -1)

    src = _np.concatenate([get["src"], _np.zeros(EP - E, get["src"].dtype)])
    dst = _np.concatenate([get["dst"], _np.full(EP - E + 1, N, get["dst"].dtype)])
    attr = _np.concatenate([get["edge_attr_32"], _np.zeros((EP - E, ED), get["edge_attr_32"].dtype)])
    dst3 = _np.stack([dst[:EP].reshape(EDGE_TILES, P).T, dst[1:].reshape(EDGE_TILES, P).T,
                      dst[:EP].reshape(P, EDGE_TILES)])
    laid = [
        ("x", get["x"]), ("src", src.reshape(EDGE_TILES, P).T), ("dst", dst3), ("edge_attr", attr),
        ("Wl1t", get["L0_gnn_Wl1"].T), ("bl1", line("L0_gnn_bl1")), ("Wr1t", get["L0_gnn_Wr1"].T),
        ("Wl2t", get["L0_gnn_Wl2"].T), ("bl2", line("L0_gnn_bl2")), ("Wr2t", get["L0_gnn_Wr2"].T),
        ("mW1", get["L1_gnn_mW1"]), ("mb1", column("L1_gnn_mb1")), ("mW2", get["L1_gnn_mW2"]),
        ("mb2", line("L1_gnn_mb2")), ("gW1", get["L1_gnn_gW1"]), ("gb1", column("L1_gnn_gb1")),
        ("gW2", get["L1_gnn_gW2"]), ("gb2", line("L1_gnn_gb2")), ("uW1", get["L1_gnn_uW1"]),
        ("ub1", column("L1_gnn_ub1")), ("uW2", get["L1_gnn_uW2"]), ("ub2", line("L1_gnn_ub2")),
        ("ln_g", line("L1_gnn_ln_g")), ("ln_b", line("L1_gnn_ln_b")),
    ]
    arrays, args = {}, []
    for name, a in laid:
        a = _np.ascontiguousarray(a)
        arrays[f"in_{name}"] = a
        args.append(nc.dram_tensor(f"in_{name}", a.shape, _mybir.dt.from_np(a.dtype), kind="ExternalInput").ap())
    out = nc.dram_tensor("out_0", (N, D), _mybir.dt.float32, kind="ExternalOutput").ap()
    gnn_kernel(nc, *args, out)
    r = _run(nc, [arrays], core_ids=[0])
    return r.results[0]["out_0"]
```

```python
import concourse.bass as bass
from concourse import mybir
from contextlib import ExitStack

FP32 = mybir.dt.float32
INT32 = mybir.dt.int32
UINT8 = mybir.dt.uint8
ALU = mybir.AluOpType
ACT = mybir.ActivationFunctionType
AXX = mybir.AxisListType.X

P = 128
D = 96
ED = 32
N = 50000
E = 25000
LN_EPS = 1e-5

T = 5
GROUP_ROWS = P * T
NODE_GROUPS = N // GROUP_ROWS
TAIL = N - NODE_GROUPS * GROUP_ROWS

Q = 4
EDGE_TILES = 200
EP = EDGE_TILES * P
EDGE_GROUPS = EDGE_TILES // Q
SPARE = 2 * Q
ROWS = N + SPARE * P
assert TAIL <= P and EP >= E and EDGE_TILES % Q == 0

RANK_CHUNK = 2560
RANK_CHUNKS = EP // RANK_CHUNK
INDEX_STEP = 1.0 / 32768.0
assert EP < 32768

UNROLL = 4
FETCH = (3, 2, 3, 2)
FETCH_AT = (0, 3, 5, 8)
FETCHES = -(-NODE_GROUPS // UNROLL)
assert FETCHES * sum(FETCH) == EDGE_TILES

ZERO_COLS = 1250
ZERO_CHUNKS = N * D // P // ZERO_COLS
assert ZERO_CHUNKS * ZERO_COLS * P == N * D


class Group:

    def __init__(self, i, c):
        self.n, self.i, self.c = UNROLL * i + c, i, c

    def slot(self, slots):
        return self.c % slots

    def use(self, slots):
        return (UNROLL // slots) * self.i + self.c // slots

    def reuses(self, slots):
        return not (isinstance(self.n, int) and self.n < slots)


def pipelined(engine, groups, *stages):
    last_lag = max(lag for lag, _ in stages)
    first = UNROLL * -(-(last_lag + 2) // UNROLL)
    bodies = (groups - first) // UNROLL

    def step(i, c):
        for lag, part in stages:
            g = Group(i + (c - lag) // UNROLL, (c - lag) % UNROLL)
            if not isinstance(g.n, int) or 0 <= g.n < groups:
                part(g)

    for t in range(first):
        step(t // UNROLL, t % UNROLL)
    with engine.Fori(first // UNROLL, first // UNROLL + bodies) as i:
        for c in range(UNROLL):
            step(i, c)
    for t in range(first + UNROLL * bodies, groups + last_lag):
        step(t // UNROLL, t % UNROLL)


def gnn_kernel(nc, x, src, dst, edge_attr, Wl1t, bl1, Wr1t, Wl2t, bl2, Wr2t, mW1, mb1, mW2, mb2, gW1, gb1, gW2, gb2,
               uW1, ub1, uW2, ub2, ln_g, ln_b, out):
    ctx = ExitStack()
    with ctx:
        def sb(name, shape, dt=FP32):
            return ctx.enter_context(nc.sbuf_tensor(name, shape, dt))

        of_stage = None

        def sem(name):
            if of_stage is None:
                return ctx.enter_context(nc.semaphore(name))
            of_stage.append(nc.alloc_semaphore(name))
            return of_stage[-1]

        def run(part, *args):
            nonlocal of_stage
            of_stage = []
            part(*args)
            nc.clear_and_free_semaphores(of_stage)
            nc.all_engine_barrier()
            of_stage = None

        s_seen = sem("s_seen")

        def wait_apart(engine, semaphore, value):
            engine.wait_ge(semaphore, value)
            engine.sem_inc(s_seen, 1)

        def dram(name, shape, dt=FP32):
            return nc.dram_tensor(name, shape, dt, kind="Internal").ap()

        pre1 = dram("pre1", (ROWS, D))
        x1 = dram("x1", (ROWS, D))
        aggu = dram("aggu", (ROWS, D))
        src_sorted = dram("src_sorted", (EP, 1), INT32)
        dst_sorted = dram("dst_sorted", (EP, 1), INT32)
        attr_sorted = dram("attr_sorted", (EP, ED))

        ident = sb("ident", [P, P])
        causal = sb("causal", [P, P])
        ones = sb("ones", [P, P])
        minus_half = sb("minus_half", [P, T])
        zeros = sb("zeros", [P, ZERO_COLS])
        wr1 = sb("wr1", [D + 1, D])
        wl1 = sb("wl1", [D + 1, D + 1])
        wr2 = sb("wr2", [D + 1, D])
        wl2 = sb("wl2", [D, D])
        mw1 = sb("mw1", [P, D])
        gw1 = sb("gw1", [P, D])
        mb1c = sb("mb1c", [D, 1])
        gb1c = sb("gb1c", [D, 1])
        mw2 = sb("mw2", [D + 1, D])
        gw2 = sb("gw2", [D + 1, 1])
        uw1n = sb("uw1n", [D, D])
        uw1e = sb("uw1e", [D, D])
        ub1c = sb("ub1c", [D, 1])
        uw2 = sb("uw2", [D + 1, D])
        lng = sb("lng", [P, D])
        lnb = sb("lnb", [P, D])

        same = sb("same", [P, EDGE_TILES, P], UINT8)
        follows = sb("follows", [P, EDGE_TILES, P], UINT8)
        src_i = sb("src_i", [P, EDGE_TILES], INT32)
        dst_i = sb("dst_i", [P, EDGE_TILES], INT32)
        next_i = sb("next_i", [P, EDGE_TILES], INT32)
        dst_f = sb("dst_f", [P, EDGE_TILES])
        row_i = sb("row_i", [P, EDGE_TILES], INT32)
        inv_deg = sb("inv_deg", [P, EDGE_TILES])
        carry0 = sb("carry0", [P, 1])

        region = sb("region", [P, EDGE_TILES * P])
        taken = [0]

        def part_of_region(slots, width):
            at = taken[0]
            taken[0] += slots * width
            assert taken[0] <= EDGE_TILES * P
            return region[:, at:taken[0]].rearrange("p (s n) -> p s n", s=slots)

        dst_wide = region[:, :].bitcast(INT32).rearrange("p (e i) -> p e i", i=P)
        edge_rows = part_of_region(EDGE_TILES, D)
        fetched = part_of_region(sum(FETCH), D)
        edge_in = part_of_region(4, Q * P)
        edge_cols = part_of_region(2, Q * P)
        same_f = part_of_region(2, Q * P)
        taken[0] = 0
        relu_rows = part_of_region(4, T * D)
        x1_biased = part_of_region(4, T * D)
        mid_rows = part_of_region(2, T * D)
        h_rows = part_of_region(2, T * D)

        rows_in = sb("rows_in", [P, 4, T * D])
        rows_in2 = sb("rows_in2", [P, 4, T * D])
        stats = sb("stats", [P, 2, T, 6])
        moments = sb("moments", [P, 2, T, 2])
        var_eps = sb("var_eps", [P, 2, T])
        rstd = sb("rstd", [P, 2, T])
        shift = sb("shift", [P, 2, T])
        stats2 = sb("stats2", [P, 2, T, 6])
        moments2 = sb("moments2", [P, 2, T, 2])
        var_eps2 = sb("var_eps2", [P, 2, T])
        rstd2 = sb("rstd2", [P, 2, T])
        normed = sb("normed", [P, 2, T * D])
        cols = sb("cols", [D + 1, 2, T * P])
        cols2 = sb("cols2", [D + 1, 2, T * P])
        rows_out = sb("rows_out", [P, 2, T * D])
        msgs = sb("msgs", [P, 2, Q, D + 1])
        aggs = sb("aggs", [D + 1, 2, Q * P])
        gate = sb("gate", [P, 2, Q])
        gate1 = sb("gate1", [P, 2, Q])
        idx = sb("idx", [P, 4, Q], INT32)
        to_row = sb("to_row", [P, 2, Q], INT32)

        psum = ctx.enter_context(nc.psum_tensor("psum", [P, 8, 512], FP32))

        def two_banks(b, w):
            return psum[:, b:b + 2, :].rearrange("p b n -> p (b n)")[:, 0:w]

        def bank(b, w):
            return psum[:, b, 0:w]

        s_weights = sem("s_weights")
        s_edges = sem("s_edges")
        s_attr = sem("s_attr")
        s_wide = sem("s_wide")
        s_const = sem("s_const")
        s_const_step = sem("s_const_step")
        s_spare = sem("s_spare")
        s_order = sem("s_order")
        s_inversions = sem("s_inversions")
        s_flag = sem("s_flag")
        flag_f = sb("flag_f", [P, 1])
        flag_i = sb("flag_i", [1, 1], INT32)
        scr = [rows_in2[:, k, 0:EDGE_TILES] for k in range(3)]

        with nc.Block() as block:
            @block.sync
            def _(sp):
                sp.dma_start(src_i[:, :], src).then_inc(s_edges, 16)
                sp.dma_start(dst_i[:, :], dst[0]).then_inc(s_edges, 16)
                sp.dma_start(next_i[:, :], dst[1]).then_inc(s_edges, 16)
                flat = dst[2].rearrange("p e -> (p e)")
                sp.dma_start(region[:, :].bitcast(INT32),
                             flat.rearrange("(a n) -> a n", a=1).broadcast_to([P, EP])).then_inc(s_wide, 16)
                loads = [(wr1[0:D, :], Wr1t), (wr1[D:D + 1, :], bl1), (wl1[0:D, 0:D], Wl1t),
                         (wr2[0:D, :], Wr2t), (wr2[D:D + 1, :], bl2), (wl2[:, :], Wl2t),
                         (mw1[:, :], mW1), (gw1[:, :], gW1), (mb1c[:, :], mb1), (gb1c[:, :], gb1),
                         (mw2[0:D, :], mW2), (mw2[D:D + 1, :], mb2), (gw2[0:D, :], gW2), (gw2[D:D + 1, :], gb2),
                         (uw1n[:, :], uW1[0:D, :]), (uw1e[:, :], uW1[D:2 * D, :]), (ub1c[:, :], ub1),
                         (uw2[0:D, :], uW2), (uw2[D:D + 1, :], ub2),
                         (lng[:, :], ln_g.broadcast_to([P, D])), (lnb[:, :], ln_b.broadcast_to([P, D]))]
                sp.wait_ge(s_const, 1)
                for dest, source in loads:
                    sp.dma_start(dest, source).then_inc(s_weights, 16)
                sp.dma_start(attr_sorted.rearrange("(p a) n -> p (a n)", p=P),
                             edge_attr.rearrange("(p a) n -> p (a n)", p=P)).then_inc(s_attr, 16)
                for rows in (pre1, x1):
                    sp.dma_start(rows[N:ROWS, :].rearrange("(p a) n -> p (a n)", p=P),
                                 zeros[:, 0:SPARE * D]).then_inc(s_spare, 16)
                sp.wait_ge(s_weights, 16 * len(loads))
                sp.wait_ge(s_wide, 16)
                sp.wait_ge(s_attr, 16)
                sp.wait_ge(s_spare, 32)

            @block.gpsimd
            def _(pool):
                step = [0]

                def done(instruction):
                    step[0] += 1
                    instruction.then_inc(s_const_step, 1)
                    pool.wait_ge(s_const_step, step[0])

                done(pool.memset(wl1[:, :], 0.0))
                done(pool.memset(wl1[D:D + 1, D:D + 1], 1.0))
                done(pool.memset(zeros[:, :], 0.0))
                pool.memset(ones[:, :], 1.0).then_inc(s_const, 1)
                pool.wait_ge(s_const, 1)
                done(pool.memset(minus_half[:, :], -0.5))
                done(pool.memset(carry0[:, :], 0.0))
                done(pool.memset(cols[D:D + 1, :, :], 1.0))
                done(pool.memset(cols2[D:D + 1, :, :], 1.0))
                done(pool.memset(msgs[:, :, :, D:D + 1], 1.0))
                done(pool.affine_select(out=ident[:, :], in_=ones[:, :], compare_op=ALU.is_equal, fill=0.0, base=0,
                                        pattern=[[-1, P]], channel_multiplier=1))
                done(pool.affine_select(out=causal[:, :], in_=ones[:, :], compare_op=ALU.is_ge, fill=0.0, base=0,
                                        pattern=[[1, P]], channel_multiplier=-1))
                done(pool.iota(row_i[:, :].rearrange("p (a b) -> p a b", b=SPARE),
                               [[0, EDGE_TILES // SPARE], [P, SPARE]], base=N, channel_multiplier=1))

            @block.vector
            def _(dve):
                dve.wait_ge(s_edges, 48)
                nc.vector.tensor_tensor(scr[0][:, :], dst_i[:, :], next_i[:, :], ALU.is_gt).then_inc(s_order, 1)
                dve.wait_ge(s_order, 1)
                nc.vector.reduce_sum(flag_f[:, :], scr[0][:, :], AXX).then_inc(s_order, 1)
                dve.wait_ge(s_inversions, 1)
                nc.vector.tensor_copy(flag_i[:, :], psum[0:1, 0, 0:1]).then_inc(s_flag, 1)

            @block.tensor
            def _(pe):
                pe.wait_ge(s_order, 2)
                pe.wait_ge(s_const, 1)
                nc.tensor.matmul(psum[0:1, 0, 0:1], flag_f[:, :], ones[:, 0:1], start=True,
                                 stop=True).then_inc(s_inversions, 1)

        place_f = sb("place_f", [P, 1])
        place_i = sb("place_i", [P, 1], INT32)
        counts = sb("counts", [P, RANK_CHUNKS])
        limits = sb("limits", [P, RANK_CHUNKS])
        chunk_tiles = 4 * RANK_CHUNK // P
        frac_i = follows[:, 0:chunk_tiles, :].rearrange("p e i -> p (e i)").bitcast(INT32)
        frac = follows[:, chunk_tiles:2 * chunk_tiles, :].rearrange("p e i -> p (e i)").bitcast(FP32)
        diff = same[:, 0:chunk_tiles, :].rearrange("p e i -> p (e i)").bitcast(FP32)
        attr_tile = sb("attr_tile", [P, ED])
        own_i = sb("own_i", [P, 2], INT32)
        index_i = rows_in[:, 0, 0:EDGE_TILES].bitcast(INT32)
        r_iota = sem("r_iota")
        r_prep = sem("r_prep")
        r_step = sem("r_step")
        r_place = sem("r_place")
        r_attr = sem("r_attr")
        r_moved = sem("r_moved")
        r_done = sem("r_done")
        r_sorted = sem("r_sorted")
        index_f = scr[1]
        limit_base = scr[2]

        with nc.Block() as block:
            @block.gpsimd
            def _(pool):
                unsorted = pool.value_load(flag_i[0:1, 0:1], min_val=0, max_val=EP)
                with pool.If(unsorted > 0):
                    pool.iota(frac_i, [[1, RANK_CHUNK]], base=0, channel_multiplier=0).then_inc(r_iota, 1)
                    pool.iota(index_i[:, :], [[P, EDGE_TILES]], base=0, channel_multiplier=1).then_inc(r_iota, 1)
                    pool.wait_ge(r_iota, 2)
                    pool.sem_inc(r_done, 1)
                    with pool.Fori(0, EDGE_TILES) as e:
                        pool.dma_start(attr_tile[:, :], edge_attr.rearrange("(e p) n -> e p n", p=P)[e])\
                            .then_inc(r_attr, 16)
                        pool.wait_ge(r_attr, 16 * e + 16)
                        wait_apart(pool, r_place, e + 1)
                        at = bass.IndirectOffsetOnAxis(ap=place_i[:, 0:1], axis=0)
                        pool.indirect_dma_start(src_sorted, at, own_i[:, 0:1], None).then_inc(r_moved, 16)
                        pool.indirect_dma_start(dst_sorted, at, own_i[:, 1:2], None).then_inc(r_moved, 16)
                        pool.indirect_dma_start(attr_sorted, at, attr_tile[:, :], None).then_inc(r_moved, 16)
                        pool.wait_ge(r_moved, 48 * e + 48)
                        pool.sem_inc(r_done, 1)
                    with pool.Fori(0, EDGE_TILES) as e:
                        with nc.allow_non_contiguous_dma(reason="one index per partition"):
                            by_tile = [a.rearrange("(e p) n -> e p n", p=P) for a in (src_sorted, dst_sorted)]
                            pool.dma_start(src_i[:, bass.ds(e, 1)], by_tile[0][e]).then_inc(r_sorted, 16)
                            pool.dma_start(dst_i[:, bass.ds(e, 1)], by_tile[1][e]).then_inc(r_sorted, 16)
                        pool.wait_ge(r_sorted, 32 * e + 32)
                    with pool.Fori(0, EDGE_TILES - 1) as e:
                        after = dst_sorted[1:EP - P + 1, :].rearrange("(e p) n -> e p n", p=P)
                        pool.dma_start(next_i[:, bass.ds(e, 1)], after[e]).then_inc(r_sorted, 16)
                        pool.wait_ge(r_sorted, 16 * e + 32 * EDGE_TILES + 16)
                    pool.dma_start(next_i[0:P - 1, EDGE_TILES - 1:EDGE_TILES], dst_sorted[EP - P + 1:EP, :])\
                        .then_inc(r_sorted, 16)
                    pool.wait_ge(r_sorted, 16 * (3 * EDGE_TILES))
                    pool.dma_start(dst_wide.rearrange("p e i -> p (e i)"),
                                   dst_sorted.rearrange("a n -> n a").broadcast_to([P, EP])).then_inc(r_sorted, 16)
                    pool.wait_ge(r_sorted, 16 * (3 * EDGE_TILES + 1))
                with pool.Else():
                    pool.sem_inc(r_iota, 1)

            @block.vector
            def _(dve):
                unsorted = dve.value_load(flag_i[0:1, 0:1], min_val=0, max_val=EP)
                with dve.If(unsorted > 0):
                    dve.wait_ge(r_iota, 2)
                    nc.vector.tensor_scalar(frac, frac_i, INDEX_STEP, None, ALU.mult).then_inc(r_prep, 1)
                    nc.vector.tensor_scalar(index_f[:, :], index_i[:, :], INDEX_STEP, None, ALU.mult)\
                        .then_inc(r_prep, 1)
                    nc.vector.tensor_copy(dst_f[:, :], dst_i[:, :]).then_inc(r_prep, 1)
                    nc.vector.tensor_scalar(limit_base[:, 0:RANK_CHUNKS], index_i[:, 0:RANK_CHUNKS], 0.0, None,
                                            ALU.mult).then_inc(r_prep, 1)
                    dve.wait_ge(r_prep, 4)
                    for c in range(RANK_CHUNKS):
                        nc.vector.memset(limit_base[:, c:c + 1], -c * RANK_CHUNK * INDEX_STEP).then_inc(r_prep, 1)
                    dve.wait_ge(r_prep, 4 + RANK_CHUNKS)
                    per_tile = 2 * RANK_CHUNKS + 5
                    with dve.Fori(0, EDGE_TILES) as e:
                        step = [0]

                        def done(instruction):
                            step[0] += 1
                            instruction.then_inc(r_step, 1)
                            dve.wait_ge(r_step, e * per_tile + step[0])

                        done(nc.vector.tensor_scalar(limits[:, :], limit_base[:, 0:RANK_CHUNKS],
                                                     index_f[:, bass.ds(e, 1)], None, ALU.add))
                        for c in range(RANK_CHUNKS):
                            wide = dst_wide.rearrange("p e i -> p (e i)")[:, c * RANK_CHUNK:(c + 1) * RANK_CHUNK]
                            done(nc.vector.scalar_tensor_tensor(out=diff, in0=wide,
                                                                scalar=dst_f[:, bass.ds(e, 1)], in1=frac,
                                                                op0=ALU.subtract, op1=ALU.add))
                            done(nc.vector.tensor_scalar(diff, diff, limits[:, c:c + 1], 0.0,
                                                         ALU.is_lt, ALU.add, accum_out=counts[:, c:c + 1]))
                        done(nc.vector.reduce_sum(place_f[:, :], counts[:, :], AXX))
                        dve.wait_ge(r_done, e + 1)
                        done(nc.vector.tensor_copy(own_i[:, 0:1], src_i[:, bass.ds(e, 1)]))
                        done(nc.vector.tensor_copy(own_i[:, 1:2], dst_i[:, bass.ds(e, 1)]))
                        done(nc.vector.tensor_copy(place_i[:, :], place_f[:, :]))
                        nc.vector.memset(counts[:, :], 0.0).then_inc(r_place, 1)
                with dve.Else():
                    dve.sem_inc(r_prep, 1)

        m_step = sem("m_step")
        m_wide = sem("m_wide")
        m_follows = sem("m_follows")
        MASK_TILES = 8
        with nc.Block() as block:
            @block.vector
            def _(dve):
                step = [0]

                def done(instruction):
                    step[0] += 1
                    instruction.then_inc(m_step, 1)
                    dve.wait_ge(m_step, step[0])

                a, b, c = scr
                done(nc.vector.tensor_copy(dst_f[:, :], dst_i[:, :]))
                done(nc.vector.tensor_tensor(a[:, :], dst_i[:, :], next_i[:, :], ALU.not_equal))
                done(nc.vector.tensor_scalar(b[:, :], dst_f[:, :], float(N), None, ALU.is_lt))
                done(nc.vector.tensor_tensor(a[:, :], a[:, :], b[:, :], ALU.mult))
                done(nc.vector.tensor_copy(c[:, :], row_i[:, :]))
                done(nc.vector.tensor_tensor(b[:, :], dst_f[:, :], c[:, :], ALU.subtract))
                done(nc.vector.tensor_tensor(b[:, :], b[:, :], a[:, :], ALU.mult))
                done(nc.vector.tensor_tensor(row_i[:, :], b[:, :], c[:, :], ALU.add))
                with dve.Fori(0, EDGE_TILES // MASK_TILES) as i:
                    for k in range(MASK_TILES):
                        e = i * MASK_TILES + k
                        nc.vector.scalar_tensor_tensor(
                            out=same[:, bass.ds(e, 1), :].rearrange("p a i -> p (a i)"),
                            in0=dst_wide[:, bass.ds(e, 1), :].rearrange("p a i -> p (a i)"),
                            scalar=dst_f[:, bass.ds(e, 1)], in1=causal[:, :],
                            op0=ALU.is_equal, op1=ALU.mult).then_inc(m_wide, 1)
                nc.vector.memset(follows[:, 0:1, :], 0.0)
                nc.vector.tensor_tensor(follows[:, 1:EDGE_TILES, :], dst_wide[:, 1:EDGE_TILES, :],
                                        dst_wide[:, 0:EDGE_TILES - 1, P - 1:P]
                                        .broadcast_to([P, EDGE_TILES - 1, P]), ALU.is_equal).then_inc(m_follows, 1)
                dve.wait_ge(m_wide, EDGE_TILES)
                dve.wait_ge(m_follows, 1)

        def by_group(rows):
            return rows[0:NODE_GROUPS * GROUP_ROWS, :].rearrange("(g p t) d -> g p (t d)", p=P, t=T)

        def tail(rows):
            return rows[NODE_GROUPS * GROUP_ROWS:N, :]

        END = Group(NODE_GROUPS // UNROLL, NODE_GROUPS % UNROLL)

        def shape(g):
            return (TAIL, 1) if g is END else (P, T)

        def rows_of(dram_rows, g):
            return tail(dram_rows) if g is END else by_group(dram_rows)[g.n]

        def by_row(buffer_rows, p, t):
            return buffer_rows[0:p, 0:t * D].rearrange("p (t d) -> p t d", t=t)

        def node_pass(name, source, addend, norm, weight, dest, edge_source):
            G = NODE_GROUPS
            loaded = [sem(f"{name}_loaded{s}") for s in range(4)]
            addend_in = [sem(f"{name}_addend{s}") for s in range(4)]
            stats_done = sem(f"{name}_stats")
            moments_done = sem(f"{name}_moments")
            var_done = sem(f"{name}_var")
            rstd_done = sem(f"{name}_rstd")
            normed_done = sem(f"{name}_normed")
            turned = sem(f"{name}_turned")
            cols_done = sem(f"{name}_cols")
            product = sem(f"{name}_product")
            result = sem(f"{name}_result")
            stored = [sem(f"{name}_stored{s}") for s in range(2)]
            indices = [sem(f"{name}_indices{s}") for s in range(UNROLL)]
            fetch_in = [sem(f"{name}_fetch{s}") for s in range(UNROLL)]
            kept = [sem(f"{name}_kept{s}") for s in range(UNROLL)]

            with nc.Block() as block:
                @block.sync
                def _(sp):
                    def load(g):
                        p, t = shape(g)
                        s = g.slot(4)
                        if g.reuses(4):
                            sp.wait_ge(normed_done if norm else turned, g.n - 3)
                        sp.dma_start(rows_in[0:p, s, 0:t * D], rows_of(source, g)).then_inc(loaded[s], 16)
                        if addend is not None:
                            if g.reuses(4):
                                sp.wait_ge(result, g.n - 3)
                            sp.dma_start(rows_in2[0:p, s, 0:t * D], rows_of(addend, g)).then_inc(addend_in[s], 16)

                    pipelined(sp, G, (0, load))
                    load(END)

                @block.gpsimd
                def _(pool):
                    def root(g):
                        p, t = shape(g)
                        s = g.slot(2)
                        wait_apart(pool, moments_done, g.n + 1)
                        if g.reuses(2):
                            wait_apart(pool, normed_done, g.n - 1)
                        pool.tensor_scalar(var_eps[0:p, s, 0:t], moments[0:p, s, 0:t, 1], LN_EPS,
                                           None, ALU.add).then_inc(var_done, 1)
                        pool.wait_ge(var_done, g.n + 1)
                        pool.tensor_tensor(rstd[0:p, s, 0:t], var_eps[0:p, s, 0:t], minus_half[0:p, 0:t],
                                           ALU.pow).then_inc(rstd_done, 1)

                    def fetch(g):
                        c, n = g.c, FETCH[g.c]
                        if g.reuses(UNROLL):
                            wait_apart(pool, kept[c], g.i)
                        first = g.i * sum(FETCH) + FETCH_AT[c]
                        pool.tensor_copy(idx[:, c, 0:n], src_i[:, bass.ds(first, n)]).then_inc(indices[c], 1)
                        wait_apart(pool, indices[c], g.i + 1)
                        for k in range(n):
                            at = bass.IndirectOffsetOnAxis(ap=idx[:, c, k:k + 1], axis=0)
                            pool.indirect_dma_start(fetched[:, FETCH_AT[c] + k, :], None, edge_source, at)\
                                .then_inc(fetch_in[c], 16)

                    if norm:
                        pipelined(pool, G, (0, root), (0, fetch))
                        root(END)
                    else:
                        pipelined(pool, G, (0, fetch))
                    for n in range(G, FETCHES * UNROLL):
                        fetch(Group(n // UNROLL, n % UNROLL))

                @block.vector
                def _(dve):
                    def measure(g):
                        p, t = shape(g)
                        s, s4 = g.slot(2), g.slot(4)
                        dve.wait_ge(loaded[s4], 16 * (g.use(4) + 1))
                        if g.reuses(2):
                            dve.wait_ge(rstd_done, g.n - 1)
                        for k in range(t):
                            last = nc.vector.bn_stats(stats[0:p, s, k, :], rows_in[0:p, s4, k * D:(k + 1) * D])
                        last.then_inc(stats_done, 1)
                        wait_apart(dve, stats_done, g.n + 1)
                        for k in range(t):
                            last = nc.vector.bn_aggr(moments[0:p, s, k, :], stats[0:p, s, k, :])
                        last.then_inc(moments_done, 1)

                    def normalize(g):
                        p, t = shape(g)
                        s, s4 = g.slot(2), g.slot(4)
                        dve.wait_ge(rstd_done, g.n + 1)
                        if g.reuses(2):
                            dve.wait_ge(turned, g.n - 1)
                        for k in range(t):
                            last = nc.vector.tensor_scalar(normed[0:p, s, k * D:(k + 1) * D],
                                                           rows_in[0:p, s4, k * D:(k + 1) * D],
                                                           moments[0:p, s, k, 0:1], rstd[0:p, s, k:k + 1],
                                                           ALU.subtract, ALU.mult)
                        last.then_inc(normed_done, 1)

                    def add(g):
                        p, t = shape(g)
                        s, s4 = g.slot(2), g.slot(4)
                        dve.wait_ge(product, g.n + 1)
                        dve.wait_ge(addend_in[s4], 16 * (g.use(4) + 1))
                        if g.reuses(2):
                            dve.wait_ge(stored[s], 16 * g.use(2))
                        nc.vector.tensor_tensor(rows_out[0:p, s, 0:t * D], bank(4 + s, t * D)[0:p, :],
                                                rows_in2[0:p, s4, 0:t * D], ALU.add).then_inc(result, 1)

                    if norm:
                        pipelined(dve, G, (0, measure), (1, normalize))
                        measure(END)
                        normalize(END)
                    if addend is not None:
                        pipelined(dve, G, (0, add))
                        add(END)

                @block.tensor
                def _(pe):
                    def turn(g):
                        p, t = shape(g)
                        s = g.slot(2)
                        if norm:
                            rows = normed[:, s, :]
                            pe.wait_ge(normed_done, g.n + 1)
                        else:
                            rows = rows_in[:, g.slot(4), :]
                            pe.wait_ge(loaded[g.slot(4)], 16 * (g.use(4) + 1))
                        if g.reuses(2):
                            pe.wait_ge(cols_done, g.n - 1)
                        for k in range(t):
                            last = nc.tensor.transpose(two_banks(2 * s, T * P)[0:D, k * P:k * P + p],
                                                       rows[0:p, k * D:(k + 1) * D], ident[0:p, 0:p])
                        last.then_inc(turned, 1)

                    def multiply(g):
                        p, t = shape(g)
                        s = g.slot(2)
                        pe.wait_ge(cols_done, g.n + 1)
                        if g.reuses(2):
                            pe.wait_ge(result, g.n - 1)
                        for k in range(t):
                            last = nc.tensor.matmul(bank(4 + s, T * D)[0:p, k * D:(k + 1) * D],
                                                    cols[:, s, k * P:k * P + p], weight[:, :],
                                                    start=True, stop=True)
                        last.then_inc(product, 1)

                    pipelined(pe, G, (0, turn), (1, multiply))
                    turn(END)
                    multiply(END)

                @block.scalar
                def _(act):
                    def rectify(g):
                        p, t = shape(g)
                        s = g.slot(2)
                        act.wait_ge(turned, g.n + 1)
                        if g.reuses(2):
                            act.wait_ge(product, g.n - 1)
                        w = (t - 1) * P + p
                        nc.scalar.activation(cols[0:D, s, 0:w], two_banks(2 * s, w)[0:D, :],
                                             ACT.Relu).then_inc(cols_done, 1)

                    def copy_out(g):
                        p, t = shape(g)
                        s = g.slot(2)
                        if addend is None:
                            act.wait_ge(product, g.n + 1)
                            if g.reuses(2):
                                act.wait_ge(stored[s], 16 * g.use(2))
                            nc.scalar.activation(rows_out[0:p, s, 0:t * D], bank(4 + s, t * D)[0:p, :],
                                                 ACT.Copy).then_inc(result, 1)
                        act.wait_ge(result, g.n + 1)
                        act.dma_start(rows_of(dest, g), rows_out[0:p, s, 0:t * D]).then_inc(stored[s], 16)

                    def keep(g):
                        c, n = g.c, FETCH[g.c]
                        act.wait_ge(fetch_in[c], 16 * n * (g.i + 1))
                        first = g.i * sum(FETCH) + FETCH_AT[c]
                        nc.scalar.activation(edge_rows[:, bass.ds(first, n), :],
                                             fetched[:, FETCH_AT[c]:FETCH_AT[c] + n, :], ACT.Copy)\
                            .then_inc(kept[c], 1)

                    pipelined(act, G, (0, rectify), (1, copy_out), (2, keep))
                    rectify(END)
                    copy_out(END)
                    for n in range(G, FETCHES * UNROLL):
                        keep(Group(n // UNROLL, n % UNROLL))
                    act.wait_ge(stored[0], 16 * -(-(G + 1) // 2))
                    act.wait_ge(stored[1], 16 * ((G + 1) // 2))

        def edge_pass(name, source, kind, weight, dest):
            mlp = kind == "mlp"
            norm = kind != "relu"
            counted = kind == "norm"
            W = D + 1 if counted else D
            G = EDGE_GROUPS
            indices = sem(f"{name}_indices")
            gathered = [sem(f"{name}_gathered{s}") for s in range(4)]
            attr_in = [sem(f"{name}_attr{s}") for s in range(4)]
            stats_done = sem(f"{name}_stats")
            moments_done = sem(f"{name}_moments")
            var_done = sem(f"{name}_var")
            rstd_done = sem(f"{name}_rstd")
            normed_done = sem(f"{name}_normed")
            turned = sem(f"{name}_turned")
            cols_done = sem(f"{name}_cols")
            attr_cols = sem(f"{name}_attr_cols")
            hidden = sem(f"{name}_hidden")
            gelu_done = sem(f"{name}_gelu")
            message_done = sem(f"{name}_message")
            tanh_done = sem(f"{name}_tanh")
            gate_done = sem(f"{name}_gate")
            msgs_done = sem(f"{name}_msgs")
            widened = sem(f"{name}_widened")
            summed = sem(f"{name}_summed")
            carried = sem(f"{name}_carried")
            product = sem(f"{name}_product")
            deg_step = sem(f"{name}_deg")
            result = sem(f"{name}_result")
            targets = sem(f"{name}_targets")
            scattered = [sem(f"{name}_scattered{s}") for s in range(2)]
            zeroed = sem(f"{name}_zeroed")
            TURN, HID, MSG, AGG, OUT = 0, 1, 3, 4, 6

            def tile_of(buffer, g, k):
                return buffer[:, bass.ds(g.n * Q + k, 1), :].rearrange("p a i -> p (a i)")

            def row(g, k):
                if mlp:
                    return edge_in[:, g.slot(4), k * P:k * P + D]
                return tile_of(edge_rows, g, k)

            def by_tile(columns):
                return columns.rearrange("p (q n) -> p q n", q=Q)

            with nc.Block() as block:
                @block.sync
                def _(sp):
                    if counted:
                        flat = aggu[0:N, :].rearrange("a n -> (a n)").rearrange("(p m) -> p m", p=P)
                        for c in range(ZERO_CHUNKS):
                            sp.dma_start(flat[:, c * ZERO_COLS:(c + 1) * ZERO_COLS], zeros[:, :])\
                                .then_inc(zeroed, 16)
                        sp.wait_ge(zeroed, 16 * ZERO_CHUNKS)
                    if mlp:
                        def load_attr(g):
                            s = g.slot(4)
                            if g.reuses(4):
                                sp.wait_ge(turned, g.n - 3)
                            at = attr_sorted.rearrange("(g q p) n -> g p q n", q=Q, p=P)[g.n]
                            sp.dma_start(by_tile(edge_in[:, s, :])[:, :, D:P], at).then_inc(attr_in[s], 16)

                        pipelined(sp, G, (0, load_attr))

                @block.gpsimd
                def _(pool):
                    def gather(g):
                        s = g.slot(4)
                        if g.reuses(4):
                            wait_apart(pool, turned, g.n - 3)
                        pool.tensor_copy(idx[:, s, :], src_i[:, bass.ds(g.n * Q, Q)]).then_inc(indices, 1)
                        wait_apart(pool, indices, g.n + 1)
                        for k in range(Q):
                            at = bass.IndirectOffsetOnAxis(ap=idx[:, s, k:k + 1], axis=0)
                            pool.indirect_dma_start(row(g, k), None, source, at).then_inc(gathered[s], 16)

                    def root(g):
                        s = g.slot(2)
                        wait_apart(pool, moments_done, g.n + 1)
                        if g.reuses(2):
                            wait_apart(pool, normed_done, g.n - 1)
                        pool.tensor_scalar(var_eps[:, s, 0:Q], moments[:, s, 0:Q, 1], LN_EPS, None,
                                           ALU.add).then_inc(var_done, 1)
                        pool.wait_ge(var_done, g.n + 1)
                        pool.tensor_tensor(rstd[:, s, 0:Q], var_eps[:, s, 0:Q], minus_half[:, 0:Q],
                                           ALU.pow).then_inc(rstd_done, 1)

                    def scatter(g):
                        s = g.slot(2)
                        if g.reuses(2):
                            pool.wait_ge(scattered[s], 16 * Q * g.use(2))
                        pool.tensor_copy(to_row[:, s, :], row_i[:, bass.ds(g.n * Q, Q)]).then_inc(targets, 1)
                        wait_apart(pool, targets, g.n + 1)
                        wait_apart(pool, result, g.n + 1)
                        for k in range(Q):
                            at = bass.IndirectOffsetOnAxis(ap=to_row[:, s, k:k + 1], axis=0)
                            pool.indirect_dma_start(dest, at, rows_out[:, s, k * D:(k + 1) * D], None,
                                                    compute_op=ALU.bypass if mlp else ALU.add)\
                                .then_inc(scattered[s], 16)

                    if mlp:
                        pipelined(pool, G, (0, gather), (1, root), (3, scatter))
                    elif norm:
                        pipelined(pool, G, (0, root), (2, scatter))
                    else:
                        pipelined(pool, G, (0, scatter))
                    for s in range(2):
                        pool.wait_ge(scattered[s], 16 * Q * (G // 2))

                @block.vector
                def _(dve):
                    def measure(g):
                        s = g.slot(2)
                        if mlp:
                            dve.wait_ge(gathered[g.slot(4)], 16 * Q * (g.use(4) + 1))
                        if g.reuses(2):
                            dve.wait_ge(rstd_done, g.n - 1)
                        for k in range(Q):
                            last = nc.vector.bn_stats(stats[:, s, k, :], row(g, k))
                        last.then_inc(stats_done, 1)
                        wait_apart(dve, stats_done, g.n + 1)
                        for k in range(Q):
                            last = nc.vector.bn_aggr(moments[:, s, k, :], stats[:, s, k, :])
                        last.then_inc(moments_done, 1)

                    def normalize(g):
                        s = g.slot(2)
                        dve.wait_ge(rstd_done, g.n + 1)
                        if g.reuses(2) and not mlp:
                            dve.wait_ge(msgs_done, g.n - 1)
                        for k in range(Q):
                            to = row(g, k) if mlp else normed[:, s, k * D:(k + 1) * D]
                            last = nc.vector.tensor_scalar(to, row(g, k), moments[:, s, k, 0:1],
                                                           rstd[:, s, k:k + 1], ALU.subtract, ALU.mult)
                        last.then_inc(normed_done, 1)

                    def copy_attr(g):
                        dve.wait_ge(turned, g.n + 1)
                        if g.reuses(2):
                            dve.wait_ge(hidden, g.n - 1)
                        nc.vector.tensor_copy(edge_cols[D:P, g.slot(2), :], bank(TURN, 512)[D:P, :])\
                            .then_inc(attr_cols, 1)

                    def gate_messages(g):
                        s = g.slot(2)
                        dve.wait_ge(tanh_done, g.n + 1)
                        nc.vector.tensor_scalar(gate1[:, s, :], gate[:, s, :], 0.5, 0.5, ALU.mult,
                                                ALU.add).then_inc(gate_done, 1)
                        dve.wait_ge(gate_done, g.n + 1)
                        if g.reuses(2):
                            dve.wait_ge(summed, g.n - 1)
                        m = by_tile(bank(MSG, Q * (D + 1)))[:, :, 0:D]
                        nc.vector.tensor_tensor(msgs[:, s, :, 0:D], m,
                                                gate1[:, s, :].rearrange("p (q a) -> p q a", a=1)
                                                .broadcast_to([P, Q, D]), ALU.mult).then_inc(msgs_done, 1)

                    def carry(g):
                        s = g.slot(2)
                        dve.wait_ge(summed, g.n + 1)
                        if g.reuses(2):
                            dve.wait_ge(product, g.n - 1)
                        for k in range(Q):
                            if k:
                                before = aggs[0:W, s, k * P - 1:k * P]
                            elif isinstance(g.n, int) and g.n == 0:
                                before = carry0[0:W, :]
                            else:
                                before = aggs[0:W, 1 - s, Q * P - 1:Q * P]
                            nc.vector.scalar_tensor_tensor(out=aggs[0:W, s, k * P:(k + 1) * P],
                                                           in0=tile_of(follows, g, k)[0:W, :], scalar=before,
                                                           in1=bank(AGG + s, 512)[0:W, k * P:(k + 1) * P],
                                                           op0=ALU.mult, op1=ALU.add).then_inc(carried, 1)
                            dve.wait_ge(carried, g.n * Q + (k + 1))

                    def finish(g):
                        s = g.slot(2)
                        dve.wait_ge(product, g.n + 1)
                        v = by_tile(bank(OUT + s, Q * W))
                        o = by_tile(rows_out[:, s, 0:Q * D])
                        inv = inv_deg[:, bass.ds(g.n * Q, Q)]
                        if counted:
                            nc.vector.tensor_scalar(gate[:, s, :], v[:, :, D], 1.0, None, ALU.max)\
                                .then_inc(deg_step, 1)
                            dve.wait_ge(deg_step, 2 * g.n + 1)
                            nc.vector.reciprocal(inv, gate[:, s, :]).then_inc(deg_step, 1)
                            dve.wait_ge(deg_step, 2 * g.n + 2)
                        if g.reuses(2):
                            dve.wait_ge(scattered[s], 16 * Q * g.use(2))
                        if mlp:
                            nc.vector.tensor_copy(o, v[:, :, 0:D]).then_inc(result, 1)
                        else:
                            nc.vector.tensor_tensor(o, v[:, :, 0:D], inv.rearrange("p (q a) -> p q a", a=1)
                                                    .broadcast_to([P, Q, D]), ALU.mult).then_inc(result, 1)

                    if mlp:
                        pipelined(dve, G, (1, measure), (2, copy_attr), (3, carry), (1, normalize), (3, finish),
                                  (2, gate_messages))
                    elif norm:
                        pipelined(dve, G, (0, measure), (2, carry), (1, normalize), (2, finish))
                    else:
                        pipelined(dve, G, (0, carry), (0, finish))

                @block.scalar
                def _(act):
                    def widen(g):
                        if g.reuses(2):
                            act.wait_ge(summed, g.n - 1)
                        nc.scalar.activation(same_f[:, g.slot(2), :],
                                             same[:, bass.ds(g.n * Q, Q), :].rearrange("p e i -> p (e i)"),
                                             ACT.Copy).then_inc(widened, 1)

                    def rectify(g):
                        s = g.slot(2)
                        if norm:
                            act.wait_ge(normed_done, g.n + 1)
                            rows = by_tile(normed[:, s, 0:Q * D])
                        else:
                            rows = edge_rows[:, bass.ds(g.n * Q, Q), :]
                        if g.reuses(2):
                            act.wait_ge(summed, g.n - 1)
                        nc.scalar.activation(msgs[:, s, :, 0:D], rows, ACT.Relu).then_inc(msgs_done, 1)

                    def rectify_cols(g):
                        act.wait_ge(turned, g.n + 1)
                        if g.reuses(2):
                            act.wait_ge(hidden, g.n - 1)
                        nc.scalar.activation(edge_cols[0:D, g.slot(2), :], bank(TURN, 512)[0:D, :], ACT.Relu)\
                            .then_inc(cols_done, 1)

                    def gelus(g):
                        s = g.slot(2)
                        act.wait_ge(hidden, g.n + 1)
                        if g.reuses(2):
                            act.wait_ge(message_done, g.n - 1)
                        nc.scalar.activation(cols[0:D, s, 0:Q * P], bank(HID, 512)[0:D, :], ACT.Gelu,
                                             bias=mb1c[:, :])
                        nc.scalar.activation(cols2[0:D, s, 0:Q * P], bank(HID + 1, 512)[0:D, :], ACT.Gelu,
                                             bias=gb1c[:, :]).then_inc(gelu_done, 1)

                    def tanh(g):
                        s = g.slot(2)
                        act.wait_ge(message_done, g.n + 1)
                        if g.reuses(2):
                            act.wait_ge(gate_done, g.n - 1)
                        z = by_tile(bank(MSG, Q * (D + 1)))[:, :, D]
                        nc.scalar.activation(gate[:, s, :], z, ACT.Tanh, scale=0.5).then_inc(tanh_done, 1)

                    if mlp:
                        pipelined(act, G, (2, rectify_cols), (2, widen), (2, gelus), (2, tanh))
                    else:
                        pipelined(act, G, (0, widen), (1 if norm else 0, rectify))

                @block.tensor
                def _(pe):
                    def turn(g):
                        s = g.slot(4)
                        pe.wait_ge(normed_done, g.n + 1)
                        pe.wait_ge(attr_in[s], 16 * (g.use(4) + 1))
                        if g.reuses(1):
                            pe.wait_ge(cols_done, g.n)
                            pe.wait_ge(attr_cols, g.n)
                        for k in range(Q):
                            last = nc.tensor.transpose(bank(TURN, 512)[:, k * P:(k + 1) * P],
                                                       edge_in[:, s, k * P:(k + 1) * P], ident[:, :])
                        last.then_inc(turned, 1)

                    def hide(g):
                        s = g.slot(2)
                        pe.wait_ge(cols_done, g.n + 1)
                        pe.wait_ge(attr_cols, g.n + 1)
                        if g.reuses(1):
                            pe.wait_ge(gelu_done, g.n)
                        nc.tensor.matmul(bank(HID, 512)[0:D, :], mw1[:, :], edge_cols[:, s, :], start=True,
                                         stop=True)
                        nc.tensor.matmul(bank(HID + 1, 512)[0:D, :], gw1[:, :], edge_cols[:, s, :], start=True,
                                         stop=True).then_inc(hidden, 1)

                    def message(g):
                        s = g.slot(2)
                        pe.wait_ge(gelu_done, g.n + 1)
                        if g.reuses(1):
                            pe.wait_ge(msgs_done, g.n)
                            pe.wait_ge(tanh_done, g.n)
                        for k in range(Q):
                            at = k * (D + 1)
                            nc.tensor.matmul(bank(MSG, 512)[:, at:at + D], cols[:, s, k * P:(k + 1) * P],
                                             mw2[:, :], start=True, stop=True)
                            last = nc.tensor.matmul(bank(MSG, 512)[:, at + D:at + D + 1],
                                                    cols2[:, s, k * P:(k + 1) * P], gw2[:, :], start=True,
                                                    stop=True)
                        last.then_inc(message_done, 1)

                    def aggregate(g):
                        s = g.slot(2)
                        pe.wait_ge(msgs_done, g.n + 1)
                        pe.wait_ge(widened, g.n + 1)
                        if g.reuses(2):
                            pe.wait_ge(carried, (g.n - 1) * Q)
                        for k in range(Q):
                            last = nc.tensor.matmul(bank(AGG + s, 512)[0:W, k * P:(k + 1) * P],
                                                    msgs[:, s, k, 0:W], same_f[:, s, k * P:(k + 1) * P],
                                                    start=True, stop=True)
                        last.then_inc(summed, 1)

                    def multiply(g):
                        s = g.slot(2)
                        pe.wait_ge(carried, g.n * Q + Q)
                        if g.reuses(2):
                            pe.wait_ge(result, g.n - 1)
                        for k in range(Q):
                            last = nc.tensor.matmul(bank(OUT + s, 512)[:, k * W:(k + 1) * W],
                                                    aggs[0:W, s, k * P:(k + 1) * P], weight[:, :], start=True,
                                                    stop=True)
                        last.then_inc(product, 1)

                    if mlp:
                        pipelined(pe, G, (2, turn), (3, aggregate), (2, hide), (3, multiply), (2, message))
                    elif norm:
                        pipelined(pe, G, (2, multiply), (1, aggregate))
                    else:
                        pipelined(pe, G, (0, aggregate), (1, multiply))

        def update_pass():
            G = NODE_GROUPS
            loaded = [sem(f"u_loaded{s}") for s in range(4)]
            agg_in = [sem(f"u_agg{s}") for s in range(4)]
            stats_done = sem("u_stats")
            moments_done = sem("u_moments")
            var_done = sem("u_var")
            rstd_done = sem("u_rstd")
            shift_done = sem("u_shift")
            relu_done = sem("u_relu")
            turned = sem("u_turned")
            cols_done = sem("u_cols")
            product = sem("u_product")
            summed = sem("u_summed")
            turned2 = sem("u_turned2")
            gelu_done = sem("u_gelu")
            product2 = sem("u_product2")
            h_done = sem("u_h")
            stats2_done = sem("u_stats2")
            moments2_done = sem("u_moments2")
            var2_done = sem("u_var2")
            rstd2_done = sem("u_rstd2")
            scaled = sem("u_scaled")
            biased = sem("u_biased")
            result = sem("u_result")
            stored = [sem(f"u_stored{s}") for s in range(2)]

            with nc.Block() as block:
                @block.sync
                def _(sp):
                    def load(g):
                        p, t = shape(g)
                        s = g.slot(4)
                        if g.reuses(4):
                            sp.wait_ge(biased, g.n - 3)
                            sp.wait_ge(relu_done, g.n - 3)
                        sp.dma_start(rows_in[0:p, s, 0:t * D], rows_of(x1, g)).then_inc(loaded[s], 16)
                        if g.reuses(4):
                            sp.wait_ge(summed, g.n - 3)
                        sp.dma_start(rows_in2[0:p, s, 0:t * D], rows_of(aggu, g)).then_inc(agg_in[s], 16)

                    pipelined(sp, G, (0, load))
                    load(END)

                @block.gpsimd
                def _(pool):
                    def root(g):
                        p, t = shape(g)
                        s = g.slot(2)
                        wait_apart(pool, moments_done, g.n + 1)
                        if g.reuses(2):
                            wait_apart(pool, relu_done, g.n - 1)
                        pool.tensor_scalar(var_eps[0:p, s, 0:t], moments[0:p, s, 0:t, 1], LN_EPS, None,
                                           ALU.add).then_inc(var_done, 1)
                        pool.wait_ge(var_done, g.n + 1)
                        pool.tensor_tensor(rstd[0:p, s, 0:t], var_eps[0:p, s, 0:t], minus_half[0:p, 0:t],
                                           ALU.pow).then_inc(rstd_done, 1)

                    def bias(g):
                        p, t = shape(g)
                        s = g.slot(4)
                        pool.wait_ge(loaded[s], 16 * (g.use(4) + 1))
                        if g.reuses(4):
                            pool.wait_ge(result, g.n - 3)
                        b = lnb[0:p, :].rearrange("p (a d) -> p a d", a=1).broadcast_to([p, t, D])
                        pool.tensor_tensor(by_row(x1_biased[:, s, :], p, t), by_row(rows_in[:, s, :], p, t), b,
                                           ALU.add).then_inc(biased, 1)

                    def root2(g):
                        p, t = shape(g)
                        s = g.slot(2)
                        wait_apart(pool, moments2_done, g.n + 1)
                        if g.reuses(2):
                            wait_apart(pool, result, g.n - 1)
                        pool.tensor_scalar(var_eps2[0:p, s, 0:t], moments2[0:p, s, 0:t, 1], LN_EPS, None,
                                           ALU.add).then_inc(var2_done, 1)
                        pool.wait_ge(var2_done, g.n + 1)
                        pool.tensor_tensor(rstd2[0:p, s, 0:t], var_eps2[0:p, s, 0:t], minus_half[0:p, 0:t],
                                           ALU.pow).then_inc(rstd2_done, 1)

                    pipelined(pool, G, (3, root2), (0, root), (0, bias))
                    for part in (root, bias, root2):
                        part(END)

                @block.vector
                def _(dve):
                    def measure(g):
                        p, t = shape(g)
                        s, s4 = g.slot(2), g.slot(4)
                        dve.wait_ge(loaded[s4], 16 * (g.use(4) + 1))
                        if g.reuses(2):
                            dve.wait_ge(rstd_done, g.n - 1)
                        for k in range(t):
                            last = nc.vector.bn_stats(stats[0:p, s, k, :], rows_in[0:p, s4, k * D:(k + 1) * D])
                        last.then_inc(stats_done, 1)
                        wait_apart(dve, stats_done, g.n + 1)
                        for k in range(t):
                            last = nc.vector.bn_aggr(moments[0:p, s, k, :], stats[0:p, s, k, :])
                        last.then_inc(moments_done, 1)

                    def shift_by(g):
                        p, t = shape(g)
                        s = g.slot(2)
                        dve.wait_ge(rstd_done, g.n + 1)
                        if g.reuses(2):
                            dve.wait_ge(relu_done, g.n - 1)
                        nc.vector.scalar_tensor_tensor(out=shift[0:p, s, 0:t], in0=moments[0:p, s, 0:t, 0],
                                                       scalar=-1.0, in1=rstd[0:p, s, 0:t], op0=ALU.mult,
                                                       op1=ALU.mult).then_inc(shift_done, 1)

                    def add_agg(g):
                        p, t = shape(g)
                        s, s4 = g.slot(2), g.slot(4)
                        dve.wait_ge(product, g.n + 1)
                        dve.wait_ge(agg_in[s4], 16 * (g.use(4) + 1))
                        if g.reuses(2):
                            dve.wait_ge(turned2, g.n - 1)
                        nc.vector.tensor_tensor(mid_rows[0:p, s, 0:t * D], bank(4 + s, t * D)[0:p, :],
                                                rows_in2[0:p, s4, 0:t * D], ALU.add).then_inc(summed, 1)

                    def residual(g):
                        p, t = shape(g)
                        s, s4 = g.slot(2), g.slot(4)
                        dve.wait_ge(product2, g.n + 1)
                        if g.reuses(2):
                            dve.wait_ge(result, g.n - 1)
                        nc.vector.tensor_tensor(h_rows[0:p, s, 0:t * D], bank(6 + s, t * D)[0:p, :],
                                                relu_rows[0:p, s4, 0:t * D], ALU.add).then_inc(h_done, 1)
                        dve.wait_ge(h_done, g.n + 1)
                        for k in range(t):
                            last = nc.vector.bn_stats(stats2[0:p, s, k, :], h_rows[0:p, s, k * D:(k + 1) * D])
                        last.then_inc(stats2_done, 1)
                        wait_apart(dve, stats2_done, g.n + 1)
                        for k in range(t):
                            last = nc.vector.bn_aggr(moments2[0:p, s, k, :], stats2[0:p, s, k, :])
                        last.then_inc(moments2_done, 1)

                    def scale(g):
                        p, t = shape(g)
                        s = g.slot(2)
                        for k in range(t):
                            v = h_rows[0:p, s, k * D:(k + 1) * D]
                            last = nc.vector.scalar_tensor_tensor(out=v, in0=v, scalar=moments2[0:p, s, k, 0:1],
                                                                  in1=lng[0:p, :], op0=ALU.subtract,
                                                                  op1=ALU.mult)
                        last.then_inc(scaled, 1)

                    def conclude(g):
                        p, t = shape(g)
                        s, s4 = g.slot(2), g.slot(4)
                        dve.wait_ge(scaled, g.n + 1)
                        dve.wait_ge(rstd2_done, g.n + 1)
                        dve.wait_ge(biased, g.n + 1)
                        if g.reuses(2):
                            dve.wait_ge(stored[s], 16 * g.use(2))
                        for k in range(t):
                            last = nc.vector.scalar_tensor_tensor(out=rows_out[0:p, s, k * D:(k + 1) * D],
                                                                  in0=h_rows[0:p, s, k * D:(k + 1) * D],
                                                                  scalar=rstd2[0:p, s, k:k + 1],
                                                                  in1=x1_biased[0:p, s4, k * D:(k + 1) * D],
                                                                  op0=ALU.mult, op1=ALU.add)
                        last.then_inc(result, 1)

                    def scale_start(g):
                        dve.wait_ge(moments2_done, g.n + 1)
                        scale(g)

                    pipelined(dve, G, (3, residual), (0, measure), (3, scale_start), (0, shift_by), (3, conclude),
                              (1, add_agg))
                    for part in (measure, shift_by, add_agg, residual, scale_start, conclude):
                        part(END)

                @block.scalar
                def _(act):
                    def normalize(g):
                        p, t = shape(g)
                        s, s4 = g.slot(2), g.slot(4)
                        act.wait_ge(shift_done, g.n + 1)
                        if g.reuses(4):
                            act.wait_ge(h_done, g.n - 3)
                        for k in range(t):
                            last = nc.scalar.activation(relu_rows[0:p, s4, k * D:(k + 1) * D],
                                                        rows_in[0:p, s4, k * D:(k + 1) * D], ACT.Relu,
                                                        bias=shift[0:p, s, k:k + 1], scale=rstd[0:p, s, k:k + 1])
                        last.then_inc(relu_done, 1)

                    def copy_cols(g):
                        p, t = shape(g)
                        s = g.slot(2)
                        act.wait_ge(turned, g.n + 1)
                        if g.reuses(2):
                            act.wait_ge(product, g.n - 1)
                        w = (t - 1) * P + p
                        nc.scalar.activation(cols2[0:D, s, 0:w], two_banks(0, w)[0:D, :], ACT.Copy)\
                            .then_inc(cols_done, 1)

                    def gelu(g):
                        p, t = shape(g)
                        s = g.slot(2)
                        act.wait_ge(turned2, g.n + 1)
                        if g.reuses(2):
                            act.wait_ge(product2, g.n - 1)
                        w = (t - 1) * P + p
                        nc.scalar.activation(cols[0:D, s, 0:w], two_banks(2, w)[0:D, :], ACT.Gelu,
                                             bias=ub1c[:, :]).then_inc(gelu_done, 1)

                    def store(g):
                        p, t = shape(g)
                        s = g.slot(2)
                        act.wait_ge(result, g.n + 1)
                        act.dma_start(rows_of(out, g), rows_out[0:p, s, 0:t * D]).then_inc(stored[s], 16)

                    pipelined(act, G, (1, copy_cols), (2, gelu), (0, normalize), (3, store))
                    for part in (normalize, copy_cols, gelu, store):
                        part(END)
                    act.wait_ge(stored[0], 16 * -(-(G + 1) // 2))
                    act.wait_ge(stored[1], 16 * ((G + 1) // 2))

                @block.tensor
                def _(pe):
                    def turn(g):
                        p, t = shape(g)
                        pe.wait_ge(relu_done, g.n + 1)
                        if g.reuses(1):
                            pe.wait_ge(cols_done, g.n)
                        for k in range(t):
                            last = nc.tensor.transpose(two_banks(0, T * P)[0:D, k * P:k * P + p],
                                                       relu_rows[0:p, g.slot(4), k * D:(k + 1) * D],
                                                       ident[0:p, 0:p])
                        last.then_inc(turned, 1)

                    def multiply(g):
                        p, t = shape(g)
                        s = g.slot(2)
                        pe.wait_ge(cols_done, g.n + 1)
                        if g.reuses(2):
                            pe.wait_ge(summed, g.n - 1)
                        for k in range(t):
                            last = nc.tensor.matmul(bank(4 + s, T * D)[0:p, k * D:(k + 1) * D],
                                                    cols2[0:D, s, k * P:k * P + p], uw1n[:, :],
                                                    start=True, stop=True)
                        last.then_inc(product, 1)

                    def turn2(g):
                        p, t = shape(g)
                        s = g.slot(2)
                        pe.wait_ge(summed, g.n + 1)
                        if g.reuses(1):
                            pe.wait_ge(gelu_done, g.n)
                        for k in range(t):
                            last = nc.tensor.transpose(two_banks(2, T * P)[0:D, k * P:k * P + p],
                                                       mid_rows[0:p, s, k * D:(k + 1) * D], ident[0:p, 0:p])
                        last.then_inc(turned2, 1)

                    def multiply2(g):
                        p, t = shape(g)
                        s = g.slot(2)
                        pe.wait_ge(gelu_done, g.n + 1)
                        if g.reuses(2):
                            pe.wait_ge(h_done, g.n - 1)
                        for k in range(t):
                            last = nc.tensor.matmul(bank(6 + s, T * D)[0:p, k * D:(k + 1) * D],
                                                    cols[:, s, k * P:k * P + p], uw2[:, :],
                                                    start=True, stop=True)
                        last.then_inc(product2, 1)

                    pipelined(pe, G, (1, turn), (2, turn2), (1, multiply), (2, multiply2))
                    for part in (turn, multiply, turn2, multiply2):
                        part(END)

        run(node_pass, "a", x, None, True, wr1, pre1, x)
        run(edge_pass, "ea", None, "norm", wl1, pre1)
        run(node_pass, "b", pre1, x, False, wr2, x1, pre1)
        run(edge_pass, "eb", None, "relu", wl2, x1)
        run(edge_pass, "ec", x1, "mlp", uw1e, aggu)
        run(update_pass)


def kernel(**inputs):
    import numpy as _np
    import concourse.bacc as _bacc
    from concourse import mybir as _mybir
    from concourse.bass_utils import run_bass_kernel_spmd as _run

    nc = _bacc.Bacc("TRN2", target_bir_lowering=False, num_devices=1)
    get = {k: _np.asarray(v) for k, v in inputs.items()}

    def column(name):
        return get[name].reshape(-1, 1)

    def line(name):
        return get[name].reshape(1, -1)

    src = _np.concatenate([get["src"], _np.zeros(EP - E, get["src"].dtype)])
    dst = _np.concatenate([get["dst"], _np.full(EP - E + 1, N, get["dst"].dtype)])
    attr = _np.concatenate([get["edge_attr_32"], _np.zeros((EP - E, ED), get["edge_attr_32"].dtype)])
    dst3 = _np.stack([dst[:EP].reshape(EDGE_TILES, P).T, dst[1:].reshape(EDGE_TILES, P).T,
                      dst[:EP].reshape(P, EDGE_TILES)])
    laid = [
        ("x", get["x"]), ("src", src.reshape(EDGE_TILES, P).T), ("dst", dst3), ("edge_attr", attr),
        ("Wl1t", get["L0_gnn_Wl1"].T), ("bl1", line("L0_gnn_bl1")), ("Wr1t", get["L0_gnn_Wr1"].T),
        ("Wl2t", get["L0_gnn_Wl2"].T), ("bl2", line("L0_gnn_bl2")), ("Wr2t", get["L0_gnn_Wr2"].T),
        ("mW1", get["L1_gnn_mW1"]), ("mb1", column("L1_gnn_mb1")), ("mW2", get["L1_gnn_mW2"]),
        ("mb2", line("L1_gnn_mb2")), ("gW1", get["L1_gnn_gW1"]), ("gb1", column("L1_gnn_gb1")),
        ("gW2", get["L1_gnn_gW2"]), ("gb2", line("L1_gnn_gb2")), ("uW1", get["L1_gnn_uW1"]),
        ("ub1", column("L1_gnn_ub1")), ("uW2", get["L1_gnn_uW2"]), ("ub2", line("L1_gnn_ub2")),
        ("ln_g", line("L1_gnn_ln_g")), ("ln_b", line("L1_gnn_ln_b")),
    ]
    arrays, args = {}, []
    for name, a in laid:
        a = _np.ascontiguousarray(a)
        arrays[f"in_{name}"] = a
        args.append(nc.dram_tensor(f"in_{name}", a.shape, _mybir.dt.from_np(a.dtype), kind="ExternalInput").ap())
    out = nc.dram_tensor("out_0", (N, D), _mybir.dt.float32, kind="ExternalOutput").ap()
    gnn_kernel(nc, *args, out)
    r = _run(nc, [arrays], core_ids=[0])
    return r.results[0]["out_0"]
```

```python
import concourse.bass as bass
from concourse import mybir
from contextlib import ExitStack

FP32 = mybir.dt.float32
INT32 = mybir.dt.int32
UINT8 = mybir.dt.uint8
ALU = mybir.AluOpType
ACT = mybir.ActivationFunctionType
AXX = mybir.AxisListType.X

P = 128
D = 96
ED = 32
N = 50000
E = 25000
LN_EPS = 1e-5

T = 5
GROUP_ROWS = P * T
NODE_GROUPS = N // GROUP_ROWS
TAIL = N - NODE_GROUPS * GROUP_ROWS

Q = 4
EDGE_TILES = Q * -(-E // (Q * P))
EP = EDGE_TILES * P
EDGE_GROUPS = EDGE_TILES // Q
SPARE = 4 * Q
ROWS = N + SPARE * P
assert TAIL <= P

RANK_CHUNK = EP // 8
RANK_CHUNKS = EP // RANK_CHUNK
ROOT_MAGIC = 1597463040.0
INDEX_STEP = 1.0 / 32768.0
assert EP < 32768

UNROLL = 4
FETCH = (3, 2, 3, 2)
FETCH_AT = (0, 3, 5, 8)
FETCHES = -(-NODE_GROUPS // UNROLL)
assert FETCHES * sum(FETCH) >= EDGE_TILES

ZERO_COLS = 1875
ZERO_CHUNKS = N * D // P // ZERO_COLS
assert ZERO_CHUNKS * ZERO_COLS * P == N * D


class Group:

    def __init__(self, i, c):
        self.n, self.i, self.c = UNROLL * i + c, i, c

    def slot(self, slots):
        return self.c % slots

    def use(self, slots):
        return (UNROLL // slots) * self.i + self.c // slots

    def reuses(self, slots):
        return not (isinstance(self.n, int) and self.n < slots)


def pipelined(engine, groups, *stages):
    lags = [lag if isinstance(lag, tuple) else (lag,) for lag, _ in stages]
    last_lag = max(max(several) for several in lags)
    first = UNROLL * -(-(last_lag + 2) // UNROLL)
    bodies = (groups - first) // UNROLL

    def step(i, c):
        for several, (_, part) in zip(lags, stages):
            gs = [Group(i + (c - lag) // UNROLL, (c - lag) % UNROLL) for lag in several]
            gs = [g if not isinstance(g.n, int) or 0 <= g.n < groups else None for g in gs]
            if any(g is not None for g in gs):
                part(*gs)

    for t in range(first):
        step(t // UNROLL, t % UNROLL)
    with engine.Fori(first // UNROLL, first // UNROLL + bodies) as i:
        for c in range(UNROLL):
            step(i, c)
    for t in range(first + UNROLL * bodies, groups + last_lag):
        step(t // UNROLL, t % UNROLL)


def gnn_kernel(nc, x, src, dst, edge_attr, Wl1t, bl1, Wr1t, Wl2t, bl2, Wr2t, mW1, mb1, mW2, mb2, gW1, gb1, gW2, gb2,
               uW1, ub1, uW2, ub2, ln_g, ln_b, out):
    ctx = ExitStack()
    with ctx:
        def sb(name, shape, dt=FP32):
            return ctx.enter_context(nc.sbuf_tensor(name, shape, dt))

        of_stage = None

        def sem(name):
            if of_stage is None:
                return ctx.enter_context(nc.semaphore(name))
            of_stage.append(nc.alloc_semaphore(name))
            return of_stage[-1]

        def run(part, *args):
            nonlocal of_stage
            of_stage = []
            part(*args)
            nc.clear_and_free_semaphores(of_stage)
            nc.all_engine_barrier()
            of_stage = None

        s_seen = sem("s_seen")

        def wait_apart(engine, semaphore, value):
            engine.wait_ge(semaphore, value)
            engine.sem_inc(s_seen, 1)

        def dram(name, shape, dt=FP32):
            return nc.dram_tensor(name, shape, dt, kind="Internal").ap()

        pre1 = dram("pre1", (ROWS, D))
        x1 = dram("x1", (ROWS, D))
        aggu = dram("aggu", (ROWS, D))
        src_sorted = dram("src_sorted", (EP, 1), INT32)
        dst_sorted = dram("dst_sorted", (EP, 1), INT32)
        attr_sorted = dram("attr_sorted", (EP, ED))

        ident = sb("ident", [P, P])
        causal = sb("causal", [P, P])
        ones = sb("ones", [P, P])
        minus_half = sb("minus_half", [P, T])
        eps = sb("eps", [P, 1])
        zeros = sb("zeros", [P, ZERO_COLS])
        wr1 = sb("wr1", [D + 1, D])
        wl1 = sb("wl1", [D + 1, D + 1])
        wr2 = sb("wr2", [D + 1, D])
        wl2 = sb("wl2", [D, D])
        mw1 = sb("mw1", [P, D])
        gw1 = sb("gw1", [P, D])
        mb1c = sb("mb1c", [D, 1])
        gb1c = sb("gb1c", [D, 1])
        mw2 = sb("mw2", [D + 1, D])
        gw2 = sb("gw2", [D + 1, 1])
        uw1n = sb("uw1n", [D, D])
        uw1e = sb("uw1e", [D, D])
        ub1c = sb("ub1c", [D, 1])
        uw2 = sb("uw2", [D + 1, D])
        lng = sb("lng", [P, D])
        lnb = sb("lnb", [P, D])

        same = sb("same", [P, EDGE_TILES, P], UINT8)
        follows = sb("follows", [P, EDGE_TILES, P], UINT8)
        src_i = sb("src_i", [P, EDGE_TILES], INT32)
        dst_i = sb("dst_i", [P, EDGE_TILES], INT32)
        next_i = sb("next_i", [P, EDGE_TILES], INT32)
        dst_f = sb("dst_f", [P, EDGE_TILES])
        row_i = sb("row_i", [P, EDGE_TILES], INT32)
        inv_deg = sb("inv_deg", [P, EDGE_TILES])
        carry0 = sb("carry0", [P, 1])

        region = sb("region", [P, EDGE_TILES * P])
        taken = [0]

        def part_of_region(slots, width):
            at = taken[0]
            taken[0] += slots * width
            assert taken[0] <= EDGE_TILES * P
            return region[:, at:taken[0]].rearrange("p (s n) -> p s n", s=slots)

        dst_wide = region[:, :].bitcast(INT32)
        edge_rows = part_of_region(EDGE_TILES, D)
        fetched = part_of_region(sum(FETCH), D)
        same_f = part_of_region(2, Q * P)
        sums_out = part_of_region(4, Q * D)
        aggs = part_of_region(2, Q * P)
        tile_dsts = part_of_region(UNROLL, 1 + 3 * P).bitcast(INT32)
        taken[0] = 0
        edge_in = part_of_region(4, Q * P)
        edge_cols = part_of_region(2, Q * P)
        taken[0] = 0
        relu_rows = part_of_region(4, T * D)
        x1_biased = part_of_region(4, T * D)
        h_rows = part_of_region(4, T * D)
        h2_cols = part_of_region(4, T * P)
        result_rows = part_of_region(4, T * D)

        rows_in = sb("rows_in", [P, 4, T * D])
        rows_in2 = sb("rows_in2", [P, 4, T * D])
        stats = sb("stats", [P, 2, T, 6])
        moments = sb("moments", [P, 2, T, 2])
        var_eps = sb("var_eps", [P, 2, T])
        rstd = sb("rstd", [P, 2, T])
        guess = sb("guess", [P, 2, T])
        factor = sb("factor", [P, 2, T])
        shift = sb("shift", [P, 2, T])
        shift2 = sb("shift2", [P, 2, T])
        stats2 = sb("stats2", [P, 2, T, 6])
        moments2 = sb("moments2", [P, 2, T, 2])
        var_eps2 = sb("var_eps2", [P, 2, T])
        rstd2 = sb("rstd2", [P, 2, T])
        normed = sb("normed", [P, 2, T * D])
        cols = sb("cols", [D + 1, 2, T * P])
        cols2 = sb("cols2", [D + 1, 2, T * P])
        rows_out = sb("rows_out", [P, 2, T * D])
        msgs = sb("msgs", [P, 2, Q, D + 1])
        gate = sb("gate", [P, 2, Q])
        gate1 = sb("gate1", [P, 2, Q])
        idx = sb("idx", [P, 4, Q], INT32)
        to_row = sb("to_row", [P, 4, Q], INT32)

        psum = ctx.enter_context(nc.psum_tensor("psum", [P, 8, 512], FP32))

        def two_banks(b, w):
            return psum[:, b:b + 2, :].rearrange("p b n -> p (b n)")[:, 0:w]

        def bank(b, w):
            return psum[:, b, 0:w]

        s_weights = sem("s_weights")
        s_edges = sem("s_edges")
        s_attr = sem("s_attr")
        s_line = sem("s_line")
        s_const = sem("s_const")
        s_const_step = sem("s_const_step")
        s_spare = sem("s_spare")
        s_order = sem("s_order")
        s_inversions = sem("s_inversions")
        s_flag = sem("s_flag")
        flag_f = sb("flag_f", [P, 1])
        flag_i = sb("flag_i", [1, 1], INT32)
        scr = [rows_in2[:, k, 0:EDGE_TILES] for k in range(3)]

        WEIGHT_LOADS = 21

        with nc.Block() as block:
            @block.sync
            def _(sp):
                sp.dma_start(src_i[:, :], src).then_inc(s_edges, 16)
                sp.dma_start(dst_i[:, :], dst[0]).then_inc(s_edges, 16)
                sp.dma_start(next_i[:, :], dst[1]).then_inc(s_edges, 16)
                sp.dma_start(dst_sorted.rearrange("(p e) a -> p (e a)", p=P), dst[2]).then_inc(s_line, 16)
                loads = [(wr1[0:D, :], Wr1t), (wr1[D:D + 1, :], bl1), (wl1[0:D, 0:D], Wl1t),
                         (wr2[0:D, :], Wr2t), (wr2[D:D + 1, :], bl2), (wl2[:, :], Wl2t),
                         (mw1[:, :], mW1), (gw1[:, :], gW1), (mb1c[:, :], mb1), (gb1c[:, :], gb1),
                         (mw2[0:D, :], mW2), (mw2[D:D + 1, :], mb2), (gw2[0:D, :], gW2), (gw2[D:D + 1, :], gb2),
                         (uw1n[:, :], uW1[0:D, :]), (uw1e[:, :], uW1[D:2 * D, :]), (ub1c[:, :], ub1),
                         (uw2[0:D, :], uW2), (uw2[D:D + 1, :], ub2),
                         (lng[:, :], ln_g.broadcast_to([P, D])), (lnb[:, :], ln_b.broadcast_to([P, D]))]
                assert len(loads) == WEIGHT_LOADS
                sp.wait_ge(s_const, 1)
                for dest, source in loads:
                    sp.dma_start(dest, source).then_inc(s_weights, 16)
                sp.dma_start(attr_sorted.rearrange("(p a) n -> p (a n)", p=P),
                             edge_attr.rearrange("(p a) n -> p (a n)", p=P)).then_inc(s_attr, 16)
                for rows in (pre1, x1):
                    sp.dma_start(rows[N:ROWS, :].rearrange("(p a) n -> p (a n)", p=P),
                                 zeros[:, 0:SPARE * D]).then_inc(s_spare, 16)
                sp.wait_ge(s_line, 16)

            @block.gpsimd
            def _(pool):
                step = [0]

                def done(instruction):
                    step[0] += 1
                    instruction.then_inc(s_const_step, 1)
                    pool.wait_ge(s_const_step, step[0])

                done(pool.memset(wl1[:, :], 0.0))
                done(pool.memset(wl1[D:D + 1, D:D + 1], 1.0))
                done(pool.memset(zeros[:, :], 0.0))
                pool.memset(ones[:, :], 1.0).then_inc(s_const, 1)
                pool.wait_ge(s_const, 1)
                done(pool.memset(minus_half[:, :], -0.5))
                done(pool.memset(eps[:, :], LN_EPS))
                done(pool.memset(carry0[:, :], 0.0))
                done(pool.memset(cols[D:D + 1, :, :], 1.0))
                done(pool.memset(cols2[D:D + 1, :, :], 1.0))
                done(pool.memset(msgs[:, :, :, D:D + 1], 1.0))
                done(pool.affine_select(out=ident[:, :], in_=ones[:, :], compare_op=ALU.is_equal, fill=0.0, base=0,
                                        pattern=[[-1, P]], channel_multiplier=1))
                done(pool.affine_select(out=causal[:, :], in_=ones[:, :], compare_op=ALU.is_ge, fill=0.0, base=0,
                                        pattern=[[1, P]], channel_multiplier=-1))
                whole = EDGE_TILES // SPARE * SPARE
                done(pool.iota(row_i[:, 0:whole].rearrange("p (a b) -> p a b", b=SPARE),
                               [[0, whole // SPARE], [P, SPARE]], base=N, channel_multiplier=1))
                done(pool.iota(row_i[:, whole:EDGE_TILES], [[P, EDGE_TILES - whole]], base=N,
                               channel_multiplier=1))

            @block.vector
            def _(dve):
                dve.wait_ge(s_edges, 48)
                nc.vector.tensor_tensor(scr[0][:, :], dst_i[:, :], next_i[:, :], ALU.is_gt).then_inc(s_order, 1)
                dve.wait_ge(s_order, 1)
                nc.vector.reduce_sum(flag_f[:, :], scr[0][:, :], AXX).then_inc(s_order, 1)
                dve.wait_ge(s_inversions, 1)
                nc.vector.tensor_copy(flag_i[:, :], psum[0:1, 0, 0:1]).then_inc(s_flag, 1)

            @block.tensor
            def _(pe):
                pe.wait_ge(s_order, 2)
                pe.wait_ge(s_const, 1)
                nc.tensor.matmul(psum[0:1, 0, 0:1], flag_f[:, :], ones[:, 0:1], start=True,
                                 stop=True).then_inc(s_inversions, 1)

        place_f = sb("place_f", [P, 1])
        place_i = sb("place_i", [P, 1], INT32)
        counts = sb("counts", [P, RANK_CHUNKS])
        limits = sb("limits", [P, RANK_CHUNKS])
        chunk_tiles = 4 * RANK_CHUNK // P
        assert 2 * chunk_tiles <= EDGE_TILES and RANK_CHUNKS * RANK_CHUNK == EP
        frac_i = follows[:, 0:chunk_tiles, :].rearrange("p e i -> p (e i)").bitcast(INT32)
        frac = follows[:, chunk_tiles:2 * chunk_tiles, :].rearrange("p e i -> p (e i)").bitcast(FP32)
        diff = same[:, 0:chunk_tiles, :].rearrange("p e i -> p (e i)").bitcast(FP32)
        attr_tile = sb("attr_tile", [P, ED])
        own_i = sb("own_i", [P, 2], INT32)
        index_i = rows_in[:, 0, 0:EDGE_TILES].bitcast(INT32)
        r_iota = sem("r_iota")
        r_wide = sem("r_wide")
        r_prep = sem("r_prep")
        r_step = sem("r_step")
        r_place = sem("r_place")
        r_attr = sem("r_attr")
        r_moved = sem("r_moved")
        r_done = sem("r_done")
        r_sorted = sem("r_sorted")
        index_f = scr[1]
        limit_base = scr[2]

        with nc.Block() as block:
            @block.gpsimd
            def _(pool):
                unsorted = pool.value_load(flag_i[0:1, 0:1], min_val=0, max_val=EP)
                with pool.If(unsorted > 0):
                    pool.iota(frac_i, [[1, RANK_CHUNK]], base=0, channel_multiplier=0).then_inc(r_iota, 1)
                    pool.iota(index_i[:, :], [[P, EDGE_TILES]], base=0, channel_multiplier=1).then_inc(r_iota, 1)
                    pool.wait_ge(r_iota, 2)
                    pool.sem_inc(r_done, 1)
                    pool.wait_ge(s_attr, 16)
                    pool.dma_start(dst_wide, dst[2].rearrange("p e -> (p e)").rearrange("(a n) -> a n", a=1)
                                   .broadcast_to([P, EP])).then_inc(r_wide, 16)
                    with pool.Fori(0, EDGE_TILES) as e:
                        pool.dma_start(attr_tile[:, :], edge_attr.rearrange("(e p) n -> e p n", p=P)[e])\
                            .then_inc(r_attr, 16)
                        pool.wait_ge(r_attr, 16 * e + 16)
                        wait_apart(pool, r_place, e + 1)
                        at = bass.IndirectOffsetOnAxis(ap=place_i[:, 0:1], axis=0)
                        pool.indirect_dma_start(src_sorted, at, own_i[:, 0:1], None).then_inc(r_moved, 16)
                        pool.indirect_dma_start(dst_sorted, at, own_i[:, 1:2], None).then_inc(r_moved, 16)
                        pool.indirect_dma_start(attr_sorted, at, attr_tile[:, :], None).then_inc(r_moved, 16)
                        pool.wait_ge(r_moved, 48 * e + 48)
                        pool.sem_inc(r_done, 1)
                    with pool.Fori(0, EDGE_TILES) as e:
                        with nc.allow_non_contiguous_dma(reason="one index per partition"):
                            by_tile = [a.rearrange("(e p) n -> e p n", p=P) for a in (src_sorted, dst_sorted)]
                            pool.dma_start(src_i[:, bass.ds(e, 1)], by_tile[0][e]).then_inc(r_sorted, 16)
                            pool.dma_start(dst_i[:, bass.ds(e, 1)], by_tile[1][e]).then_inc(r_sorted, 16)
                        pool.wait_ge(r_sorted, 32 * e + 32)
                    with pool.Fori(0, EDGE_TILES - 1) as e:
                        after = dst_sorted[1:EP - P + 1, :].rearrange("(e p) n -> e p n", p=P)
                        pool.dma_start(next_i[:, bass.ds(e, 1)], after[e]).then_inc(r_sorted, 16)
                        pool.wait_ge(r_sorted, 16 * e + 32 * EDGE_TILES + 16)
                    pool.dma_start(next_i[0:P - 1, EDGE_TILES - 1:EDGE_TILES], dst_sorted[EP - P + 1:EP, :])\
                        .then_inc(r_sorted, 16)
                    pool.wait_ge(r_sorted, 16 * (3 * EDGE_TILES))
                with pool.Else():
                    pool.sem_inc(r_iota, 1)

            @block.vector
            def _(dve):
                unsorted = dve.value_load(flag_i[0:1, 0:1], min_val=0, max_val=EP)
                with dve.If(unsorted > 0):
                    dve.wait_ge(r_iota, 2)
                    dve.wait_ge(r_wide, 16)
                    nc.vector.tensor_scalar(frac, frac_i, INDEX_STEP, None, ALU.mult).then_inc(r_prep, 1)
                    nc.vector.tensor_scalar(index_f[:, :], index_i[:, :], INDEX_STEP, None, ALU.mult)\
                        .then_inc(r_prep, 1)
                    nc.vector.tensor_copy(dst_f[:, :], dst_i[:, :]).then_inc(r_prep, 1)
                    nc.vector.tensor_scalar(limit_base[:, 0:RANK_CHUNKS], index_i[:, 0:RANK_CHUNKS], 0.0, None,
                                            ALU.mult).then_inc(r_prep, 1)
                    dve.wait_ge(r_prep, 4)
                    for c in range(RANK_CHUNKS):
                        nc.vector.memset(limit_base[:, c:c + 1], -c * RANK_CHUNK * INDEX_STEP).then_inc(r_prep, 1)
                    dve.wait_ge(r_prep, 4 + RANK_CHUNKS)
                    per_tile = 2 * RANK_CHUNKS + 5
                    with dve.Fori(0, EDGE_TILES) as e:
                        step = [0]

                        def done(instruction):
                            step[0] += 1
                            instruction.then_inc(r_step, 1)
                            dve.wait_ge(r_step, e * per_tile + step[0])

                        done(nc.vector.tensor_scalar(limits[:, :], limit_base[:, 0:RANK_CHUNKS],
                                                     index_f[:, bass.ds(e, 1)], None, ALU.add))
                        for c in range(RANK_CHUNKS):
                            wide = dst_wide[:, c * RANK_CHUNK:(c + 1) * RANK_CHUNK]
                            done(nc.vector.scalar_tensor_tensor(out=diff, in0=wide,
                                                                scalar=dst_f[:, bass.ds(e, 1)], in1=frac,
                                                                op0=ALU.subtract, op1=ALU.add))
                            done(nc.vector.tensor_scalar(diff, diff, limits[:, c:c + 1], 0.0,
                                                         ALU.is_lt, ALU.add, accum_out=counts[:, c:c + 1]))
                        done(nc.vector.reduce_sum(place_f[:, :], counts[:, :], AXX))
                        dve.wait_ge(r_done, e + 1)
                        done(nc.vector.tensor_copy(own_i[:, 0:1], src_i[:, bass.ds(e, 1)]))
                        done(nc.vector.tensor_copy(own_i[:, 1:2], dst_i[:, bass.ds(e, 1)]))
                        done(nc.vector.tensor_copy(place_i[:, :], place_f[:, :]))
                        nc.vector.memset(counts[:, :], 0.0).then_inc(r_place, 1)
                with dve.Else():
                    dve.sem_inc(r_prep, 1)

        row_step = sem("row_step")
        with nc.Block() as block:
            @block.vector
            def _(dve):
                step = [0]

                def done(instruction):
                    step[0] += 1
                    instruction.then_inc(row_step, 1)
                    dve.wait_ge(row_step, step[0])

                a, b, c = scr
                done(nc.vector.tensor_copy(dst_f[:, :], dst_i[:, :]))
                done(nc.vector.memset(tile_dsts[:, 0, 0:1], -1))
                done(nc.vector.tensor_tensor(a[:, :], dst_i[:, :], next_i[:, :], ALU.not_equal))
                done(nc.vector.tensor_scalar(b[:, :], dst_f[:, :], float(N), None, ALU.is_lt))
                done(nc.vector.tensor_tensor(a[:, :], a[:, :], b[:, :], ALU.mult))
                done(nc.vector.tensor_copy(c[:, :], row_i[:, :]))
                done(nc.vector.tensor_tensor(b[:, :], dst_f[:, :], c[:, :], ALU.subtract))
                done(nc.vector.tensor_tensor(b[:, :], b[:, :], a[:, :], ALU.mult))
                done(nc.vector.tensor_tensor(row_i[:, :], b[:, :], c[:, :], ALU.add))

        def by_group(rows):
            return rows[0:NODE_GROUPS * GROUP_ROWS, :].rearrange("(g p t) d -> g p (t d)", p=P, t=T)

        def tail(rows):
            return rows[NODE_GROUPS * GROUP_ROWS:N, :]

        END = Group(NODE_GROUPS // UNROLL, NODE_GROUPS % UNROLL)

        def shape(g):
            return (TAIL, 1) if g is END else (P, T)

        def rows_of(dram_rows, g):
            return tail(dram_rows) if g is END else by_group(dram_rows)[g.n]

        def tiles_of(g):
            first = g.i * sum(FETCH) + FETCH_AT[g.c]
            if isinstance(g.n, int):
                return first, min(FETCH[g.c], EDGE_TILES - first)
            return first, FETCH[g.c]

        def by_row(buffer_rows, p, t):
            return buffer_rows[0:p, 0:t * D].rearrange("p (t d) -> p t d", t=t)

        def refine(dve, s, p, t, steps, before, done, parts=(0, 1, 2)):
            y, a = guess[0:p, s, 0:t], factor[0:p, s, 0:t]
            if 0 in parts:
                dve.wait_ge(steps, before)
                nc.vector.scalar_tensor_tensor(out=a, in0=moments[0:p, s, 0:t, 1], scalar=LN_EPS, in1=y,
                                               op0=ALU.add, op1=ALU.mult).then_inc(steps, 1)
            if 1 in parts:
                dve.wait_ge(steps, before + 1)
                nc.vector.scalar_tensor_tensor(out=a, in0=a, scalar=-0.5, in1=y, op0=ALU.mult,
                                               op1=ALU.mult).then_inc(steps, 1)
            if 2 in parts:
                dve.wait_ge(steps, before + 2)
                to, signal = done
                nc.vector.scalar_tensor_tensor(out=to[0:p, s, 0:t], in0=a, scalar=1.5, in1=y, op0=ALU.add,
                                               op1=ALU.mult).then_inc(signal, 1)

        def node_pass(name, source, addend, norm, weight, dest, edge_source):
            masks = norm
            G = NODE_GROUPS
            loaded = [sem(f"{name}_loaded{s}") for s in range(4)]
            addend_in = [sem(f"{name}_addend{s}") for s in range(4)]
            stats_done = sem(f"{name}_stats")
            moments_done = sem(f"{name}_moments")
            root_done = sem(f"{name}_root")
            root_steps = sem(f"{name}_root_steps")
            rstd_done = sem(f"{name}_rstd")
            shift_done = sem(f"{name}_shift")
            normed_done = sem(f"{name}_normed")
            turned = sem(f"{name}_turned")
            cols_done = sem(f"{name}_cols")
            product = sem(f"{name}_product")
            result = sem(f"{name}_result")
            stored = [sem(f"{name}_stored{s}") for s in range(2)]
            indices = [sem(f"{name}_indices{s}") for s in range(UNROLL)]
            fetch_in = [sem(f"{name}_fetch{s}") for s in range(UNROLL)]
            kept = [sem(f"{name}_kept{s}") for s in range(UNROLL)]
            dsts_in = [sem(f"{name}_dsts{s}") for s in range(UNROLL)]
            masked = [sem(f"{name}_masked{s}") for s in range(UNROLL)]

            def rest(part):
                for n in range(G, FETCHES * UNROLL):
                    g = Group(n // UNROLL, n % UNROLL)
                    if tiles_of(g)[1] > 0:
                        part(g)

            with nc.Block() as block:
                @block.sync
                def _(sp):
                    def load(g):
                        p, t = shape(g)
                        s = g.slot(4)
                        if g.reuses(4):
                            sp.wait_ge(normed_done if norm else turned, g.n - 3)
                        sp.dma_start(rows_in[0:p, s, 0:t * D], rows_of(source, g)).then_inc(loaded[s], 16)
                        if addend is not None:
                            if g.reuses(4):
                                sp.wait_ge(result, g.n - 3)
                            sp.dma_start(rows_in2[0:p, s, 0:t * D], rows_of(addend, g)).then_inc(addend_in[s], 16)

                    def load_dsts(g):
                        c = g.c
                        tile, n = tiles_of(g)
                        first = tile * P
                        line = dst_sorted.rearrange("n a -> a n")
                        if isinstance(g.n, int) and g.n == 0:
                            sp.dma_start(tile_dsts[:, c, 1:1 + n * P], line[:, 0:n * P].broadcast_to([P, n * P]))\
                                .then_inc(dsts_in[c], 16)
                            return
                        if g.reuses(UNROLL):
                            sp.wait_ge(masked[c], g.i)
                        sp.dma_start(tile_dsts[:, c, 0:1 + n * P],
                                     line[:, bass.ds(first - 1, 1 + n * P)].broadcast_to([P, 1 + n * P]))\
                            .then_inc(dsts_in[c], 16)

                    def store(g):
                        p, t = shape(g)
                        s = g.slot(2)
                        sp.wait_ge(result, g.n + 1)
                        sp.dma_start(rows_of(dest, g), rows_out[0:p, s, 0:t * D]).then_inc(stored[s], 16)

                    if masks:
                        pipelined(sp, G, (8, store), (0, load), (0, load_dsts))
                        rest(load_dsts)
                    else:
                        pipelined(sp, G, (4, store), (0, load))
                    load(END)
                    store(END)
                    sp.wait_ge(stored[0], 16 * -(-(G + 1) // 2))
                    sp.wait_ge(stored[1], 16 * ((G + 1) // 2))
                    if masks:
                        sp.wait_ge(s_spare, 32)

                @block.gpsimd
                def _(pool):
                    def fetch(g):
                        c = g.c
                        first, n = tiles_of(g)
                        if g.reuses(UNROLL):
                            wait_apart(pool, kept[c], g.i)
                        pool.tensor_copy(idx[:, c, 0:n], src_i[:, bass.ds(first, n)]).then_inc(indices[c], 1)
                        wait_apart(pool, indices[c], g.i + 1)
                        for k in range(n):
                            at = bass.IndirectOffsetOnAxis(ap=idx[:, c, k:k + 1], axis=0)
                            pool.indirect_dma_start(fetched[:, FETCH_AT[c] + k, :], None, edge_source, at)\
                                .then_inc(fetch_in[c], 16)

                    pipelined(pool, G, (0, fetch))
                    rest(fetch)

                @block.vector
                def _(dve):
                    def norm_step(new, old):
                        masked_too = old and old is not END and tiles_of(old)[1] > 0
                        if new:
                            p, t = shape(new)
                            s, s4 = new.slot(2), new.slot(4)
                            dve.wait_ge(loaded[s4], 16 * (new.use(4) + 1))
                            if new.reuses(2):
                                dve.wait_ge(shift_done, new.n - 1)
                            for k in range(t):
                                last = nc.vector.bn_stats(stats[0:p, s, k, :],
                                                          rows_in[0:p, s4, k * D:(k + 1) * D])
                            last.then_inc(stats_done, 1)
                        if old:
                            op, ot = shape(old)
                            o = old.slot(2)
                            dve.wait_ge(root_done, old.n + 1)
                            nc.vector.reciprocal(guess[0:op, o, 0:ot], var_eps[0:op, o, 0:ot])\
                                .then_inc(root_steps, 1)
                        if new:
                            wait_apart(dve, stats_done, new.n + 1)
                            for k in range(t):
                                last = nc.vector.bn_aggr(moments[0:p, s, k, :], stats[0:p, s, k, :])
                            last.then_inc(moments_done, 1)
                        for part in range(3):
                            if old:
                                if part == 2 and old.reuses(2):
                                    dve.wait_ge(normed_done, old.n - 1)
                                refine(dve, o, op, ot, root_steps, 3 * old.n + 1, (rstd, rstd_done), (part,))
                            if masked_too and part < tiles_of(old)[1]:
                                mask_tile(old, part)
                        if masked_too:
                            mask_follows(old)

                    def shift_by(g):
                        p, t = shape(g)
                        s = g.slot(2)
                        dve.wait_ge(rstd_done, g.n + 1)
                        if g.reuses(2):
                            dve.wait_ge(normed_done, g.n - 1)
                        nc.vector.scalar_tensor_tensor(out=shift[0:p, s, 0:t], in0=moments[0:p, s, 0:t, 0],
                                                       scalar=-1.0, in1=rstd[0:p, s, 0:t], op0=ALU.mult,
                                                       op1=ALU.mult).then_inc(shift_done, 1)

                    def add(g):
                        p, t = shape(g)
                        s, s4 = g.slot(2), g.slot(4)
                        dve.wait_ge(product, g.n + 1)
                        dve.wait_ge(addend_in[s4], 16 * (g.use(4) + 1))
                        if g.reuses(2):
                            dve.wait_ge(stored[s], 16 * g.use(2))
                        nc.vector.tensor_tensor(rows_out[0:p, s, 0:t * D], bank(4 + s, t * D)[0:p, :],
                                                rows_in2[0:p, s4, 0:t * D], ALU.add).then_inc(result, 1)

                    def mask_tile(g, k):
                        c = g.c
                        tile = tiles_of(g)[0] + k
                        dve.wait_ge(dsts_in[c], 16 * (g.i + 1))
                        nc.vector.scalar_tensor_tensor(out=same[:, bass.ds(tile, 1), :].rearrange("p a i -> p (a i)"),
                                                       in0=tile_dsts[:, c, 1 + k * P:1 + (k + 1) * P],
                                                       scalar=dst_f[:, bass.ds(tile, 1)], in1=causal[:, :],
                                                       op0=ALU.is_equal, op1=ALU.mult)

                    def mask_follows(g):
                        c = g.c
                        first, n = tiles_of(g)
                        tiles = tile_dsts[:, c, 1:1 + n * P].rearrange("p (e i) -> p e i", i=P)
                        before = tile_dsts[:, c, 0:n * P].rearrange("p (e i) -> p e i", i=P)[:, :, 0:1]
                        nc.vector.tensor_tensor(follows[:, bass.ds(first, n), :], tiles,
                                                before.broadcast_to([P, n, P]), ALU.is_equal)\
                            .then_inc(masked[c], 1)

                    def mask(g):
                        for k in range(tiles_of(g)[1]):
                            mask_tile(g, k)
                        mask_follows(g)

                    if norm:
                        pipelined(dve, G, ((0, 1), norm_step), (1, shift_by))
                        norm_step(END, None)
                        rest(mask)
                        norm_step(None, END)
                        shift_by(END)
                    if addend is not None:
                        pipelined(dve, G, (0, add))
                        add(END)

                @block.tensor
                def _(pe):
                    def turn(g):
                        p, t = shape(g)
                        s = g.slot(2)
                        if norm:
                            rows = normed[:, s, :]
                            pe.wait_ge(normed_done, g.n + 1)
                        else:
                            rows = rows_in[:, g.slot(4), :]
                            pe.wait_ge(loaded[g.slot(4)], 16 * (g.use(4) + 1))
                        if g.reuses(2):
                            pe.wait_ge(cols_done, g.n - 1)
                        for k in range(t):
                            last = nc.tensor.transpose(two_banks(2 * s, T * P)[0:D, k * P:k * P + p],
                                                       rows[0:p, k * D:(k + 1) * D], ident[0:p, 0:p])
                        last.then_inc(turned, 1)

                    def multiply(g):
                        p, t = shape(g)
                        s = g.slot(2)
                        pe.wait_ge(cols_done, g.n + 1)
                        if g.reuses(2):
                            pe.wait_ge(result, g.n - 1)
                        for k in range(t):
                            last = nc.tensor.matmul(bank(4 + s, T * D)[0:p, k * D:(k + 1) * D],
                                                    cols[:, s, k * P:k * P + p], weight[:, :],
                                                    start=True, stop=True)
                        last.then_inc(product, 1)

                    if masks:
                        pe.wait_ge(s_weights, 16 * WEIGHT_LOADS)
                    if norm:
                        pipelined(pe, G, (4, multiply), (2, turn))
                    else:
                        pipelined(pe, G, (0, turn), (1, multiply))
                    turn(END)
                    multiply(END)

                @block.scalar
                def _(act):
                    def rectify(g):
                        p, t = shape(g)
                        s = g.slot(2)
                        act.wait_ge(turned, g.n + 1)
                        if g.reuses(2):
                            act.wait_ge(product, g.n - 1)
                        w = (t - 1) * P + p
                        nc.scalar.activation(cols[0:D, s, 0:w], two_banks(2 * s, w)[0:D, :],
                                             ACT.Relu).then_inc(cols_done, 1)

                    def root(g):
                        p, t = shape(g)
                        s = g.slot(2)
                        act.wait_ge(moments_done, g.n + 1)
                        if g.reuses(2):
                            act.wait_ge(rstd_done, g.n - 1)
                        nc.scalar.activation(var_eps[0:p, s, 0:t], moments[0:p, s, 0:t, 1], ACT.Sqrt,
                                             bias=eps[0:p, :]).then_inc(root_done, 1)

                    def normalize(g):
                        p, t = shape(g)
                        s, s4 = g.slot(2), g.slot(4)
                        act.wait_ge(shift_done, g.n + 1)
                        if g.reuses(2):
                            act.wait_ge(turned, g.n - 1)
                        for k in range(t):
                            last = nc.scalar.activation(normed[0:p, s, k * D:(k + 1) * D],
                                                        rows_in[0:p, s4, k * D:(k + 1) * D], ACT.Relu,
                                                        bias=shift[0:p, s, k:k + 1], scale=rstd[0:p, s, k:k + 1])
                        last.then_inc(normed_done, 1)

                    def copy_out(g):
                        p, t = shape(g)
                        s = g.slot(2)
                        act.wait_ge(product, g.n + 1)
                        if g.reuses(2):
                            act.wait_ge(stored[s], 16 * g.use(2))
                        nc.scalar.activation(rows_out[0:p, s, 0:t * D], bank(4 + s, t * D)[0:p, :],
                                             ACT.Copy).then_inc(result, 1)

                    def keep(g):
                        c = g.c
                        first, n = tiles_of(g)
                        act.wait_ge(fetch_in[c], 16 * (FETCH[c] * g.i + n))
                        nc.scalar.activation(edge_rows[:, bass.ds(first, n), :],
                                             fetched[:, FETCH_AT[c]:FETCH_AT[c] + n, :], ACT.Copy)\
                            .then_inc(kept[c], 1)

                    if norm:
                        pipelined(act, G, (5, copy_out), (3, rectify), (0, root), (1, normalize), (3, keep))
                        root(END)
                        normalize(END)
                    else:
                        pipelined(act, G, (0, rectify), (2, keep))
                    rectify(END)
                    if addend is None:
                        copy_out(END)
                    rest(keep)

        def edge_pass(name, source, kind, weight, dest):
            mlp = kind == "mlp"
            norm = kind != "relu"
            counted = kind == "norm"
            W = D + 1 if counted else D
            G = EDGE_GROUPS
            indices = sem(f"{name}_indices")
            gathered = [sem(f"{name}_gathered{s}") for s in range(4)]
            attr_in = [sem(f"{name}_attr{s}") for s in range(4)]
            stats_done = sem(f"{name}_stats")
            moments_done = sem(f"{name}_moments")
            root_done = sem(f"{name}_root")
            root_steps = sem(f"{name}_root_steps")
            rstd_done = sem(f"{name}_rstd")
            shift_done = sem(f"{name}_shift")
            normed_done = sem(f"{name}_normed")
            turned = sem(f"{name}_turned")
            cols_done = sem(f"{name}_cols")
            attr_cols = sem(f"{name}_attr_cols")
            hidden = sem(f"{name}_hidden")
            gelu_done = sem(f"{name}_gelu")
            message_done = sem(f"{name}_message")
            tanh_done = sem(f"{name}_tanh")
            gate_done = sem(f"{name}_gate")
            msgs_done = sem(f"{name}_msgs")
            widened = sem(f"{name}_widened")
            summed = sem(f"{name}_summed")
            carried = sem(f"{name}_carried")
            product = sem(f"{name}_product")
            deg_step = sem(f"{name}_deg")
            result = sem(f"{name}_result")
            targets = sem(f"{name}_targets")
            scattered = [sem(f"{name}_scattered{s}") for s in range(4)]
            zeroed = sem(f"{name}_zeroed")
            TURN, HID, MSG, AGG, OUT = 0, 1, 3, 4, 6

            def tile_of(buffer, g, k):
                return buffer[:, bass.ds(g.n * Q + k, 1), :].rearrange("p a i -> p (a i)")

            def row(g, k):
                if mlp:
                    return edge_in[:, g.slot(4), k * P:k * P + D]
                return tile_of(edge_rows, g, k)

            def by_tile(columns):
                return columns.rearrange("p (q n) -> p q n", q=Q)

            with nc.Block() as block:
                @block.sync
                def _(sp):
                    if counted:
                        flat = aggu[0:N, :].rearrange("a n -> (a n)").rearrange("(p m) -> p m", p=P)
                        for c in range(ZERO_CHUNKS):
                            sp.dma_start(flat[:, c * ZERO_COLS:(c + 1) * ZERO_COLS], zeros[:, :])\
                                .then_inc(zeroed, 16)
                        sp.wait_ge(zeroed, 16 * ZERO_CHUNKS)
                    if mlp:
                        sp.wait_ge(s_attr, 16)

                        def load_attr(g):
                            s = g.slot(4)
                            if g.reuses(4):
                                sp.wait_ge(turned, g.n - 3)
                            at = attr_sorted.rearrange("(g q p) n -> g p q n", q=Q, p=P)[g.n]
                            sp.dma_start(by_tile(edge_in[:, s, :])[:, :, D:P], at).then_inc(attr_in[s], 16)

                        pipelined(sp, G, (0, load_attr))

                @block.gpsimd
                def _(pool):
                    def gather(g):
                        s = g.slot(4)
                        if g.reuses(4):
                            wait_apart(pool, turned, g.n - 3)
                        pool.tensor_copy(idx[:, s, :], src_i[:, bass.ds(g.n * Q, Q)]).then_inc(indices, 1)
                        wait_apart(pool, indices, g.n + 1)
                        for k in range(Q):
                            at = bass.IndirectOffsetOnAxis(ap=idx[:, s, k:k + 1], axis=0)
                            pool.indirect_dma_start(row(g, k), None, source, at).then_inc(gathered[s], 16)

                    def scatter(g):
                        s = g.slot(4)
                        if g.reuses(4):
                            pool.wait_ge(scattered[s], 16 * Q * g.use(4))
                        pool.tensor_copy(to_row[:, s, :], row_i[:, bass.ds(g.n * Q, Q)]).then_inc(targets, 1)
                        wait_apart(pool, targets, g.n + 1)
                        wait_apart(pool, result, g.n + 1)
                        for k in range(Q):
                            at = bass.IndirectOffsetOnAxis(ap=to_row[:, s, k:k + 1], axis=0)
                            pool.indirect_dma_start(dest, at, sums_out[:, s, k * D:(k + 1) * D], None,
                                                    compute_op=ALU.bypass if mlp else ALU.add)\
                                .then_inc(scattered[s], 16)

                    if mlp:
                        pipelined(pool, G, (0, gather), (7, scatter))
                    elif norm:
                        pipelined(pool, G, (6, scatter))
                    else:
                        pipelined(pool, G, (0, scatter))
                    for s in range(4):
                        pool.wait_ge(scattered[s], 16 * Q * -(-(G - s) // 4))

                @block.vector
                def _(dve):
                    def measure(new, old):
                        if new:
                            s = new.slot(2)
                            if mlp:
                                dve.wait_ge(gathered[new.slot(4)], 16 * Q * (new.use(4) + 1))
                            if new.reuses(2):
                                dve.wait_ge(normed_done if mlp else shift_done, new.n - 1)
                            for k in range(Q):
                                last = nc.vector.bn_stats(stats[:, s, k, :], row(new, k))
                            last.then_inc(stats_done, 1)
                        if old:
                            o = old.slot(2)
                            dve.wait_ge(root_done, old.n + 1)
                            nc.vector.reciprocal(guess[:, o, 0:Q], var_eps[:, o, 0:Q]).then_inc(root_steps, 1)
                        if new:
                            wait_apart(dve, stats_done, new.n + 1)
                            for k in range(Q):
                                last = nc.vector.bn_aggr(moments[:, s, k, :], stats[:, s, k, :])
                            last.then_inc(moments_done, 1)
                        if old:
                            if old.reuses(2):
                                dve.wait_ge(msgs_done, old.n - 1)
                            refine(dve, o, P, Q, root_steps, 3 * old.n + 1, (rstd, rstd_done))

                    def guess_root(g):
                        s = g.slot(2)
                        v = var_eps[:, s, 0:Q]
                        dve.wait_ge(moments_done, g.n + 1)
                        nc.vector.tensor_scalar(v, moments[:, s, 0:Q, 1], LN_EPS, None,
                                                ALU.add).then_inc(root_steps, 1)
                        dve.wait_ge(root_steps, 10 * g.n + 1)
                        nc.vector.tensor_scalar(guess[:, s, 0:Q].bitcast(INT32), v.bitcast(INT32), -0.5,
                                                ROOT_MAGIC, ALU.mult, ALU.add).then_inc(root_steps, 1)

                    def improve(g, round):
                        s = g.slot(2)
                        before = 10 * g.n + 2 + 3 * round
                        refine(dve, s, P, Q, root_steps, before,
                               (rstd, rstd_done) if round == 2 else (guess, root_steps))

                    def normalize(g):
                        s = g.slot(2)
                        dve.wait_ge(rstd_done, g.n + 1)
                        for k in range(Q):
                            last = nc.vector.tensor_scalar(row(g, k), row(g, k), moments[:, s, k, 0:1],
                                                           rstd[:, s, k:k + 1], ALU.subtract, ALU.mult)
                        last.then_inc(normed_done, 1)

                    def shift_by(g):
                        s = g.slot(2)
                        dve.wait_ge(rstd_done, g.n + 1)
                        if g.reuses(2):
                            dve.wait_ge(msgs_done, g.n - 1)
                        nc.vector.scalar_tensor_tensor(out=shift[:, s, 0:Q], in0=moments[:, s, 0:Q, 0],
                                                       scalar=-1.0, in1=rstd[:, s, 0:Q], op0=ALU.mult,
                                                       op1=ALU.mult).then_inc(shift_done, 1)

                    def copy_attr(g):
                        dve.wait_ge(turned, g.n + 1)
                        if g.reuses(2):
                            dve.wait_ge(hidden, g.n - 1)
                        nc.vector.tensor_copy(edge_cols[D:P, g.slot(2), :], bank(TURN, 512)[D:P, :])\
                            .then_inc(attr_cols, 1)

                    def gate_messages(g):
                        s = g.slot(2)
                        dve.wait_ge(tanh_done, g.n + 1)
                        nc.vector.tensor_scalar(gate1[:, s, :], gate[:, s, :], 0.5, 0.5, ALU.mult,
                                                ALU.add).then_inc(gate_done, 1)
                        dve.wait_ge(gate_done, g.n + 1)
                        if g.reuses(2):
                            dve.wait_ge(summed, g.n - 1)
                        m = by_tile(bank(MSG, Q * (D + 1)))[:, :, 0:D]
                        nc.vector.tensor_tensor(msgs[:, s, :, 0:D], m,
                                                gate1[:, s, :].rearrange("p (q a) -> p q a", a=1)
                                                .broadcast_to([P, Q, D]), ALU.mult).then_inc(msgs_done, 1)

                    def carry(g, k):
                        s = g.slot(2)
                        if k == 0:
                            dve.wait_ge(summed, g.n + 1)
                            if g.reuses(2):
                                dve.wait_ge(product, g.n - 1)
                        if k:
                            before = aggs[0:W, s, k * P - 1:k * P]
                            dve.wait_ge(carried, g.n * Q + k)
                        elif isinstance(g.n, int) and g.n == 0:
                            before = carry0[0:W, :]
                        else:
                            before = aggs[0:W, 1 - s, Q * P - 1:Q * P]
                            dve.wait_ge(carried, g.n * Q)
                        nc.vector.scalar_tensor_tensor(out=aggs[0:W, s, k * P:(k + 1) * P],
                                                       in0=tile_of(follows, g, k)[0:W, :], scalar=before,
                                                       in1=bank(AGG + s, 512)[0:W, k * P:(k + 1) * P],
                                                       op0=ALU.mult, op1=ALU.add).then_inc(carried, 1)

                    def degrees(g):
                        dve.wait_ge(product, g.n + 1)
                        v = by_tile(bank(OUT + g.slot(2), Q * W))
                        nc.vector.tensor_scalar(gate[:, g.slot(2), :], v[:, :, D], 1.0, None, ALU.max)\
                            .then_inc(deg_step, 1)

                    def invert_degrees(g):
                        dve.wait_ge(deg_step, 2 * g.n + 1)
                        nc.vector.reciprocal(inv_deg[:, bass.ds(g.n * Q, Q)], gate[:, g.slot(2), :])\
                            .then_inc(deg_step, 1)

                    def finish(g):
                        s, s4 = g.slot(2), g.slot(4)
                        v = by_tile(bank(OUT + s, Q * W))
                        o = by_tile(sums_out[:, s4, :])
                        inv = inv_deg[:, bass.ds(g.n * Q, Q)]
                        if counted:
                            dve.wait_ge(deg_step, 2 * g.n + 2)
                        else:
                            dve.wait_ge(product, g.n + 1)
                        if g.reuses(4):
                            dve.wait_ge(scattered[s4], 16 * Q * g.use(4))
                        if mlp:
                            nc.vector.tensor_copy(o, v[:, :, 0:D]).then_inc(result, 1)
                        else:
                            nc.vector.tensor_tensor(o, v[:, :, 0:D], inv.rearrange("p (q a) -> p q a", a=1)
                                                    .broadcast_to([P, Q, D]), ALU.mult).then_inc(result, 1)

                    def norm_step(new, cur, old, last):
                        if last:
                            degrees(last)
                        if old:
                            carry(old, 0)
                        if last:
                            invert_degrees(last)
                        if old:
                            carry(old, 1)
                        if new or cur:
                            measure(new, cur)
                        if old:
                            carry(old, 2)
                        if last:
                            finish(last)
                        if cur:
                            shift_by(cur)
                        if old:
                            carry(old, 3)

                    def mlp_step(new, turned_one, messages, old, last):
                        if new:
                            measure(new, None)
                        if turned_one:
                            copy_attr(turned_one)
                        if new:
                            guess_root(new)
                        if old:
                            carry(old, 0)
                        if new:
                            improve(new, 0)
                        if old:
                            carry(old, 1)
                        if new:
                            improve(new, 1)
                        if old:
                            carry(old, 2)
                        if new:
                            improve(new, 2)
                        if old:
                            carry(old, 3)
                        if new:
                            normalize(new)
                        if last:
                            finish(last)
                        if messages:
                            gate_messages(messages)

                    def relu_step(old, last):
                        if old:
                            carry(old, 0)
                            carry(old, 1)
                        if last:
                            finish(last)
                        if old:
                            carry(old, 2)
                            carry(old, 3)

                    if mlp:
                        pipelined(dve, G, ((2, 3, 4, 5, 6), mlp_step))
                    elif norm:
                        pipelined(dve, G, ((0, 1, 3, 5), norm_step))
                    else:
                        pipelined(dve, G, ((0, 1), relu_step))

                @block.scalar
                def _(act):
                    def widen(g):
                        if g.reuses(2):
                            act.wait_ge(summed, g.n - 1)
                        nc.scalar.activation(same_f[:, g.slot(2), :],
                                             same[:, bass.ds(g.n * Q, Q), :].rearrange("p e i -> p (e i)"),
                                             ACT.Copy).then_inc(widened, 1)

                    def rectify(g):
                        s = g.slot(2)
                        if g.reuses(2):
                            act.wait_ge(summed, g.n - 1)
                        if norm:
                            act.wait_ge(shift_done, g.n + 1)
                            for k in range(Q):
                                last = nc.scalar.activation(msgs[:, s, k, 0:D], row(g, k), ACT.Relu,
                                                            bias=shift[:, s, k:k + 1], scale=rstd[:, s, k:k + 1])
                            last.then_inc(msgs_done, 1)
                        else:
                            nc.scalar.activation(msgs[:, s, :, 0:D], edge_rows[:, bass.ds(g.n * Q, Q), :],
                                                 ACT.Relu).then_inc(msgs_done, 1)

                    def rectify_cols(g):
                        act.wait_ge(turned, g.n + 1)
                        if g.reuses(2):
                            act.wait_ge(hidden, g.n - 1)
                        nc.scalar.activation(edge_cols[0:D, g.slot(2), :], bank(TURN, 512)[0:D, :], ACT.Relu)\
                            .then_inc(cols_done, 1)

                    def gelus(g):
                        s = g.slot(2)
                        act.wait_ge(hidden, g.n + 1)
                        if g.reuses(2):
                            act.wait_ge(message_done, g.n - 1)
                        nc.scalar.activation(cols[0:D, s, 0:Q * P], bank(HID, 512)[0:D, :], ACT.Gelu,
                                             bias=mb1c[:, :])
                        nc.scalar.activation(cols2[0:D, s, 0:Q * P], bank(HID + 1, 512)[0:D, :], ACT.Gelu,
                                             bias=gb1c[:, :]).then_inc(gelu_done, 1)

                    def tanh(g):
                        s = g.slot(2)
                        act.wait_ge(message_done, g.n + 1)
                        if g.reuses(2):
                            act.wait_ge(gate_done, g.n - 1)
                        z = by_tile(bank(MSG, Q * (D + 1)))[:, :, D]
                        nc.scalar.activation(gate[:, s, :], z, ACT.Tanh, scale=0.5).then_inc(tanh_done, 1)

                    def root(g):
                        s = g.slot(2)
                        act.wait_ge(moments_done, g.n + 1)
                        if g.reuses(2):
                            act.wait_ge(rstd_done, g.n - 1)
                        nc.scalar.activation(var_eps[:, s, 0:Q], moments[:, s, 0:Q, 1], ACT.Sqrt,
                                             bias=eps[:, :]).then_inc(root_done, 1)

                    if mlp:
                        pipelined(act, G, (4, widen), (3, rectify_cols), (4, tanh), (3, gelus))
                    elif norm:
                        pipelined(act, G, (2, rectify), (2, widen), (0, root))
                    else:
                        pipelined(act, G, (0, widen), (0, rectify))

                @block.tensor
                def _(pe):
                    def turn(g):
                        s = g.slot(4)
                        pe.wait_ge(normed_done, g.n + 1)
                        pe.wait_ge(attr_in[s], 16 * (g.use(4) + 1))
                        if g.reuses(1):
                            pe.wait_ge(cols_done, g.n)
                            pe.wait_ge(attr_cols, g.n)
                        for k in range(Q):
                            last = nc.tensor.transpose(bank(TURN, 512)[:, k * P:(k + 1) * P],
                                                       edge_in[:, s, k * P:(k + 1) * P], ident[:, :])
                        last.then_inc(turned, 1)

                    def hide(g):
                        s = g.slot(2)
                        pe.wait_ge(cols_done, g.n + 1)
                        pe.wait_ge(attr_cols, g.n + 1)
                        if g.reuses(1):
                            pe.wait_ge(gelu_done, g.n)
                        nc.tensor.matmul(bank(HID, 512)[0:D, :], mw1[:, :], edge_cols[:, s, :], start=True,
                                         stop=True)
                        nc.tensor.matmul(bank(HID + 1, 512)[0:D, :], gw1[:, :], edge_cols[:, s, :], start=True,
                                         stop=True).then_inc(hidden, 1)

                    def message(g):
                        s = g.slot(2)
                        pe.wait_ge(gelu_done, g.n + 1)
                        if g.reuses(1):
                            pe.wait_ge(msgs_done, g.n)
                            pe.wait_ge(tanh_done, g.n)
                        for k in range(Q):
                            at = k * (D + 1)
                            nc.tensor.matmul(bank(MSG, 512)[:, at:at + D], cols[:, s, k * P:(k + 1) * P],
                                             mw2[:, :], start=True, stop=True)
                            last = nc.tensor.matmul(bank(MSG, 512)[:, at + D:at + D + 1],
                                                    cols2[:, s, k * P:(k + 1) * P], gw2[:, :], start=True,
                                                    stop=True)
                        last.then_inc(message_done, 1)

                    def aggregate(g):
                        s = g.slot(2)
                        pe.wait_ge(msgs_done, g.n + 1)
                        pe.wait_ge(widened, g.n + 1)
                        if g.reuses(2):
                            pe.wait_ge(carried, (g.n - 1) * Q)
                        for k in range(Q):
                            last = nc.tensor.matmul(bank(AGG + s, 512)[0:W, k * P:(k + 1) * P],
                                                    msgs[:, s, k, 0:W], same_f[:, s, k * P:(k + 1) * P],
                                                    start=True, stop=True)
                        last.then_inc(summed, 1)

                    def multiply(g):
                        s = g.slot(2)
                        pe.wait_ge(carried, g.n * Q + Q)
                        if g.reuses(2):
                            pe.wait_ge(result, g.n - 1)
                        for k in range(Q):
                            last = nc.tensor.matmul(bank(OUT + s, 512)[:, k * W:(k + 1) * W],
                                                    aggs[0:W, s, k * P:(k + 1) * P], weight[:, :], start=True,
                                                    stop=True)
                        last.then_inc(product, 1)

                    if mlp:
                        pipelined(pe, G, (3, turn), (5, aggregate), (6, multiply), (4, message), (3, hide))
                    elif norm:
                        pipelined(pe, G, (4, multiply), (2, aggregate))
                    else:
                        pipelined(pe, G, (0, aggregate), (1, multiply))

        def update_pass():
            G = NODE_GROUPS
            loaded = [sem(f"u_loaded{s}") for s in range(4)]
            agg_in = [sem(f"u_agg{s}") for s in range(4)]
            stats_done = sem("u_stats")
            moments_done = sem("u_moments")
            var_done = sem("u_var")
            rstd_done = sem("u_rstd")
            shift_done = sem("u_shift")
            relu_done = sem("u_relu")
            turned = sem("u_turned")
            cols_done = sem("u_cols")
            hidden = sem("u_hidden")
            gelu_done = sem("u_gelu")
            product = sem("u_product")
            stats2_done = sem("u_stats2")
            moments2_done = sem("u_moments2")
            var2_done = sem("u_var2")
            rstd2_done = sem("u_rstd2")
            shift2_done = sem("u_shift2")
            normed2_done = sem("u_normed2")
            scaled = sem("u_scaled")
            biased = sem("u_biased")
            result = sem("u_result")
            stored = [sem(f"u_stored{s}") for s in range(4)]
            TURN, HID, OUT = 0, 2, 6

            with nc.Block() as block:
                @block.sync
                def _(sp):
                    def load(g):
                        p, t = shape(g)
                        s = g.slot(4)
                        if g.reuses(4):
                            sp.wait_ge(biased, g.n - 3)
                            sp.wait_ge(relu_done, g.n - 3)
                        sp.dma_start(rows_in[0:p, s, 0:t * D], rows_of(x1, g)).then_inc(loaded[s], 16)
                        if g.reuses(4):
                            sp.wait_ge(hidden, g.n - 3)
                        sp.dma_start(rows_in2[0:p, s, 0:t * D], rows_of(aggu, g)).then_inc(agg_in[s], 16)

                    def store(g):
                        p, t = shape(g)
                        s = g.slot(4)
                        sp.wait_ge(result, g.n + 1)
                        sp.dma_start(rows_of(out, g), result_rows[0:p, s, 0:t * D]).then_inc(stored[s], 16)

                    pipelined(sp, G, (9, store), (0, load))
                    load(END)
                    store(END)
                    for s in range(4):
                        sp.wait_ge(stored[s], 16 * -(-(G + 1 - s) // 4))

                @block.gpsimd
                def _(pool):
                    def root(g):
                        p, t = shape(g)
                        s = g.slot(2)
                        wait_apart(pool, moments_done, g.n + 1)
                        if g.reuses(2):
                            wait_apart(pool, relu_done, g.n - 1)
                        pool.tensor_scalar(var_eps[0:p, s, 0:t], moments[0:p, s, 0:t, 1], LN_EPS, None,
                                           ALU.add).then_inc(var_done, 1)
                        pool.wait_ge(var_done, g.n + 1)
                        pool.tensor_tensor(rstd[0:p, s, 0:t], var_eps[0:p, s, 0:t], minus_half[0:p, 0:t],
                                           ALU.pow).then_inc(rstd_done, 1)

                    def bias(g):
                        p, t = shape(g)
                        s = g.slot(4)
                        pool.wait_ge(loaded[s], 16 * (g.use(4) + 1))
                        if g.reuses(4):
                            pool.wait_ge(result, g.n - 3)
                        b = lnb[0:p, :].rearrange("p (a d) -> p a d", a=1).broadcast_to([p, t, D])
                        pool.tensor_tensor(by_row(x1_biased[:, s, :], p, t), by_row(rows_in[:, s, :], p, t), b,
                                           ALU.add).then_inc(biased, 1)

                    def root2(g):
                        p, t = shape(g)
                        s = g.slot(2)
                        wait_apart(pool, moments2_done, g.n + 1)
                        if g.reuses(2):
                            wait_apart(pool, normed2_done, g.n - 1)
                        pool.tensor_scalar(var_eps2[0:p, s, 0:t], moments2[0:p, s, 0:t, 1], LN_EPS, None,
                                           ALU.add).then_inc(var2_done, 1)
                        pool.wait_ge(var2_done, g.n + 1)
                        pool.tensor_tensor(rstd2[0:p, s, 0:t], var_eps2[0:p, s, 0:t], minus_half[0:p, 0:t],
                                           ALU.pow).then_inc(rstd2_done, 1)

                    pipelined(pool, G, (0, root), (4, root2), (2, bias))
                    for part in (root, bias, root2):
                        part(END)

                @block.vector
                def _(dve):
                    def shift_by(g):
                        p, t = shape(g)
                        s = g.slot(2)
                        dve.wait_ge(rstd_done, g.n + 1)
                        if g.reuses(2):
                            dve.wait_ge(relu_done, g.n - 1)
                        nc.vector.scalar_tensor_tensor(out=shift[0:p, s, 0:t], in0=moments[0:p, s, 0:t, 0],
                                                       scalar=-1.0, in1=rstd[0:p, s, 0:t], op0=ALU.mult,
                                                       op1=ALU.mult).then_inc(shift_done, 1)

                    def shift2_by(g):
                        p, t = shape(g)
                        s = g.slot(2)
                        dve.wait_ge(rstd2_done, g.n + 1)
                        if g.reuses(2):
                            dve.wait_ge(normed2_done, g.n - 1)
                        nc.vector.scalar_tensor_tensor(out=shift2[0:p, s, 0:t], in0=moments2[0:p, s, 0:t, 0],
                                                       scalar=-1.0, in1=rstd2[0:p, s, 0:t], op0=ALU.mult,
                                                       op1=ALU.mult).then_inc(shift2_done, 1)

                    def step(new, old, cur, last):
                        if new:
                            p, t = shape(new)
                            s, s4 = new.slot(2), new.slot(4)
                            dve.wait_ge(loaded[s4], 16 * (new.use(4) + 1))
                            if new.reuses(2):
                                dve.wait_ge(rstd_done, new.n - 1)
                            for k in range(t):
                                i = nc.vector.bn_stats(stats[0:p, s, k, :], rows_in[0:p, s4, k * D:(k + 1) * D])
                            i.then_inc(stats_done, 1)
                        if last:
                            lp, lt = shape(last)
                            l4 = last.slot(4)
                            v = by_row(h_rows[:, l4, :], lp, lt)
                            dve.wait_ge(normed2_done, last.n + 1)
                            nc.vector.tensor_tensor(v, v, lng[0:lp, :].rearrange("p (a d) -> p a d", a=1)
                                                    .broadcast_to([lp, lt, D]), ALU.mult).then_inc(scaled, 1)
                        if new:
                            wait_apart(dve, stats_done, new.n + 1)
                            for k in range(t):
                                i = nc.vector.bn_aggr(moments[0:p, s, k, :], stats[0:p, s, k, :])
                            i.then_inc(moments_done, 1)
                        if last:
                            dve.wait_ge(scaled, last.n + 1)
                            dve.wait_ge(biased, last.n + 1)
                            if last.reuses(4):
                                dve.wait_ge(stored[l4], 16 * last.use(4))
                            nc.vector.tensor_tensor(result_rows[0:lp, l4, 0:lt * D], h_rows[0:lp, l4, 0:lt * D],
                                                    x1_biased[0:lp, l4, 0:lt * D], ALU.add).then_inc(result, 1)
                        if cur:
                            shift2_by(cur)
                        if old:
                            op, ot = shape(old)
                            o = old.slot(2)
                            dve.wait_ge(product, old.n + 1)
                            if old.reuses(2):
                                dve.wait_ge(rstd2_done, old.n - 1)
                            for k in range(ot):
                                i = nc.vector.bn_stats(stats2[0:op, o, k, :],
                                                       bank(OUT + o, ot * D)[0:op, k * D:(k + 1) * D])
                            i.then_inc(stats2_done, 1)
                        if new:
                            shift_by(new)
                        if old:
                            wait_apart(dve, stats2_done, old.n + 1)
                            for k in range(ot):
                                i = nc.vector.bn_aggr(moments2[0:op, o, k, :], stats2[0:op, o, k, :])
                            i.then_inc(moments2_done, 1)

                    pipelined(dve, G, ((0, 4, 5, 6), step))
                    step(END, None, None, None)
                    step(None, END, None, None)
                    step(None, None, END, None)
                    step(None, None, None, END)

                @block.scalar
                def _(act):
                    def normalize(g):
                        p, t = shape(g)
                        s, s4 = g.slot(2), g.slot(4)
                        act.wait_ge(shift_done, g.n + 1)
                        if g.reuses(4):
                            act.wait_ge(turned, g.n - 3)
                        for k in range(t):
                            last = nc.scalar.activation(relu_rows[0:p, s4, k * D:(k + 1) * D],
                                                        rows_in[0:p, s4, k * D:(k + 1) * D], ACT.Relu,
                                                        bias=shift[0:p, s, k:k + 1], scale=rstd[0:p, s, k:k + 1])
                        last.then_inc(relu_done, 1)

                    def normalize2(g):
                        p, t = shape(g)
                        s, s4 = g.slot(2), g.slot(4)
                        act.wait_ge(shift2_done, g.n + 1)
                        if g.reuses(4):
                            act.wait_ge(result, g.n - 3)
                        for k in range(t):
                            last = nc.scalar.activation(h_rows[0:p, s4, k * D:(k + 1) * D],
                                                        bank(OUT + s, t * D)[0:p, k * D:(k + 1) * D],
                                                        ACT.Identity, bias=shift2[0:p, s, k:k + 1],
                                                        scale=rstd2[0:p, s, k:k + 1])
                        last.then_inc(normed2_done, 1)

                    def copy_cols(g):
                        p, t = shape(g)
                        s = g.slot(4)
                        act.wait_ge(turned, g.n + 1)
                        if g.reuses(4):
                            act.wait_ge(product, g.n - 3)
                        w = (t - 1) * P + p
                        nc.scalar.activation(h2_cols[0:D, s, 0:w], two_banks(TURN, w)[0:D, :], ACT.Copy)\
                            .then_inc(cols_done, 1)

                    def gelu(g):
                        p, t = shape(g)
                        s = g.slot(2)
                        act.wait_ge(hidden, g.n + 1)
                        if g.reuses(2):
                            act.wait_ge(product, g.n - 1)
                        w = (t - 1) * P + p
                        nc.scalar.activation(cols[0:D, s, 0:w], two_banks(HID + 2 * s, w)[0:D, :], ACT.Gelu,
                                             bias=ub1c[:, :]).then_inc(gelu_done, 1)

                    pipelined(act, G, (1, normalize), (2, copy_cols), (5, normalize2), (3, gelu))
                    for part in (normalize, copy_cols, gelu, normalize2):
                        part(END)

                @block.tensor
                def _(pe):
                    def turn(g):
                        p, t = shape(g)
                        pe.wait_ge(relu_done, g.n + 1)
                        if g.reuses(1):
                            pe.wait_ge(cols_done, g.n)
                        for k in range(t):
                            last = nc.tensor.transpose(two_banks(TURN, T * P)[0:D, k * P:k * P + p],
                                                       relu_rows[0:p, g.slot(4), k * D:(k + 1) * D],
                                                       ident[0:p, 0:p])
                        last.then_inc(turned, 1)

                    def hide(g):
                        p, t = shape(g)
                        s, s4 = g.slot(2), g.slot(4)
                        w = (t - 1) * P + p
                        pe.wait_ge(cols_done, g.n + 1)
                        pe.wait_ge(agg_in[s4], 16 * (g.use(4) + 1))
                        if g.reuses(2):
                            pe.wait_ge(gelu_done, g.n - 1)
                        for at in range(0, w, 512):
                            to = min(w, at + 512)
                            nc.tensor.matmul(two_banks(HID + 2 * s, w)[0:D, at:to], uw1n[:, :],
                                             h2_cols[0:D, s4, at:to], start=True, stop=False)
                            for k in range(at // P, -(-to // P)):
                                last = nc.tensor.matmul(two_banks(HID + 2 * s, w)[0:D, k * P:k * P + p],
                                                        rows_in2[0:p, s4, k * D:(k + 1) * D], ident[0:p, 0:p],
                                                        start=False, stop=(k + 1) * P >= to)
                        last.then_inc(hidden, 1)

                    def multiply(g):
                        p, t = shape(g)
                        s = g.slot(2)
                        pe.wait_ge(gelu_done, g.n + 1)
                        if g.reuses(2):
                            pe.wait_ge(stats2_done, g.n - 1)
                            pe.wait_ge(normed2_done, g.n - 1)
                        for k in range(t):
                            to = bank(OUT + s, T * D)[0:p, k * D:(k + 1) * D]
                            nc.tensor.matmul(to, cols[:, s, k * P:k * P + p], uw2[:, :], start=True, stop=False)
                            last = nc.tensor.matmul(to, h2_cols[0:D, g.slot(4), k * P:k * P + p], ident[0:D, 0:D],
                                                    start=False, stop=True)
                        last.then_inc(product, 1)

                    pipelined(pe, G, (2, turn), (3, hide), (4, multiply))
                    for part in (turn, hide, multiply):
                        part(END)

        run(node_pass, "a", x, None, True, wr1, pre1, x)
        run(edge_pass, "ea", None, "norm", wl1, pre1)
        run(node_pass, "b", pre1, x, False, wr2, x1, pre1)
        run(edge_pass, "eb", None, "relu", wl2, x1)
        run(edge_pass, "ec", x1, "mlp", uw1e, aggu)
        run(update_pass)


def kernel(**inputs):
    import numpy as _np
    import concourse.bacc as _bacc
    from concourse import mybir as _mybir
    from concourse.bass_utils import run_bass_kernel_spmd as _run

    nc = _bacc.Bacc("TRN2", target_bir_lowering=False, num_devices=1)
    get = {k: _np.asarray(v) for k, v in inputs.items()}

    def column(name):
        return get[name].reshape(-1, 1)

    def line(name):
        return get[name].reshape(1, -1)

    src = _np.concatenate([get["src"], _np.zeros(EP - E, get["src"].dtype)])
    dst = _np.concatenate([get["dst"], _np.full(EP - E + 1, N, get["dst"].dtype)])
    attr = _np.concatenate([get["edge_attr_32"], _np.zeros((EP - E, ED), get["edge_attr_32"].dtype)])
    dst3 = _np.stack([dst[:EP].reshape(EDGE_TILES, P).T, dst[1:].reshape(EDGE_TILES, P).T,
                      dst[:EP].reshape(P, EDGE_TILES)])
    laid = [
        ("x", get["x"]), ("src", src.reshape(EDGE_TILES, P).T), ("dst", dst3), ("edge_attr", attr),
        ("Wl1t", get["L0_gnn_Wl1"].T), ("bl1", line("L0_gnn_bl1")), ("Wr1t", get["L0_gnn_Wr1"].T),
        ("Wl2t", get["L0_gnn_Wl2"].T), ("bl2", line("L0_gnn_bl2")), ("Wr2t", get["L0_gnn_Wr2"].T),
        ("mW1", get["L1_gnn_mW1"]), ("mb1", column("L1_gnn_mb1")), ("mW2", get["L1_gnn_mW2"]),
        ("mb2", line("L1_gnn_mb2")), ("gW1", get["L1_gnn_gW1"]), ("gb1", column("L1_gnn_gb1")),
        ("gW2", get["L1_gnn_gW2"]), ("gb2", line("L1_gnn_gb2")), ("uW1", get["L1_gnn_uW1"]),
        ("ub1", column("L1_gnn_ub1")), ("uW2", get["L1_gnn_uW2"]), ("ub2", line("L1_gnn_ub2")),
        ("ln_g", line("L1_gnn_ln_g")), ("ln_b", line("L1_gnn_ln_b")),
    ]
    arrays, args = {}, []
    for name, a in laid:
        a = _np.ascontiguousarray(a)
        arrays[f"in_{name}"] = a
        args.append(nc.dram_tensor(f"in_{name}", a.shape, _mybir.dt.from_np(a.dtype), kind="ExternalInput").ap())
    out = nc.dram_tensor("out_0", (N, D), _mybir.dt.float32, kind="ExternalOutput").ap()
    gnn_kernel(nc, *args, out)
    r = _run(nc, [arrays], core_ids=[0])
    return r.results[0]["out_0"]
```
